# Optimizing a Trainium2 kernel written in Bass

```python
import numpy as np
import jax
import jax.numpy as jnp

def _softmax(x, axis=-1):
    return jax.nn.softmax(x, axis=axis)

def _gelu(x):
    return jax.nn.gelu(x, approximate=True)

def _silu(x):
    return jax.nn.silu(x)

def _sigmoid(x):
    return jax.nn.sigmoid(x)

def _layernorm(x, axis=-1, eps=1e-05):
    m = jnp.mean(x, axis=axis, keepdims=True)
    v = jnp.var(x, axis=axis, keepdims=True)
    return (x - m) / jnp.sqrt(v + eps)

def _scatter_add(tgt, idx, src, axis=0):
    return tgt.at[idx].add(src)

def _segment_sum(src, seg, n):
    return jax.ops.segment_sum(src, seg, n)
kernel_name = 'mk_perceiver_d1_seqx_r2_e5a53f'

def setup_inputs(seed: int=0):
    np.random.seed(seed)
    _w = jnp.asarray

    def _rec_inputs():
        import jax
        import jax.numpy as jnp
        _rk = jax.random.key(seed)
        x = -0.0005207 + 1.001 * jax.random.normal(jax.random.fold_in(_rk, 1), (4, 128, 512), jnp.float32)
        _lenS = 128 - jax.random.randint(jax.random.fold_in(_rk, 7), (4,), 0, max(1, 128 // 4) + 1, jnp.int32)
        _lenS2 = 2048 - jax.random.randint(jax.random.fold_in(_rk, 8), (4,), 0, max(1, 2048 // 4) + 1, jnp.int32)
        _ctx_1024P = jax.random.normal(jax.random.fold_in(_rk, 11), (4, 16, 512), jnp.float32)
        _ctx_1024c = jax.random.dirichlet(jax.random.fold_in(_rk, 511), 0.3 * jnp.ones((16,), jnp.float32), (4, 2048))
        _ctx_1024t = jnp.einsum('bsk,bkd->bsd', _ctx_1024c, _ctx_1024P)
        _ctx_1024t = _ctx_1024t * jax.lax.rsqrt(jnp.mean(jnp.square(_ctx_1024t)) + 1e-12) * 0.953939
        ctx_1024 = 2.81802e-05 + 1.00001 * (_ctx_1024t + 0.3 * jax.random.normal(jax.random.fold_in(_rk, 611), (4, 2048, 512), jnp.float32))
        _validS = jnp.arange(128)[None, :] < _lenS[:, None]
        _validS2 = jnp.arange(2048)[None, :] < _lenS2[:, None]
        _causal = jnp.tril(jnp.ones((128, 128), dtype=bool))
        mask_BxS2_bf1 = jnp.ones((4, 2048), dtype=bool)
        return (x, ctx_1024, mask_BxS2_bf1)
    x, ctx_1024, mask_BxS2_bf1 = _rec_inputs()

    def _L0_xattn_setup():
        import jax, jax.numpy as jnp
        import numpy as np
        EMB = 512
        HEADS = 16
        HEAD_DIM = EMB // HEADS
        EPS = 1e-05

        def _layer_norm(x, gamma, beta):
            m = jnp.mean(x, axis=-1, keepdims=True)
            v = jnp.mean(jnp.square(x - m), axis=-1, keepdims=True)
            return (x - m) / jnp.sqrt(v + EPS) * gamma + beta
        key = jax.random.key(seed)
        ks = jax.random.split(key, 8)
        B, Tx, Tc = (2, 512, 4096)
        scale = 1.0 / np.sqrt(EMB)
        return {'x': jax.random.normal(ks[0], (B, Tx, EMB), dtype=jnp.float32), 'context': jax.random.normal(ks[1], (B, Tc, EMB), dtype=jnp.float32), 'context_mask': jnp.ones((B, Tc), dtype=bool), 'Wq': jax.random.normal(ks[2], (EMB, EMB), dtype=jnp.float32) * scale, 'Wk': jax.random.normal(ks[3], (EMB, EMB), dtype=jnp.float32) * scale, 'Wv': jax.random.normal(ks[4], (EMB, EMB), dtype=jnp.float32) * scale, 'Wo': jax.random.normal(ks[5], (EMB, EMB), dtype=jnp.float32) * scale, 'bo': jnp.zeros((EMB,), dtype=jnp.float32), 'g1': jnp.ones((EMB,), dtype=jnp.float32), 'b1': jnp.zeros((EMB,), dtype=jnp.float32), 'g2': jnp.ones((EMB,), dtype=jnp.float32), 'b2': jnp.zeros((EMB,), dtype=jnp.float32)}
    _L0_xattn_all = _L0_xattn_setup()
    _L0_xattn_in = {k: v for k, v in _L0_xattn_all.items() if k in ('Wq', 'Wk', 'Wv', 'Wo', 'bo', 'g1', 'b1', 'g2', 'b2')}
    del _L0_xattn_all

    def _L0_attn_setup():
        import jax, jax.numpy as jnp
        import numpy as np
        D_MODEL = 512
        NHEAD = 16
        HEAD_DIM = D_MODEL // NHEAD
        MAX_POS = 1024

        def _rope_tables(seq_len, dim):
            inv_freq = 1.0 / 10000.0 ** (jnp.arange(0, dim, 2, dtype=jnp.float32) / dim)
            t = jnp.arange(seq_len, dtype=jnp.float32)[:, None]
            freqs = t * inv_freq[None, :]
            emb = jnp.concatenate([freqs, freqs], axis=-1)
            return (jnp.cos(emb), jnp.sin(emb))

        def _rotate_half(x):
            x1, x2 = jnp.split(x, 2, axis=-1)
            return jnp.concatenate([-x2, x1], axis=-1)

        def _apply_rope(x, cos, sin):
            c = cos[None, :, None, :]
            s = sin[None, :, None, :]
            return x * c + _rotate_half(x) * s
        key = jax.random.key(seed)
        ks = jax.random.split(key, 9)
        B, L, D = (4, 1024, D_MODEL)
        lim = 1.0 / np.sqrt(D)

        def lin(k):
            kw, kb = jax.random.split(k)
            W = jax.random.uniform(kw, (D, D), jnp.float32, -lim, lim)
            b = jax.random.uniform(kb, (D,), jnp.float32, -lim, lim)
            return (W, b)
        Wq, bq = lin(ks[0])
        Wk, bk = lin(ks[1])
        Wv, bv = lin(ks[2])
        Wo, bo = lin(ks[3])
        x = jax.random.normal(ks[4], (B, L, D), jnp.float32)
        return {'x': x, 'Wq': Wq, 'bq': bq, 'Wk': Wk, 'bk': bk, 'Wv': Wv, 'bv': bv, 'Wo': Wo, 'bo': bo}
    _L0_attn_all = _L0_attn_setup()
    _L0_attn_in = {k: v for k, v in _L0_attn_all.items() if k in ('Wq', 'bq', 'Wk', 'bk', 'Wv', 'bv', 'Wo', 'bo')}
    del _L0_attn_all

    def _L0_ffn_setup():
        import jax, jax.numpy as jnp
        import numpy as np
        E = 8
        K = 2
        C = 512
        F = 1024
        EPS = 1e-05
        key = jax.random.key(seed)
        ks = jax.random.split(key, 6)
        x = jax.random.normal(ks[0], (2, 512, C), dtype=jnp.float32)
        ln_gamma = 1.0 + 0.02 * jax.random.normal(ks[1], (C,), dtype=jnp.float32)
        ln_beta = 0.02 * jax.random.normal(ks[2], (C,), dtype=jnp.float32)
        gate_w = jax.random.normal(ks[3], (E, C), dtype=jnp.float32) / np.sqrt(C)
        w1 = jax.random.normal(ks[4], (E, F, C), dtype=jnp.float32) / np.sqrt(C)
        w2 = jax.random.normal(ks[5], (E, C, F), dtype=jnp.float32) / np.sqrt(F)
        return {'x': x, 'ln_gamma': ln_gamma, 'ln_beta': ln_beta, 'gate_w': gate_w, 'w1': w1, 'w2': w2}
    _L0_ffn_all = _L0_ffn_setup()
    _L0_ffn_in = {k: v for k, v in _L0_ffn_all.items() if k in ('ln_gamma', 'ln_beta', 'gate_w', 'w1', 'w2')}
    del _L0_ffn_all
    return {'x': x, 'ctx_1024': ctx_1024, 'mask_BxS2_bf1': mask_BxS2_bf1, 'L0_xattn_Wq': _L0_xattn_in['Wq'], 'L0_xattn_Wk': _L0_xattn_in['Wk'], 'L0_xattn_Wv': _L0_xattn_in['Wv'], 'L0_xattn_Wo': _L0_xattn_in['Wo'], 'L0_xattn_bo': _L0_xattn_in['bo'], 'L0_xattn_g1': _L0_xattn_in['g1'], 'L0_xattn_b1': _L0_xattn_in['b1'], 'L0_xattn_g2': _L0_xattn_in['g2'], 'L0_xattn_b2': _L0_xattn_in['b2'], 'L0_attn_Wq': _L0_attn_in['Wq'], 'L0_attn_bq': _L0_attn_in['bq'], 'L0_attn_Wk': _L0_attn_in['Wk'], 'L0_attn_bk': _L0_attn_in['bk'], 'L0_attn_Wv': _L0_attn_in['Wv'], 'L0_attn_bv': _L0_attn_in['bv'], 'L0_attn_Wo': _L0_attn_in['Wo'], 'L0_attn_bo': _L0_attn_in['bo'], 'L0_ffn_ln_gamma': _L0_ffn_in['ln_gamma'], 'L0_ffn_ln_beta': _L0_ffn_in['ln_beta'], 'L0_ffn_gate_w': _L0_ffn_in['gate_w'], 'L0_ffn_w1': _L0_ffn_in['w1'], 'L0_ffn_w2': _L0_ffn_in['w2']}

def reference(x, ctx_1024, mask_BxS2_bf1, L0_xattn_Wq, L0_xattn_Wk, L0_xattn_Wv, L0_xattn_Wo, L0_xattn_bo, L0_xattn_g1, L0_xattn_b1, L0_xattn_g2, L0_xattn_b2, L0_attn_Wq, L0_attn_bq, L0_attn_Wk, L0_attn_bk, L0_attn_Wv, L0_attn_bv, L0_attn_Wo, L0_attn_bo, L0_ffn_ln_gamma, L0_ffn_ln_beta, L0_ffn_gate_w, L0_ffn_w1, L0_ffn_w2):
    import jax
    import jax.numpy as jnp

    def _L0_xattn_ref(x, context, context_mask, Wq, Wk, Wv, Wo, bo, g1, b1, g2, b2):
        import jax, jax.numpy as jnp
        import numpy as np
        EMB = 512
        HEADS = 16
        HEAD_DIM = EMB // HEADS
        EPS = 1e-05

        def _layer_norm(x, gamma, beta):
            m = jnp.mean(x, axis=-1, keepdims=True)
            v = jnp.mean(jnp.square(x - m), axis=-1, keepdims=True)
            return (x - m) / jnp.sqrt(v + EPS) * gamma + beta
        B, Tx, C = x.shape
        Tc = context.shape[1]
        xn = _layer_norm(x, g1, b1)
        cn = _layer_norm(context, g2, b2)
        q = (xn @ Wq.T).reshape(B, Tx, HEADS, HEAD_DIM)
        k = (cn @ Wk.T).reshape(B, Tc, HEADS, HEAD_DIM)
        v = (cn @ Wv.T).reshape(B, Tc, HEADS, HEAD_DIM)
        scores = jnp.einsum('bqhs,bkhs->bhqk', q, k) / np.sqrt(HEAD_DIM)
        scores = jnp.where(context_mask[:, None, None, :], scores, -jnp.inf)
        attn = jax.nn.softmax(scores, axis=-1)
        out = jnp.einsum('bhqk,bkhs->bqhs', attn, v).reshape(B, Tx, C)
        return out @ Wo.T + bo

    def _L0_attn_ref(x, Wq, bq, Wk, bk, Wv, bv, Wo, bo):
        import jax, jax.numpy as jnp
        import numpy as np
        D_MODEL = 512
        NHEAD = 16
        HEAD_DIM = D_MODEL // NHEAD
        MAX_POS = 1024

        def _rope_tables(seq_len, dim):
            inv_freq = 1.0 / 10000.0 ** (jnp.arange(0, dim, 2, dtype=jnp.float32) / dim)
            t = jnp.arange(seq_len, dtype=jnp.float32)[:, None]
            freqs = t * inv_freq[None, :]
            emb = jnp.concatenate([freqs, freqs], axis=-1)
            return (jnp.cos(emb), jnp.sin(emb))

        def _rotate_half(x):
            x1, x2 = jnp.split(x, 2, axis=-1)
            return jnp.concatenate([-x2, x1], axis=-1)

        def _apply_rope(x, cos, sin):
            c = cos[None, :, None, :]
            s = sin[None, :, None, :]
            return x * c + _rotate_half(x) * s
        B, L, D = x.shape
        H, hd = (NHEAD, HEAD_DIM)
        q = (x @ Wq.T + bq).reshape(B, L, H, hd)
        k = (x @ Wk.T + bk).reshape(B, L, H, hd)
        v = (x @ Wv.T + bv).reshape(B, L, H, hd)
        cos, sin = _rope_tables(L, hd)
        q = _apply_rope(q, cos, sin)
        k = _apply_rope(k, cos, sin)
        scores = jnp.einsum('bqhd,bkhd->bhqk', q, k) / np.sqrt(hd).astype(np.float32)
        attn = jax.nn.softmax(scores, axis=-1)
        out = jnp.einsum('bhqk,bkhd->bqhd', attn, v).reshape(B, L, D)
        return out @ Wo.T + bo

    def _L0_ffn_ref(x, ln_gamma, ln_beta, gate_w, w1, w2):
        import jax, jax.numpy as jnp
        import numpy as np
        E = 8
        K = 2
        C = 512
        F = 1024
        EPS = 1e-05
        B, T, Cc = x.shape
        xf = x.reshape(-1, Cc)
        mu = jnp.mean(xf, axis=-1, keepdims=True)
        var = jnp.var(xf, axis=-1, keepdims=True)
        rn = (xf - mu) * jax.lax.rsqrt(var + EPS) * ln_gamma + ln_beta
        logits = rn @ gate_w.T
        probs = jax.nn.softmax(logits, axis=-1)
        rw, sel = jax.lax.top_k(probs, K)
        comb = jnp.sum(jax.nn.one_hot(sel, E, dtype=xf.dtype) * rw[..., None], axis=1)
        h = jax.nn.gelu(jnp.einsum('nc,efc->enf', xf, w1), approximate=False)
        y = jnp.einsum('enf,ecf->enc', h, w2)
        out = jnp.einsum('enc,ne->nc', y, comb)
        return out.reshape(B, T, Cc)
    x = x + _L0_xattn_ref(_layernorm(x, axis=-1), ctx_1024, mask_BxS2_bf1, L0_xattn_Wq, L0_xattn_Wk, L0_xattn_Wv, L0_xattn_Wo, L0_xattn_bo, L0_xattn_g1, L0_xattn_b1, L0_xattn_g2, L0_xattn_b2)
    x = x + _L0_attn_ref(_layernorm(x, axis=-1), L0_attn_Wq, L0_attn_bq, L0_attn_Wk, L0_attn_bk, L0_attn_Wv, L0_attn_bv, L0_attn_Wo, L0_attn_bo)
    x = x + _L0_ffn_ref(_layernorm(x, axis=-1), L0_ffn_ln_gamma, L0_ffn_ln_beta, L0_ffn_gate_w, L0_ffn_w1, L0_ffn_w2)
    return x

_drawn_inputs = setup_inputs


def setup_inputs(seed=0):
    import zlib

    import numpy as np

    out = dict(_drawn_inputs(seed))
    spreads = {'L0_xattn_bo': (0.0, 0.1),
     'L0_xattn_g1': (1.0, 0.2),
     'L0_xattn_b1': (0.0, 0.33),
     'L0_xattn_g2': (1.0, 0.2),
     'L0_xattn_b2': (0.0, 0.1)}
    factors = {'L0_attn_Wq': 4.874,
     'L0_attn_bq': 8.0,
     'L0_attn_Wk': 4.176,
     'L0_attn_bk': 8.0,
     'L0_attn_bv': 3.201,
     'L0_ffn_ln_gamma': 9.056,
     'L0_ffn_ln_beta': 39.971}
    for name, (base, spread) in spreads.items():
        noise = np.random.default_rng([zlib.crc32(name.encode()), seed]).standard_normal(out[name].shape)
        drawn = base * np.exp(spread * noise) if base else spread * noise
        out[name] = jnp.asarray(drawn.astype(out[name].dtype))
    for name, factor in factors.items():
        out[name] = (out[name] * factor).astype(out[name].dtype)
    return out
```

```python
from contextlib import ExitStack

import numpy as np
import concourse.bass as bass
from concourse import mybir

F32, F16, U8 = mybir.dt.float32, mybir.dt.float16, mybir.dt.uint8
ALU, ACT, AX = mybir.AluOpType, mybir.ActivationFunctionType, mybir.AxisListType

P = 128
NB = 4
D = 512
NC = D // P
TOK = NB * P
KEYS = 2048
NKT = KEYS // P
HEADS, HD = 16, 32
HPG = P // HD
NG = HEADS // HPG
NPAIR = NKT // 2
EPS = 1e-5
A_SCALE, W_SCALE = 16.0, 64.0
UNSCALE = 1.0 / (A_SCALE * W_SCALE)
SM_SCALE = float(1.0 / np.sqrt(HD))
MASKED = -60000.0
SHIFT_ROW, MASK_ROW = 96, 97
ROWS = 98
EXPERTS, FF = 8, 1024
NF = FF // P


def chunked(ap):
    return ap.rearrange("(c p) n -> p c n", p=P)


def prologue(nc, io, t, s):
    with ExitStack() as ctx:
        def sb(name, shape, dt=F32):
            return ctx.enter_context(nc.sbuf_tensor(name, shape, dt))

        def sem(name):
            return ctx.enter_context(nc.semaphore(name))

        w_raw = [sb(f"w_raw{i}", [P, NC, D]) for i in range(3)]
        w_fold = sb("w_fold", [P, NC, D])
        wq_hi, wq_lo = sb("wq_hi", [P, NC, D], F16), sb("wq_lo", [P, NC, D], F16)
        gains = sb("gains", [P, 3, NC])
        offsets = sb("offsets", [P, 2, NC])
        bo_bc = sb("bo_bc", [P, D])
        hat = sb("hat", [P, NB, D])
        hat2 = sb("hat2", [P, NB, D])
        xT_hi, xT_lo = sb("xT_hi", [P, NC, TOK], F16), sb("xT_lo", [P, NC, TOK], F16)
        q_f = sb("q_f", [P, NG, TOK])
        q_hi, q_lo = sb("q_hi", [P, NG, TOK], F16), sb("q_lo", [P, NG, TOK], F16)
        qbias = sb("qbias", [P, NG])
        stats = sb("stats", [P, NB, 6])
        mv = sb("mv", [P, 2, NB, 2])
        rstd = sb("rstd", [P, 2, NB])
        mask_u8 = sb("mask_u8", [NB, KEYS], U8)
        mask_neg = sb("mask_neg", [NB, KEYS], F16)
        ps_t = [ctx.enter_context(nc.psum_tensor(f"pro_t{i}", [P, D], F32)) for i in range(2)]
        ps_q = [ctx.enter_context(nc.psum_tensor(f"pro_q{i}", [P, D], F32)) for i in range(2)]
        ps_b = ctx.enter_context(nc.psum_tensor("pro_b", [P, 3, NG], F32))

        x_in, w_in, vec_in = sem("x_in"), [sem(f"w_in{i}") for i in range(3)], sem("vec_in")
        const = sem("const")
        pow_done = sem("pow_done")
        stat_done = sem("stat_done")
        dve = sem("dve_pro")
        folded = sem("folded")
        w_hi = sem("w_hi")
        w_lo = sem("w_lo")
        normed = sem("normed")
        tr, tr_hi, tr_lo = sem("tr"), sem("tr_hi"), sem("tr_lo")
        bias_mm, bias_out = sem("bias_mm"), sem("bias_out")
        q_mm, q_out, q_hi_s, q_lo_s = sem("q_mm"), sem("q_out"), sem("q_hi_s"), sem("q_lo_s")
        mask_in, mask_done, placed = sem("mask_in"), sem("mask_done"), sem("placed")
        ones_rows = sem("ones_rows")

        targets = [(wq_hi, wq_lo), (t.wk_hi, t.wk_lo), (t.wv_hi, t.wv_lo)]
        block = ctx.enter_context(nc.Block())

        @block.sync
        def _(sp):
            sp.dma_start(t.x[:, :, :], io.x.rearrange("b t c -> t b c")).then_inc(x_in, 16)
            sp.dma_start(t.ident[:, :], io.ident).then_inc(x_in, 16)
            sp.dma_start(w_raw[0][:, :, :], chunked(io.wqT)).then_inc(w_in[0], 16)
            sp.dma_start(gains[:, 0, :], io.g1).then_inc(vec_in, 16)
            sp.dma_start(gains[:, 1, :], io.g2).then_inc(vec_in, 16)
            sp.dma_start(gains[:, 2, :], io.g2).then_inc(vec_in, 16)
            sp.dma_start(offsets[:, 0, :], io.b1).then_inc(vec_in, 16)
            sp.dma_start(offsets[:, 1, :], io.b2).then_inc(vec_in, 16)
            sp.dma_start(bo_bc[:, :], io.xbo.partition_broadcast(P)).then_inc(vec_in, 16)
            for i, w in ((1, io.wkT), (2, io.wvT)):
                sp.dma_start(w_raw[i][:, :, :], chunked(w)).then_inc(w_in[i], 16)
            sp.dma_start(mask_u8[:, :], io.mask).then_inc(mask_in, 16)
            sp.dma_start(t.wo[:, :, :], chunked(io.woT)).then_inc(s.wo_in, 16)
            sp.wait_ge(mask_done, 1)
            sp.dma_start(io.mask_rows, mask_neg[:, :]).then_inc(s.mask_rows_out, 16)
            for part_sem, k, part in ((q_hi_s, 0, q_hi), (q_hi_s, 2, q_hi), (q_lo_s, 1, q_lo)):
                sp.wait_ge(part_sem, NG)
                for j in range(HPG):
                    heads = t.q_stack[HD * k:HD * (k + 1), :, :].rearrange("p (g j) n -> p j g n", j=HPG)
                    sp.dma_start(heads[:, j, :, :], part[HD * j:HD * (j + 1), :, :]).then_inc(placed, 16)
            sp.wait_ge(placed, 16 * 3 * HPG)
            sp.wait_ge(s.mask_rows_out, 16)

        @block.gpsimd
        def _(pool):
            small = [(t.half_neg[:, :], -0.5), (t.eps[:, :], EPS), (t.inv_scale2[:, :], A_SCALE ** -2)]
            whole = small + [(t.ones32[:, :], 1.0), (t.q_stack[SHIFT_ROW:ROWS, :, :], 1.0),
                             (t.q_stack[SHIFT_ROW:SHIFT_ROW + 1, :, :], 0.0)]
            whole += [(t.k_stack[u][SHIFT_ROW:ROWS, :, :], 1.0) for u in range(2)]
            for n, (what, value) in enumerate(small):
                nc.gpsimd.memset(what, value).then_inc(const, 1)
                pool.wait_ge(const, n + 1)
            for k in range(2):
                pool.wait_ge(dve, k + 1)
                nc.gpsimd.tensor_scalar(rstd[:, k, :], mv[:, k, :, 1], EPS, 1.0 if k == 0 else A_SCALE ** -2,
                                        ALU.add, ALU.mult).then_inc(pow_done, 1)
                pool.wait_ge(pow_done, 2 * k + 1)
                nc.gpsimd.tensor_tensor(rstd[:, k, :], rstd[:, k, :], t.half_neg[:, 0:NB],
                                        ALU.pow).then_inc(pow_done, 1)
                pool.wait_ge(pow_done, 2 * k + 2)
            for n in range(len(small), len(whole)):
                nc.gpsimd.memset(*whole[n]).then_inc(const, 1)
                pool.wait_ge(const, n + 1)

        @block.vector
        def _(v):
            n_stat = 0
            v.wait_ge(x_in, 32)
            for k, src in enumerate((t.x, hat)):
                for b in range(NB):
                    nc.vector.bn_stats(stats[:, b, :], src[:, b, :]).then_inc(stat_done, 1)
                n_stat += NB
                v.wait_ge(stat_done, n_stat)
                for b in range(NB):
                    last = nc.vector.bn_aggr(mv[:, k, b, :], stats[:, b, :])
                last.then_inc(dve, 1)
                v.wait_ge(dve, k + 1)
                v.wait_ge(pow_done, 2 * k + 2)
                for b in range(NB):
                    ins = nc.vector.tensor_scalar((hat, hat2)[k][:, b, :], src[:, b, :], mv[:, k, b, 0:1],
                                                  rstd[:, k, b:b + 1], ALU.subtract, ALU.mult)
                    ins.then_inc(normed, 1)
                v.wait_ge(normed, NB * (k + 1))
            v.wait_ge(vec_in, 96)
            for b in range(NB):
                nc.vector.tensor_tensor(t.x[:, b, :], t.x[:, b, :], bo_bc[:, :], ALU.add)
            for i in range(3):
                v.wait_ge(w_in[i], 16)
                if i:
                    v.wait_ge(w_hi, i)
                    v.wait_ge(w_lo, i)
                for c in range(NC):
                    ins = nc.vector.tensor_scalar(w_fold[:, c, :], w_raw[i][:, c, :], gains[:, i, c:c + 1],
                                                  W_SCALE, ALU.mult, ALU.mult)
                ins.then_inc(folded, 1)
                v.wait_ge(folded, i + 1)
                v.wait_ge(w_hi, i + 1)
                nc.vector.tensor_tensor(targets[i][1][:, :, :], w_fold[:, :, :], targets[i][0][:, :, :],
                                        ALU.subtract).then_inc(w_lo, 1)
                if i == 0:
                    for b in range(NB):
                        v.wait_ge(tr_hi, b + 1)
                        nc.vector.tensor_tensor(xT_lo[:, :, P * b:P * (b + 1)],
                                                ps_t[b % 2][:, :].rearrange("p (c n) -> p c n", c=NC),
                                                xT_hi[:, :, P * b:P * (b + 1)], ALU.subtract).then_inc(tr_lo, 1)
            v.wait_ge(mask_in, 16)
            nc.vector.tensor_scalar(mask_neg[:, :], mask_u8[:, :], 1.0, -MASKED,
                                    ALU.subtract, ALU.mult).then_inc(mask_done, 1)
            for g in range(NG):
                v.wait_ge(q_hi_s, g + 1)
                nc.vector.tensor_tensor(q_lo[:, g, :], q_f[:, g, :], q_hi[:, g, :],
                                        ALU.subtract).then_inc(q_lo_s, 1)

        @block.scalar
        def _(act):
            act.wait_ge(folded, 1)
            nc.scalar.activation(wq_hi[:, :, :], w_fold[:, :, :], ACT.Copy).then_inc(w_hi, 1)
            for b in range(NB):
                act.wait_ge(tr, b + 1)
                nc.scalar.activation(xT_hi[:, :, P * b:P * (b + 1)],
                                     ps_t[b % 2][:, :].rearrange("p (c n) -> p c n", c=NC),
                                     ACT.Copy).then_inc(tr_hi, 1)
            for i in (1, 2):
                act.wait_ge(folded, i + 1)
                nc.scalar.activation(targets[i][0][:, :, :], w_fold[:, :, :], ACT.Copy).then_inc(w_hi, 1)
            act.wait_ge(bias_mm, 1)
            for dst, i in ((qbias, 0), (t.kbias, 1), (t.vbias, 2)):
                nc.scalar.activation(dst[:, :], ps_b[:, i, :], ACT.Copy).then_inc(bias_out, 1)
            act.wait_ge(bias_out, 3)
            for g in range(NG):
                act.wait_ge(q_mm, g + 1)
                nc.scalar.activation(q_f[:, g, :], ps_q[g % 2][:, :], ACT.Identity, bias=qbias[:, g:g + 1],
                                     scale=UNSCALE).then_inc(q_out, 1)
                act.wait_ge(q_out, g + 1)
                nc.scalar.activation(q_hi[:, g, :], q_f[:, g, :], ACT.Copy).then_inc(q_hi_s, 1)

        @block.tensor
        def _(pe):
            for b in range(NB):
                pe.wait_ge(normed, NB + b + 1)
                if b >= 2:
                    pe.wait_ge(tr_lo, b - 1)
                for c in range(NC):
                    last = nc.tensor.transpose(ps_t[b % 2][:, P * c:P * (c + 1)], hat2[:, b, P * c:P * (c + 1)],
                                               t.ident[:, :])
                last.then_inc(tr, 1)
            pe.wait_ge(vec_in, 96)
            for i in range(3):
                pe.wait_ge(w_in[i], 16)
                for g in range(NG):
                    for c in range(NC):
                        last = nc.tensor.matmul(ps_b[:, i, g:g + 1], w_raw[i][:, c, P * g:P * (g + 1)],
                                                offsets[:, min(i, 1), c:c + 1], start=(c == 0), stop=(c == NC - 1))
            last.then_inc(bias_mm, 1)
            pe.wait_ge(w_lo, 1)
            pe.wait_ge(tr_lo, NB)
            for g in range(NG):
                if g >= 2:
                    pe.wait_ge(q_out, g - 1)
                col = slice(P * g, P * (g + 1))
                for c in range(NC):
                    nc.tensor.matmul(ps_q[g % 2][:, :], wq_hi[:, c, col], xT_hi[:, c, :], start=(c == 0), stop=False)
                    nc.tensor.matmul(ps_q[g % 2][:, :], wq_hi[:, c, col], xT_lo[:, c, :], start=False, stop=False)
                    last = nc.tensor.matmul(ps_q[g % 2][:, :], wq_lo[:, c, col], xT_hi[:, c, :], start=False,
                                            stop=(c == NC - 1))
                last.then_inc(q_mm, 1)


KB = 512
NKB = KEYS // KB
RAW = 4
PT = 4


def attention_steps():
    def scores(g, p):
        return [("s", g, p, 0), ("s", g, p, 1)]

    steps, t = [], RAW
    for kt in range(2, 10):
        while t < min(NKT, (7 * (kt - 2)) // 4 + RAW + 2):
            steps += [("ln", t // 2), ("t", t), ("t", t + 1)]
            t += 2
        steps += [("v", kt, c) for c in range(NC)]
    assert t == NKT
    steps += [("k", g, kb) for g in (0, 1) for kb in range(NKB)]
    p1 = [[("p1", g, j, kb) for h in range(2) for j in range(HPG) for kb in (2 * h, 2 * h + 1)] for g in range(NG)]
    for kt in range(10, 14):
        for c in range(NC):
            steps += [("v", kt, c), p1[0].pop(0)]
    steps += [("v", 14, c) for c in range(NC)] + [("mt", 0)] + scores(0, 0) + scores(0, 1)
    steps += [("v", 15, c) for c in range(NC)]
    p1_at = [{3: 3, 4: 3, 5: 3, 6: 3, 7: 4}] * 2 + [{3: 4, 4: 4, 5: 4, 6: 4}] + [{}]
    for g in range(NG):
        for p in range(NPAIR):
            work = [("av", g, p, 0), ("av", g, p, 1)]
            if p + 2 < NPAIR:
                work += scores(g, p + 2)
            tiles = [p1[g + 1].pop(0) for _ in range(p1_at[g].get(p, 0))]
            for n in range(4):
                steps += work[n:n + 1] + tiles[n:n + 1]
            if p == 1 and g:
                steps.append(("den", g - 1))
        steps.append(("sums", g))
        if g < 2:
            steps += [("k", g + 2, 0), ("mt", g + 1), ("k", g + 2, 1), ("k", g + 2, 2)]
            steps += scores(g + 1, 0) + scores(g + 1, 1) + [("k", g + 2, 3)]
        if g == 2:
            steps += [("mt", 3)] + scores(3, 0) + scores(3, 1) + [("next ln", 0), ("next ln", 1)]
    return steps + [("next t", kt) for kt in range(RAW)] + [("next v", 0, c) for c in range(NC)] + \
        [("den", NG - 1)] + [("next v", 1, c) for c in range(NC)] + [("op",)]


AHEAD_LN = (0, 1)
AHEAD_T = range(RAW)
AHEAD_V = (0, 1)


def of_batch(step, b):
    return ((step[0][5:], *step[1:]), b + 1) if step[0].startswith("next ") else (step, b)


def cross_attention(nc, io, t, s):
    steps = attention_steps()
    ring = [("v", kt) for kt in AHEAD_V]
    ring += [step[:2] if step[0] == "v" else step for step in steps
             if step[0] in ("k", "mt") or (step[0] == "v" and step[2] == 0) or (step[0] == "p1" and step[1] > 0)]
    assert len(ring) % 2 == 0
    PER_BATCH = {"v": NKT, "k": NG * NKB, "p1": NG * HPG * NKB, "mt": NG}

    def ring_place(step):
        return ring.index(step[:2] if step[0] == "v" else step)

    KIN = 16 * 3 * HPG

    with ExitStack() as ctx:
        def sb(name, shape, dt=F32):
            return ctx.enter_context(nc.sbuf_tensor(name, shape, dt))

        def sem(name):
            return ctx.enter_context(nc.semaphore(name))

        raw = sb("raw", [P, RAW, D])
        xn = sb("xn", [P, RAW, D])
        stats = sb("c_stats", [P, 4, 6])
        mv = sb("c_mv", [P, 4, 2])
        carrier = sb("carrier", [P, 1])
        rstd = sb("c_rstd", [P, 4])
        cT_hi, cT_lo = sb("cT_hi", [P, NC, KEYS], F16), sb("cT_lo", [P, NC, KEYS], F16)
        vals = sb("vals", [P, NKT, D])
        k_f = sb("k_f", [P, 2, KB])
        k_hi = [sb(f"k_hi{h}", [P, 2 * KB], F16) for h in range(2)]
        k_lo = [sb(f"k_lo{h}", [P, 2 * KB], F16) for h in range(2)]
        mpart = sb("mpart", [P, HPG, NKB])
        mgroup = sb("mgroup", [P, 2, HPG])
        pT = sb("pT", [P, PT, 2 * KB])
        acc_pool, acc_dve, acc = sb("acc_pool", [P, 2 * KB]), sb("acc_dve", [P, 2 * KB]), sb("acc", [P, KB])
        rden = sb("rden", [P, P])
        oT = sb("oT", [P, NG, P])
        ps_s = [ctx.enter_context(nc.psum_tensor(f"ps_s{i}", [P, 2 * KB], F32)) for i in range(2)]
        ps_r = [ctx.enter_context(nc.psum_tensor(f"ps_r{i}", [P, KB], F32)) for i in range(2)]
        ps_o = [ctx.enter_context(nc.psum_tensor(f"ps_o{i}", [P, KB], F32)) for i in range(2)]

        raw_in = [sem(f"raw_in{i}") for i in range(RAW)]
        stat_dve, var_dve, normed = sem("c_stat"), sem("c_var"), sem("c_normed")
        pool_pow = sem("c_pow")
        tr, tr_hi, tr_lo = sem("c_tr"), sem("c_tr_hi"), sem("c_tr_lo")
        v_mm, v_out = sem("v_mm"), sem("v_out")
        k_mm, k_f_out, k_hi_out, k_lo_out = sem("k_mm"), sem("k_f_out"), sem("k_hi_out"), sem("k_lo_out")
        k_in = [[sem(f"k_in{u}{h}") for h in range(2)] for u in range(2)]
        mask_in = sem("c_mask_in")
        p1_mm, p1_max, m_max, mt_mm, m_row = (sem("p1_mm"), sem("p1_max"), sem("m_max"), sem("mt_mm"),
                                                        sem("m_row"))
        s_mm, exp_done, av_mm = sem("s_mm"), sem("exp_done"), sem("av_mm")
        pool_add, dve_first, dve_second, sums_done = sem("pool_add"), sem("dve_first"), sem("dve_second"), sem("sums_done")
        den_mm, rden_done, norm_out, fin = sem("den_mm"), sem("rden_done"), sem("norm_out"), sem("fin")
        op_mm, x_done = sem("op_mm"), sem("x_done")

        def p1_bank(step, n):
            if step[1] == 0:
                return ps_s[n % 2][:, KB * (n // 2 % 2):KB * (n // 2 % 2 + 1)]
            return ps_r[ring_place(step) % 2][:, :]

        block = ctx.enter_context(nc.Block())

        @block.sync
        def _(sp):
            def load(b, kt):
                sp.dma_start(raw[:, kt % RAW, :],
                             io.context[bass.ds(b * NKT + kt, 1), :, :].rearrange("o p c -> (o p) c")
                             ).then_inc(raw_in[kt % RAW], 16)

            def reload(step, b):
                for kt in (2 * step[1], 2 * step[1] + 1):
                    sp.wait_ge(normed, b * NKT + kt + 1)
                    load(b, kt + RAW)

            for kt in range(RAW):
                load(0, kt)
            for n in AHEAD_LN:
                reload(("ln", n), 0)
            with sp.Fori(0, NB) as b:
                sp.wait_ge(tr, b * NKT + 1)
                for u in range(2):
                    for j in range(HPG):
                        sp.dma_start(t.k_stack[u][MASK_ROW:MASK_ROW + 1, j, :],
                                     io.mask_rows[bass.ds(b, 1), :]).then_inc(mask_in, 16)
                for step in steps:
                    step, bb = of_batch(step, b)
                    if step[0] == "ln":
                        reload(step, bb)
                    if step[0] == "k" and step[2] % 2 == 1:
                        g, h = step[1], step[2] // 2
                        u = g % 2
                        sp.wait_ge(k_lo_out, b * NG * NKB + NKB * g + 2 * h + 2)
                        for j in range(HPG):
                            for k, part in enumerate((k_hi[h], k_hi[h], k_lo[h])):
                                sp.dma_start(t.k_stack[u][HD * k:HD * (k + 1), j, 2 * KB * h:2 * KB * (h + 1)],
                                             part[HD * j:HD * (j + 1), :]).then_inc(k_in[u][h], 16)
            for i in range(RAW):
                sp.wait_ge(raw_in[i], (NB * (NKT // RAW) + 2) * 16)

        @block.gpsimd
        def _(pool):
            def deviations(n, b):
                two = slice(2 * (n % 2), 2 * (n % 2) + 2)
                pool.wait_ge(var_dve, b * (NKT // 2) + n + 1)
                for k, (x, y, op) in enumerate(((mv[:, two, 1], t.eps[:, 0:2], ALU.add),
                                                (rstd[:, two], t.inv_scale2[:, 0:2], ALU.mult),
                                                (rstd[:, two], t.half_neg[:, 0:2], ALU.pow))):
                    nc.gpsimd.tensor_tensor(rstd[:, two], x, y, op).then_inc(pool_pow, 1)
                    pool.wait_ge(pool_pow, (b * (NKT // 2) + n) * 3 + k + 1)

            deviations(0, 0)
            deviations(1, 0)
            with pool.Fori(0, NB) as b:
                n_add = 0
                for step in steps:
                    step, bb = of_batch(step, b)
                    if step[0] == "ln":
                        deviations(step[1], bb)
                    if step[0] == "sums":
                        g = step[1]
                        if g:
                            pool.wait_ge(dve_second, b * NG + g)
                        for p in range(1, 6):
                            pool.wait_ge(exp_done, b * NG * NPAIR + NPAIR * g + p + 1)
                            nc.gpsimd.tensor_tensor(acc_pool[:, :], pT[:, 0, :] if p == 1 else acc_pool[:, :],
                                                    pT[:, p % PT, :], ALU.add).then_inc(pool_add, 1)
                            n_add += 1
                            pool.wait_ge(pool_add, b * 5 * NG + n_add)

        @block.vector
        def _(v):
            def statistics(kt, b):
                v.wait_ge(raw_in[kt % RAW], (b * (NKT // RAW) + kt // RAW + 1) * 16)
                nc.vector.bn_stats(stats[:, kt % 4, :], raw[:, kt % RAW, :]).then_inc(stat_dve, 1)

            def variances(n, b):
                v.wait_ge(stat_dve, b * NKT + 2 * n + 2)
                nc.vector.memset(carrier[:, :], 0.0)
                for kt in (2 * n, 2 * n + 1):
                    last = nc.vector.bn_aggr(mv[:, kt % 4, :], stats[:, kt % 4, :])
                last.then_inc(var_dve, 1)

            def normalise(n, b):
                v.wait_ge(pool_pow, (b * (NKT // 2) + n + 1) * 3)
                for kt in (2 * n, 2 * n + 1):
                    if kt >= RAW:
                        v.wait_ge(tr, b * NKT + kt - RAW + 1)
                    nc.vector.tensor_scalar(xn[:, kt % RAW, :], raw[:, kt % RAW, :], mv[:, kt % 4, 0:1],
                                            rstd[:, kt % 4:kt % 4 + 1], ALU.subtract,
                                            ALU.mult).then_inc(normed, 1)

            def low_half(kt, b):
                if 2 <= kt < NKT - 2:
                    statistics(kt + 2, b)
                    if kt % 2:
                        variances(kt // 2 + 1, b)
                v.wait_ge(tr_hi, b * NKT + kt + 1)
                nc.vector.tensor_tensor(cT_lo[:, :, P * kt:P * (kt + 1)],
                                        ps_s[kt % 2][:, 0:KB].rearrange("p (c n) -> p c n", c=NC),
                                        cT_hi[:, :, P * kt:P * (kt + 1)], ALU.subtract).then_inc(tr_lo, 1)

            def first_tiles(b):
                for n in AHEAD_LN:
                    statistics(2 * n, b)
                    statistics(2 * n + 1, b)
                    variances(n, b)
                for n in AHEAD_LN:
                    normalise(n, b)

            first_tiles(0)
            for kt in AHEAD_T:
                low_half(kt, 0)
            with v.Fori(0, NB) as b:
                n_p1 = 0
                for step in steps:
                    step, bb = of_batch(step, b)
                    kind = step[0]
                    if kind == "ln":
                        if bb is b:
                            normalise(step[1], b)
                        elif step[1] == AHEAD_LN[-1]:
                            first_tiles(bb)
                    elif kind == "t":
                        low_half(step[1], bb)
                    elif kind == "k":
                        g, kb = step[1:]
                        n = NKB * g + kb
                        h, half = kb // 2, slice(KB * (kb % 2), KB * (kb % 2 + 1))
                        v.wait_ge(k_hi_out, b * NG * NKB + n + 1)
                        nc.vector.tensor_tensor(k_lo[h][:, half], k_f[:, kb % 2, :], k_hi[h][:, half],
                                                ALU.subtract).then_inc(k_lo_out, 1)
                    elif kind == "p1":
                        g, j, kb = step[1:]
                        n_p1 += 1
                        n = n_p1
                        v.wait_ge(p1_mm, b * PER_BATCH["p1"] + n)
                        nc.vector.tensor_reduce(mpart[:, j, kb:kb + 1], p1_bank(step, n - 1), AX.X,
                                                ALU.max).then_inc(p1_max, 1)
                        if (j, kb) == (HPG - 1, NKB - 1):
                            v.wait_ge(p1_max, b * PER_BATCH["p1"] + n)
                            nc.vector.tensor_reduce(mgroup[:, g % 2, :], mpart[:, :, :], AX.X,
                                                    ALU.max).then_inc(m_max, 1)
                    elif kind == "sums":
                        g = step[1]
                        v.wait_ge(exp_done, b * NG * NPAIR + NPAIR * (g + 1))
                        nc.vector.tensor_tensor(acc_dve[:, :], pT[:, 6 % PT, :], pT[:, 7 % PT, :],
                                                ALU.add).then_inc(dve_first, 1)
                        v.wait_ge(dve_first, b * NG + g + 1)
                        v.wait_ge(pool_add, b * 5 * NG + 5 * (g + 1))
                        nc.vector.tensor_tensor(acc_dve[:, :], acc_dve[:, :], acc_pool[:, :],
                                                ALU.add).then_inc(dve_second, 1)
                        v.wait_ge(dve_second, b * NG + g + 1)
                        if g:
                            v.wait_ge(den_mm, b * NG + g)
                        nc.vector.tensor_tensor(acc[:, :], acc_dve[:, 0:KB], acc_dve[:, KB:2 * KB],
                                                ALU.add).then_inc(sums_done, 1)
                    elif kind == "den":
                        g = step[1]
                        v.wait_ge(den_mm, b * NG + g + 1)
                        nc.vector.reciprocal(rden[:, :], ps_o[g % 2][:, P:2 * P]).then_inc(rden_done, 1)
                        v.wait_ge(rden_done, b * NG + g + 1)
                        nc.vector.tensor_tensor(oT[:, g, :], ps_o[g % 2][:, 0:P], rden[:, :],
                                                ALU.mult).then_inc(norm_out, 1)
                        v.wait_ge(norm_out, b * NG + g + 1)
                        nc.vector.tensor_scalar(oT[:, g, :], oT[:, g, :], t.vbias[:, g:g + 1], None,
                                                ALU.add).then_inc(fin, 1)
                    elif kind == "op":
                        v.wait_ge(op_mm, b + 1)
                        here = t.x[:, bass.ds(b, 1), :].rearrange("p o c -> p (o c)")
                        nc.vector.tensor_tensor(here, ps_s[0][:, KB:2 * KB], here, ALU.add).then_inc(x_done, 1)

        @block.scalar
        def _(act):
            def high_half(kt, b):
                act.wait_ge(tr, b * NKT + kt + 1)
                nc.scalar.activation(cT_hi[:, :, P * kt:P * (kt + 1)],
                                     ps_s[kt % 2][:, 0:KB].rearrange("p (c n) -> p c n", c=NC),
                                     ACT.Copy).then_inc(tr_hi, 1)

            def values_out(kt, b):
                act.wait_ge(v_mm, b * NKT + kt + 1)
                nc.scalar.activation(vals[:, kt, :], ps_r[ring_place(("v", kt)) % 2][:, :], ACT.Copy,
                                     scale=UNSCALE).then_inc(v_out, 1)

            for kt in AHEAD_T:
                high_half(kt, 0)
            for kt in AHEAD_V:
                values_out(kt, 0)
            with act.Fori(0, NB) as b:
                def exp(g, p):
                    n = NPAIR * g + p
                    act.wait_ge(s_mm, b * NG * NPAIR + n + 1)
                    if n >= PT:
                        act.wait_ge(av_mm, b * NG * NPAIR + n - PT + 1)
                        q = (n - PT) % NPAIR
                        before = (n - PT) // NPAIR
                        if q < 6:
                            act.wait_ge(pool_add, b * 5 * NG + 5 * before + max(q, 1))
                        else:
                            act.wait_ge(dve_first, b * NG + before + 1)
                    nc.scalar.activation(pT[:, p % PT, :], ps_s[p % 2][:, :], ACT.Exp,
                                         scale=SM_SCALE).then_inc(exp_done, 1)

                for step in steps:
                    step, bb = of_batch(step, b)
                    kind = step[0]
                    if kind == "t":
                        high_half(step[1], bb)
                    elif kind == "v" and step[2] == NC - 1:
                        values_out(step[1], bb)
                    elif kind == "k":
                        g, kb = step[1:]
                        n = NKB * g + kb
                        h, half = kb // 2, slice(KB * (kb % 2), KB * (kb % 2 + 1))
                        act.wait_ge(k_mm, b * NG * NKB + n + 1)
                        if n >= 2:
                            act.wait_ge(k_lo_out, b * NG * NKB + n - 1)
                        nc.scalar.activation(k_f[:, kb % 2, :], ps_r[ring_place(step) % 2][:, :], ACT.Identity,
                                             bias=t.kbias[:, g:g + 1], scale=UNSCALE).then_inc(k_f_out, 1)
                        act.wait_ge(k_f_out, b * NG * NKB + n + 1)
                        if g:
                            act.wait_ge(k_in[(g - 1) % 2][h], (b * 2 + (g - 1) // 2 + 1) * KIN)
                        nc.scalar.activation(k_hi[h][:, half], k_f[:, kb % 2, :], ACT.Copy).then_inc(k_hi_out, 1)
                    elif kind == "mt":
                        g = step[1]
                        act.wait_ge(mt_mm, b * NG + g + 1)
                        nc.scalar.activation(
                            t.q_stack[SHIFT_ROW:SHIFT_ROW + 1, HPG * g:HPG * (g + 1), bass.ds(b * P, P)],
                            ps_r[ring_place(step) % 2][SHIFT_ROW:SHIFT_ROW + 1, :].rearrange("o (j n) -> o j n", j=HPG),
                            ACT.Copy, scale=-1.0).then_inc(m_row, 1)
                    elif kind == "s" and step[3] == 1:
                        exp(*step[1:3])

        @block.tensor
        def _(pe):
            def transposes(kt, b):
                pe.wait_ge(normed, b * NKT + kt + 1)
                if kt >= 2:
                    pe.wait_ge(tr_lo, b * NKT + kt - 1)
                for c in range(NC):
                    last = nc.tensor.transpose(ps_s[kt % 2][:, P * c:P * (c + 1)],
                                               xn[:, kt % RAW, P * c:P * (c + 1)], t.ident[:, :])
                last.then_inc(tr, 1)

            released = {"v": v_out, "k": k_f_out, "p1": p1_max, "mt": m_row}

            def ring_bank(step, b):
                n = ring_place(step)
                kind = ring[n - 2][0]
                if n >= 2:
                    before = sum(r[0] == kind for r in ring[:n - 1]) + (HPG * NKB if kind == "p1" else 0)
                    pe.wait_ge(released[kind], b * PER_BATCH[kind] + before)
                return ps_r[n % 2]

            def values_quarter(kt, c, b):
                if c == 0:
                    ring_bank(("v", kt), b)
                    pe.wait_ge(tr_lo, b * NKT + kt + 1)
                bank, keys = ps_r[ring_place(("v", kt)) % 2], slice(P * kt, P * (kt + 1))
                nc.tensor.matmul(bank[:, :], cT_hi[:, c, keys], t.wv_hi[:, c, :], start=(c == 0), stop=False)
                nc.tensor.matmul(bank[:, :], cT_hi[:, c, keys], t.wv_lo[:, c, :], start=False, stop=False)
                last = nc.tensor.matmul(bank[:, :], cT_lo[:, c, keys], t.wv_hi[:, c, :], start=False,
                                        stop=(c == NC - 1))
                if c == NC - 1:
                    last.then_inc(v_mm, 1)

            for kt in AHEAD_T:
                transposes(kt, 0)
            for kt in AHEAD_V:
                for c in range(NC):
                    values_quarter(kt, c, 0)
            with pe.Fori(0, NB) as b:
                n_p1 = 0
                for step in steps:
                    step, bb = of_batch(step, b)
                    kind = step[0]
                    if kind == "t":
                        transposes(step[1], bb)
                    elif kind == "v":
                        kt, c = step[1:]
                        values_quarter(kt, c, bb)
                    elif kind == "k":
                        g, kb = step[1:]
                        bank = ring_bank(step, b)
                        if kb == 0:
                            pe.wait_ge(tr_lo, b * NKT + NKT)
                        col, keys = slice(P * g, P * (g + 1)), slice(KB * kb, KB * (kb + 1))
                        for c in range(NC):
                            nc.tensor.matmul(bank[:, :], t.wk_hi[:, c, col], cT_hi[:, c, keys], start=(c == 0), stop=False)
                            nc.tensor.matmul(bank[:, :], t.wk_hi[:, c, col], cT_lo[:, c, keys], start=False, stop=False)
                            last = nc.tensor.matmul(bank[:, :], t.wk_lo[:, c, col], cT_hi[:, c, keys], start=False,
                                                    stop=(c == NC - 1))
                        last.then_inc(k_mm, 1)
                    elif kind == "p1":
                        g, j, kb = step[1:]
                        if g:
                            ring_bank(step, b)
                        elif n_p1 >= 4:
                            pe.wait_ge(p1_max, b * PER_BATCH["p1"] + n_p1 - 3)
                        bank = p1_bank(step, n_p1)
                        n_p1 += 1
                        if (g, j, kb) == (0, 0, 0):
                            pe.wait_ge(mask_in, (b + 1) * 16 * 2 * HPG)
                        if j == 0 and kb % 2 == 0:
                            pe.wait_ge(k_in[g % 2][kb // 2], (b * 2 + g // 2 + 1) * KIN)
                        nc.tensor.matmul(bank, t.q_stack[0:ROWS, HPG * g + j, bass.ds(b * P, P)],
                                         t.k_stack[g % 2][0:ROWS, j, KB * kb:KB * (kb + 1)],
                                         start=True, stop=True).then_inc(p1_mm, 1)
                    elif kind == "mt":
                        g = step[1]
                        bank = ring_bank(step, b)
                        pe.wait_ge(m_max, b * NG + g + 1)
                        for j in range(HPG):
                            last = nc.tensor.matmul(bank[SHIFT_ROW:SHIFT_ROW + 1, P * j:P * (j + 1)],
                                                    mgroup[:, g % 2, j:j + 1], t.ident[:, :], start=True, stop=True)
                        last.then_inc(mt_mm, 1)
                    elif kind == "s":
                        g, p, i = step[1:]
                        n = NPAIR * g + p
                        if n >= 2 and i == 0:
                            pe.wait_ge(exp_done, b * NG * NPAIR + n - 1)
                        if p == 0 and i == 0:
                            pe.wait_ge(m_row, b * NG + g + 1)
                        for j in range(HPG):
                            at = KB * i + P * j
                            kt = 2 * p + i
                            last = nc.tensor.matmul(ps_s[p % 2][:, at:at + P],
                                                    t.k_stack[g % 2][0:ROWS, j, P * kt:P * (kt + 1)],
                                                    t.q_stack[0:ROWS, HPG * g + j, bass.ds(b * P, P)],
                                                    start=True, stop=True)
                        if i == 1:
                            last.then_inc(s_mm, 1)
                    elif kind == "av":
                        g, p, i = step[1:]
                        if i == 0:
                            pe.wait_ge(exp_done, b * NG * NPAIR + NPAIR * g + p + 1)
                            if g >= 2 and p == 0:
                                pe.wait_ge(fin, b * NG + g - 1)
                        for j in range(HPG):
                            at = KB * i + P * j
                            head = HD * (HPG * g + j)
                            last = nc.tensor.matmul(ps_o[g % 2][HD * j:HD * (j + 1), 0:P],
                                                    vals[:, 2 * p + i, head:head + HD],
                                                    pT[:, p % PT, at:at + P], start=(p == 0 and i == 0),
                                                    stop=(p == NPAIR - 1 and i == 1))
                        if i == 1:
                            last.then_inc(av_mm, 1)
                    elif kind == "den":
                        g = step[1]
                        pe.wait_ge(sums_done, b * NG + g + 1)
                        for j in range(HPG):
                            last = nc.tensor.matmul(ps_o[g % 2][HD * j:HD * (j + 1), P:2 * P], t.ones32[:, :],
                                                    acc[:, P * j:P * (j + 1)], start=True, stop=True)
                        last.then_inc(den_mm, 1)
                    elif kind == "op":
                        pe.wait_ge(fin, b * NG + NG)
                        pe.wait_ge(s.wo_in, 16)
                        for g in range(NG):
                            last = nc.tensor.matmul(ps_s[0][:, KB:2 * KB], oT[:, g, :], t.wo[:, g, :],
                                                    start=(g == 0), stop=(g == NG - 1))
                        last.then_inc(op_mm, 1)


def self_attention(nc, io, t, s):
    with ExitStack() as ctx:
        def sb(name, shape, dt=F32):
            return ctx.enter_context(nc.sbuf_tensor(name, shape, dt))

        def sem(name):
            return ctx.enter_context(nc.semaphore(name))

        w_raw = [sb(f"a_raw{i}", [P, NC, D]) for i in range(3)]
        w_hi = [sb(f"a_hi{i}", [P, NC, D], F16) for i in range(3)]
        w_lo = [sb(f"a_lo{i}", [P, NC, D], F16) for i in range(3)]
        w_out = sb("a_wo", [P, NC, D])
        bias = sb("a_bias", [P, 4, D])
        rope = sb("a_rope", [P, 2, HD])
        stats, mv, rstd = sb("a_stats", [P, NB, 6]), sb("a_mv", [P, NB, 2]), sb("a_rstd", [P, NB])
        hat = sb("a_hat", [P, NB, D])
        xT_hi, xT_lo = sb("a_xT_hi", [P, 2, NC, P], F16), sb("a_xT_lo", [P, 2, NC, P], F16)
        qkv = sb("a_qkv", [P, 2, 3, D])
        rot, cosed = sb("a_rot", [P, 2, D]), sb("a_cosed", [P, 2, D])
        qkT = sb("a_qkT", [P, 2, 2, NG, P])
        m, rsum, rinv = sb("a_m", [P, HEADS]), sb("a_rsum", [P, HEADS]), sb("a_rinv", [P, HEADS])
        prob = sb("a_prob", [P, HEADS, P])
        probT = sb("a_probT", [P, HEADS, P])
        oT = sb("a_oT", [P, NG, P])
        ps_a = [ctx.enter_context(nc.psum_tensor(f"a_ps{i}", [P, D], F32)) for i in range(4)]
        ps_p = ctx.enter_context(nc.psum_tensor("a_psp", [P, HEADS, P], F32))

        w_in, misc_in = [sem(f"a_w_in{i}") for i in range(4)], sem("a_misc_in")
        st, var, powed, normed = sem("a_st"), sem("a_var"), sem("a_pow"), sem("a_normed")
        hi_done, lo_done = sem("a_hi_done"), sem("a_lo_done")
        tr, tr_hi, tr_lo = sem("a_tr"), sem("a_tr_hi"), sem("a_tr_lo")
        mm, biased = sem("a_mm"), sem("a_biased")
        cos_done, rot_done, roped = sem("a_cos"), sem("a_rot_s"), sem("a_roped")
        qk_tr, qk_out = sem("a_qk_tr"), sem("a_qk_out")
        scored, maxed, exped, inv, scaled = sem("a_scored"), sem("a_maxed"), sem("a_exped"), sem("a_inv"), sem("a_scaled")
        p_tr, p_out, o_mm, o_out, y_mm, y_out = (sem("a_p_tr"), sem("a_p_out"), sem("a_o_mm"), sem("a_o_out"),
                                                 sem("a_y_mm"), sem("a_y_out"))
        def slot(h):
            return NG * (h % HPG) + h // HPG

        order = [("front", 0)]
        for b in range(1, NB):
            order += [("front", b), ("back", b - 1)]
        order.append(("back", NB - 1))
        block = ctx.enter_context(nc.Block())

        @block.sync
        def _(sp):
            for i, w in enumerate((io.a_wqT, io.a_wkT, io.a_wvT)):
                sp.dma_start(w_raw[i][:, :, :], chunked(w)).then_inc(w_in[i], 16)
            sp.dma_start(rope[:, :, :], io.rope).then_inc(misc_in, 16)
            for i, v in enumerate((io.a_bq, io.a_bk, io.a_bv, io.a_bo)):
                sp.dma_start(bias[:, i, :], v.partition_broadcast(P)).then_inc(misc_in, 16)
            sp.dma_start(w_out[:, :, :], chunked(io.a_woT)).then_inc(w_in[3], 16)

        @block.gpsimd
        def _(pool):
            pool.wait_ge(var, 1)
            for k, (x, y, op) in enumerate(((mv[:, :, 1], t.eps[:, :], ALU.add),
                                            (rstd[:, :], t.inv_scale2[:, :], ALU.mult),
                                            (rstd[:, :], t.half_neg[:, :], ALU.pow))):
                nc.gpsimd.tensor_tensor(rstd[:, :], x, y, op).then_inc(powed, 1)
                pool.wait_ge(powed, k + 1)
            pool.wait_ge(misc_in, 16 * 5)
            for b in range(NB):
                for i in range(2):
                    n = 2 * b + i
                    src = qkv[:, b % 2, i, :].rearrange("p (h k) -> p h k", k=HD)
                    dst = rot[:, i, :].rearrange("p (h k) -> p h k", k=HD)
                    pool.wait_ge(biased, 3 * b + i + 1)
                    if n >= 2:
                        pool.wait_ge(roped, n - 1)
                    for half in range(2):
                        here, there = slice(HD // 2 * half, HD // 2 * (half + 1)), slice(HD // 2 * (1 - half), HD // 2 * (2 - half))
                        sines = rope[:, 1:2, here].broadcast_to([P, HEADS, HD // 2])
                        nc.gpsimd.tensor_tensor(dst[:, :, here], src[:, :, there], sines,
                                                ALU.mult).then_inc(rot_done, 1)
                        pool.wait_ge(rot_done, 2 * n + half + 1)

        @block.vector
        def _(v):
            for b in range(NB):
                nc.vector.bn_stats(stats[:, b, :], t.x[:, b, :]).then_inc(st, 1)
            v.wait_ge(st, NB)
            for b in range(NB):
                last = nc.vector.bn_aggr(mv[:, b, :], stats[:, b, :])
            last.then_inc(var, 1)
            v.wait_ge(powed, 3)
            for b in range(NB):
                nc.vector.tensor_scalar(hat[:, b, :], t.x[:, b, :], mv[:, b, 0:1], rstd[:, b:b + 1],
                                        ALU.subtract, ALU.mult).then_inc(normed, 1)
            v.wait_ge(misc_in, 16 * 5)
            for kind, b in order:
                if kind == "front":
                    v.wait_ge(tr_hi, b + 1)
                    nc.vector.tensor_tensor(xT_lo[:, b % 2, :, :],
                                            ps_a[0][:, :].rearrange("p (c n) -> p c n", c=NC),
                                            xT_hi[:, b % 2, :, :], ALU.subtract).then_inc(tr_lo, 1)
                    for i in range(3):
                        if b == 0:
                            v.wait_ge(hi_done, i + 1)
                            nc.vector.scalar_tensor_tensor(
                                out=w_lo[i][:, :, :].rearrange("p c n -> p (c n)"),
                                in0=w_raw[i][:, :, :].rearrange("p c n -> p (c n)"), scalar=W_SCALE,
                                in1=w_hi[i][:, :, :].rearrange("p c n -> p (c n)"), op0=ALU.mult,
                                op1=ALU.subtract).then_inc(lo_done, 1)
                    for i in range(3):
                        n = 3 * b + i
                        v.wait_ge(mm, n + 1)
                        if b >= 2 and i == 2:
                            v.wait_ge(o_mm, b - 1)
                        nc.vector.scalar_tensor_tensor(out=qkv[:, b % 2, i, :], in0=ps_a[1 + n % 2][:, :],
                                                       scalar=UNSCALE, in1=bias[:, i, :], op0=ALU.mult,
                                                       op1=ALU.add).then_inc(biased, 1)
                        if i < 2:
                            n = 2 * b + i
                            v.wait_ge(biased, 3 * b + i + 1)
                            cosines = rope[:, 0:1, :].broadcast_to([P, HEADS, HD])
                            nc.vector.tensor_tensor(cosed[:, i, :].rearrange("p (h k) -> p h k", k=HD),
                                                    qkv[:, b % 2, i, :].rearrange("p (h k) -> p h k", k=HD),
                                                    cosines, ALU.mult).then_inc(cos_done, 1)
                    for i in range(2):
                        n = 2 * b + i
                        v.wait_ge(cos_done, n + 1)
                        v.wait_ge(rot_done, 2 * n + 2)
                        nc.vector.tensor_tensor(qkv[:, b % 2, i, :], cosed[:, i, :], rot[:, i, :],
                                                ALU.add).then_inc(roped, 1)
                else:
                    v.wait_ge(scored, b + 1)
                    nc.vector.tensor_reduce(m[:, :], ps_p[:, :, :], AX.X, ALU.max).then_inc(maxed, 1)
                    v.wait_ge(maxed, 2 * b + 1)
                    nc.vector.tensor_scalar(m[:, :], m[:, :], -SM_SCALE, None, ALU.mult).then_inc(maxed, 1)
                    v.wait_ge(exped, b + 1)
                    nc.vector.reciprocal(rinv[:, :], rsum[:, :]).then_inc(inv, 1)
                    v.wait_ge(inv, b + 1)
                    nc.vector.tensor_tensor(prob[:, :, :], prob[:, :, :],
                                            rinv[:, :].unsqueeze(2).broadcast_to([P, HEADS, P]),
                                            ALU.mult).then_inc(scaled, 1)
                    v.wait_ge(p_tr, b + 1)
                    nc.vector.tensor_copy(probT[:, HEADS // 2:HEADS, :], ps_p[:, HEADS // 2:HEADS, :]).then_inc(p_out, 1)
                    v.wait_ge(y_mm, b + 1)
                    nc.vector.tensor_tensor(hat[:, b, :], ps_a[3][:, :], bias[:, 3, :], ALU.add).then_inc(y_out, 1)
                    v.wait_ge(y_out, 2 * b + 1)
                    nc.vector.tensor_tensor(t.x[:, b, :], t.x[:, b, :], hat[:, b, :], ALU.add).then_inc(y_out, 1)

        @block.scalar
        def _(act):
            for kind, b in order:
                if kind == "front":
                    if b == 0:
                        for i in range(3):
                            act.wait_ge(w_in[i], 16)
                            nc.scalar.activation(w_hi[i][:, :, :], w_raw[i][:, :, :], ACT.Copy,
                                                 scale=W_SCALE).then_inc(hi_done, 1)
                    act.wait_ge(tr, b + 1)
                    nc.scalar.activation(xT_hi[:, b % 2, :, :], ps_a[0][:, :].rearrange("p (c n) -> p c n", c=NC),
                                         ACT.Copy).then_inc(tr_hi, 1)
                    for i in range(2):
                        n = 2 * b + i
                        act.wait_ge(qk_tr, n + 1)
                        nc.scalar.activation(qkT[:, b % 2, i, :, :], ps_a[1 + i][:, :].rearrange("p (g n) -> p g n", g=NG),
                                             ACT.Copy).then_inc(qk_out, 1)
                else:
                    act.wait_ge(maxed, 2 * b + 2)
                    if b:
                        act.wait_ge(p_tr, b)
                    for h in range(HEADS):
                        last = nc.scalar.activation(prob[:, h, :], ps_p[:, h, :], ACT.Exp, bias=m[:, h:h + 1],
                                                    scale=SM_SCALE, accum_out=rsum[:, h:h + 1])
                    last.then_inc(exped, 1)
                    act.wait_ge(p_tr, b + 1)
                    nc.scalar.activation(probT[:, 0:HEADS // 2, :], ps_p[:, 0:HEADS // 2, :], ACT.Copy).then_inc(p_out, 1)
                    act.wait_ge(o_mm, b + 1)
                    nc.scalar.activation(oT[:, :, :], ps_a[3][:, :].rearrange("p (g n) -> p g n", g=NG),
                                         ACT.Copy).then_inc(o_out, 1)

        @block.tensor
        def _(pe):
            for kind, b in order:
                if kind == "front":
                    pe.wait_ge(normed, b + 1)
                    if b:
                        pe.wait_ge(tr_lo, b)
                    for c in range(NC):
                        last = nc.tensor.transpose(ps_a[0][:, P * c:P * (c + 1)], hat[:, b, P * c:P * (c + 1)],
                                                   t.ident[:, :])
                    last.then_inc(tr, 1)
                    pe.wait_ge(tr_lo, b + 1)
                    for i in range(3):
                        n = 3 * b + i
                        if b == 0:
                            pe.wait_ge(lo_done, i + 1)
                        if i < 2 and b:
                            pe.wait_ge(qk_out, 2 * b)
                        if n >= 2:
                            pe.wait_ge(biased, n - 1)
                        bank = ps_a[1 + n % 2]
                        for c in range(NC):
                            nc.tensor.matmul(bank[:, :], xT_hi[:, b % 2, c, :], w_hi[i][:, c, :], start=(c == 0), stop=False)
                            nc.tensor.matmul(bank[:, :], xT_hi[:, b % 2, c, :], w_lo[i][:, c, :], start=False, stop=False)
                            last = nc.tensor.matmul(bank[:, :], xT_lo[:, b % 2, c, :], w_hi[i][:, c, :], start=False,
                                                    stop=(c == NC - 1))
                        last.then_inc(mm, 1)
                    for i in range(2):
                        pe.wait_ge(roped, 2 * b + i + 1)
                        pe.wait_ge(biased, 3 * b + 3)
                        for g in range(NG):
                            last = nc.tensor.transpose(ps_a[1 + i][:, P * g:P * (g + 1)],
                                                       qkv[:, b % 2, i, P * g:P * (g + 1)], t.ident[:, :])
                        last.then_inc(qk_tr, 1)
                else:
                    pe.wait_ge(qk_out, 2 * b + 2)
                    if b:
                        pe.wait_ge(p_out, 2 * b)
                    for h in range(HEADS):
                        g, rows = h // HPG, slice(HD * (h % HPG), HD * (h % HPG + 1))
                        last = nc.tensor.matmul(ps_p[:, slot(h), :], qkT[rows, b % 2, 0, g, :], qkT[rows, b % 2, 1, g, :],
                                                start=True, stop=True)
                    last.then_inc(scored, 1)
                    pe.wait_ge(scaled, b + 1)
                    for h in range(HEADS):
                        last = nc.tensor.transpose(ps_p[:, h, :], prob[:, h, :], t.ident[:, :])
                    last.then_inc(p_tr, 1)
                    pe.wait_ge(p_out, 2 * b + 2)
                    if b:
                        pe.wait_ge(y_out, 2 * b)
                    for h in range(HEADS):
                        g, rows = h // HPG, slice(HD * (h % HPG), HD * (h % HPG + 1))
                        last = nc.tensor.matmul(ps_a[3][rows, P * g:P * (g + 1)], qkv[:, b % 2, 2, HD * h:HD * (h + 1)],
                                                probT[:, slot(h), :], start=True, stop=True)
                    last.then_inc(o_mm, 1)
                    pe.wait_ge(o_out, b + 1)
                    pe.wait_ge(w_in[3], 16)
                    for g in range(NG):
                        last = nc.tensor.matmul(ps_a[3][:, :], oT[:, g, :], w_out[:, g, :], start=(g == 0),
                                                stop=(g == NG - 1))
                    last.then_inc(y_mm, 1)


def mixture(nc, io, t, s):
    with ExitStack() as ctx:
        def sb(name, shape, dt=F32):
            return ctx.enter_context(nc.sbuf_tensor(name, shape, dt))

        def sem(name):
            return ctx.enter_context(nc.semaphore(name))

        w1_raw, w2_raw = sb("w1_raw", [P, NC, FF]), sb("w2_raw", [P, NF, D])
        w1_hi, w1_lo = sb("w1_hi", [P, NC, FF], F16), sb("w1_lo", [P, NC, FF], F16)
        w2_hi, w2_lo = sb("w2_hi", [P, NF, D], F16), sb("w2_lo", [P, NF, D], F16)
        xT_hi, xT_lo = sb("m_xT_hi", [P, NC, TOK], F16), sb("m_xT_lo", [P, NC, TOK], F16)
        h_f = sb("h_f", [P, 2, TOK])
        h_hi, h_lo = sb("h_hi", [P, NF, TOK], F16), sb("h_lo", [P, NF, TOK], F16)
        stats, mv, rstd = sb("m_stats", [P, 2, NB, 6]), sb("m_mv", [P, 2, NB, 2]), sb("m_rstd", [P, 2, NB])
        hat, hat2 = sb("m_hat", [P, NB, D]), sb("m_hat2", [P, NB, D])
        gT = sb("gT", [P, NC, TOK])
        affine, gate = sb("affine", [P, 2, NC]), sb("gate", [P, NC, EXPERTS])
        rank = sb("rank", [P, NB, EXPERTS])
        prob, left = sb("m_prob", [P, NB, EXPERTS]), sb("m_left", [P, NB, EXPERTS])
        best, first = sb("m_best", [P, NB]), sb("m_first", [P, NB])
        sel = sb("m_sel", [P, 2, NB, EXPERTS])
        comb = sb("m_comb", [P, NB, EXPERTS])
        ps_h = [ctx.enter_context(nc.psum_tensor(f"ps_h{i}", [P, TOK], F32)) for i in range(2)]
        ps_y = [ctx.enter_context(nc.psum_tensor(f"ps_y{i}", [P, D], F32)) for i in range(NB)]
        ps_g = ctx.enter_context(nc.psum_tensor("ps_g", [P, NB, EXPERTS], F32))

        misc_in, w1_in, w2_in = sem("m_misc_in"), sem("w1_in"), sem("w2_in")
        st, var, powed, chain = sem("m_st"), sem("m_var"), sem("m_pow"), sem("m_chain")
        normed, ranked = sem("m_normed"), sem("ranked")
        tr, tr_hi, tr_lo, g_tr, g_out, g_mm, g_exp = (sem("m_tr"), sem("m_tr_hi"), sem("m_tr_lo"), sem("g_tr"),
                                                      sem("g_out"), sem("g_mm"), sem("g_exp"))
        w1_hi_s, w1_lo_s, w2_hi_s, w2_lo_s = sem("w1_hi_s"), sem("w1_lo_s"), sem("w2_hi_s"), sem("w2_lo_s")
        up, gelu, h_hi_s, h_lo_s, down, y_out = (sem("up"), sem("gelu"), sem("h_hi_s"), sem("h_lo_s"), sem("down"),
                                                 sem("m_y_out"))
        out_sem = sem("out_sem")
        block = ctx.enter_context(nc.Block())

        def w1_part(n):
            return slice(n // 2, n // 2 + 1), slice(FF // 2 * (n % 2), FF // 2 * (n % 2 + 1))

        @block.sync
        def _(sp):
            sp.dma_start(w1_raw[:, :, :], io.w1[0:1, :, :, :].rearrange("e p c n -> (e p) c n")).then_inc(w1_in, 16)
            sp.dma_start(w2_raw[:, :, :], io.w2[0:1, :, :, :].rearrange("e p c n -> (e p) c n")).then_inc(w2_in, 16)
            sp.dma_start(affine[:, :, :], io.affine).then_inc(misc_in, 16)
            sp.dma_start(gate[:, :, :], io.gate).then_inc(misc_in, 16)
            sp.wait_ge(w1_lo_s, NF)
            sp.dma_start(w1_raw[:, :, :], io.w1[1:2, :, :, :].rearrange("e p c n -> (e p) c n")).then_inc(w1_in, 16)
            with sp.Fori(0, EXPERTS) as e:
                sp.wait_ge(w2_lo_s, (e + 1) * NF)
                sp.dma_start(w2_raw[:, :, :],
                             io.w2[bass.ds(e + 1, 1), :, :, :].rearrange("e p c n -> (e p) c n")).then_inc(w2_in, 16)
                sp.wait_ge(w1_lo_s, (e + 2) * NF)
                sp.dma_start(w1_raw[:, :, :],
                             io.w1[bass.ds(e + 2, 1), :, :, :].rearrange("e p c n -> (e p) c n")).then_inc(w1_in, 16)
            sp.wait_ge(w1_in, 16 * (EXPERTS + 2))
            sp.wait_ge(w2_in, 16 * (EXPERTS + 1))
            sp.wait_ge(y_out, NB * EXPERTS)
            sp.dma_start(io.out.rearrange("b t c -> t b c"), t.x[:, :, :]).then_inc(out_sem, 16)
            sp.wait_ge(out_sem, 16)

        @block.gpsimd
        def _(pool):
            for i in range(EXPERTS):
                nc.gpsimd.memset(rank[:, :, i:i + 1], float(EXPERTS - i)).then_inc(ranked, 1)
                pool.wait_ge(ranked, i + 1)
            for k in range(2):
                pool.wait_ge(var, k + 1)
                nc.gpsimd.tensor_tensor(rstd[:, k, :], mv[:, k, :, 1], t.eps[:, :], ALU.add).then_inc(powed, 1)
                pool.wait_ge(powed, 2 * k + 1)
                nc.gpsimd.tensor_tensor(rstd[:, k, :], rstd[:, k, :], t.half_neg[:, :], ALU.pow).then_inc(powed, 1)
                pool.wait_ge(powed, 2 * k + 2)

        @block.vector
        def _(v):
            done = [0]

            def then_wait(ins):
                done[0] += 1
                ins.then_inc(chain, 1)
                v.wait_ge(chain, done[0])

            for k, (src, dst) in enumerate(((t.x, hat), (hat, hat2))):
                for b in range(NB):
                    nc.vector.bn_stats(stats[:, k, b, :], src[:, b, :]).then_inc(st, 1)
                v.wait_ge(st, NB * (k + 1))
                for b in range(NB):
                    last = nc.vector.bn_aggr(mv[:, k, b, :], stats[:, k, b, :])
                last.then_inc(var, 1)
                v.wait_ge(var, k + 1)
                v.wait_ge(powed, 2 * k + 2)
                for b in range(NB):
                    nc.vector.tensor_scalar(dst[:, b, :], src[:, b, :], mv[:, k, b, 0:1], rstd[:, k, b:b + 1],
                                            ALU.subtract, ALU.mult).then_inc(normed, 1)
                v.wait_ge(normed, NB * (k + 1))

            def split_w1(n, e):
                c, half = w1_part(n)
                v.wait_ge(w1_hi_s, e * NF + n + 1)
                nc.vector.scalar_tensor_tensor(out=w1_lo[:, c, half].rearrange("p c n -> p (c n)"),
                                               in0=w1_raw[:, c, half].rearrange("p c n -> p (c n)"), scalar=W_SCALE,
                                               in1=w1_hi[:, c, half].rearrange("p c n -> p (c n)"), op0=ALU.mult,
                                               op1=ALU.subtract).then_inc(w1_lo_s, 1)

            for b in range(NB):
                v.wait_ge(tr_hi, b + 1)
                nc.vector.scalar_tensor_tensor(out=xT_lo[:, :, P * b:P * (b + 1)],
                                               in0=ps_h[b % 2][:, :].rearrange("p (c n) -> p c n", c=NC), scalar=A_SCALE,
                                               in1=xT_hi[:, :, P * b:P * (b + 1)], op0=ALU.mult,
                                               op1=ALU.subtract).then_inc(tr_lo, 1)
            for n in range(NF):
                split_w1(n, 0)
            v.wait_ge(g_mm, 1)
            wide = [P, NB, EXPERTS]
            then_wait(nc.vector.tensor_reduce(best[:, :], ps_g[:, :, :], AX.X, ALU.max))
            then_wait(nc.vector.tensor_tensor(prob[:, :, :], ps_g[:, :, :], best[:, :].unsqueeze(2).broadcast_to(wide),
                                              ALU.subtract))
            v.wait_ge(g_exp, 1)
            then_wait(nc.vector.tensor_reduce(best[:, :], prob[:, :, :], AX.X, ALU.add))
            then_wait(nc.vector.reciprocal(best[:, :], best[:, :]))
            then_wait(nc.vector.tensor_tensor(prob[:, :, :], prob[:, :, :], best[:, :].unsqueeze(2).broadcast_to(wide),
                                              ALU.mult))
            v.wait_ge(ranked, EXPERTS)
            for k in range(2):
                src = prob if k == 0 else left
                now = sel[:, k, :, :]
                then_wait(nc.vector.tensor_reduce(best[:, :], src[:, :, :], AX.X, ALU.max))
                then_wait(nc.vector.tensor_tensor(now, src[:, :, :], best[:, :].unsqueeze(2).broadcast_to(wide),
                                                  ALU.is_equal))
                then_wait(nc.vector.tensor_tensor(now, now, rank[:, :, :], ALU.mult))
                then_wait(nc.vector.tensor_reduce(first[:, :], now, AX.X, ALU.max))
                then_wait(nc.vector.tensor_tensor(now, now, first[:, :].unsqueeze(2).broadcast_to(wide), ALU.is_equal))
                if k == 0:
                    then_wait(nc.vector.scalar_tensor_tensor(
                        out=left[:, :, :].rearrange("p b e -> p (b e)"), in0=now.rearrange("p b e -> p (b e)"), scalar=-4.0,
                        in1=prob[:, :, :].rearrange("p b e -> p (b e)"), op0=ALU.mult, op1=ALU.add))
            then_wait(nc.vector.tensor_tensor(sel[:, 0, :, :], sel[:, 0, :, :], sel[:, 1, :, :], ALU.add))
            then_wait(nc.vector.tensor_tensor(comb[:, :, :], sel[:, 0, :, :], prob[:, :, :], ALU.mult))
            then_wait(nc.vector.tensor_scalar(comb[:, :, :], comb[:, :, :], UNSCALE, None, ALU.mult))

            with v.Fori(0, EXPERTS) as e:
                for f in range(NF):
                    v.wait_ge(h_hi_s, e * NF + f + 1)
                    nc.vector.scalar_tensor_tensor(out=h_lo[:, f, :], in0=h_f[:, f % 2, :], scalar=A_SCALE,
                                                   in1=h_hi[:, f, :], op0=ALU.mult, op1=ALU.subtract).then_inc(h_lo_s, 1)
                    v.wait_ge(w2_hi_s, e * NF + f + 1)
                    nc.vector.scalar_tensor_tensor(out=w2_lo[:, f, :], in0=w2_raw[:, f, :], scalar=W_SCALE,
                                                   in1=w2_hi[:, f, :], op0=ALU.mult, op1=ALU.subtract).then_inc(w2_lo_s, 1)
                for n in range(NF):
                    split_w1(n, e + 1)
                v.wait_ge(down, e + 1)
                for b in range(NB):
                    nc.vector.scalar_tensor_tensor(
                        out=t.x[:, b, :], in0=ps_y[b][:, :],
                        scalar=comb[:, b, bass.ds(e, 1)], in1=t.x[:, b, :], op0=ALU.mult, op1=ALU.add).then_inc(y_out, 1)

        @block.scalar
        def _(act):
            def split_w1(n, e):
                c, half = w1_part(n)
                if n == 0:
                    act.wait_ge(w1_in, (e + 1) * 16)
                nc.scalar.activation(w1_hi[:, c, half], w1_raw[:, c, half], ACT.Copy, scale=W_SCALE).then_inc(w1_hi_s, 1)

            for b in range(NB):
                act.wait_ge(tr, b + 1)
                nc.scalar.activation(xT_hi[:, :, P * b:P * (b + 1)], ps_h[b % 2][:, :].rearrange("p (c n) -> p c n", c=NC),
                                     ACT.Copy, scale=A_SCALE).then_inc(tr_hi, 1)
            for n in range(NF):
                split_w1(n, 0)
            act.wait_ge(misc_in, 32)
            for b in range(NB):
                act.wait_ge(g_tr, b + 1)
                for c in range(NC):
                    last = nc.scalar.activation(gT[:, c, P * b:P * (b + 1)], ps_y[b][:, P * c:P * (c + 1)], ACT.Identity,
                                                bias=affine[:, 1, c:c + 1], scale=affine[:, 0, c:c + 1])
                last.then_inc(g_out, 1)
            act.wait_ge(chain, 2)
            nc.scalar.activation(prob[:, :, :], prob[:, :, :], ACT.Exp).then_inc(g_exp, 1)
            with act.Fori(0, EXPERTS) as e:
                act.wait_ge(w2_in, (e + 1) * 16)
                for f in range(NF):
                    act.wait_ge(up, e * NF + f + 1)
                    if f >= 2:
                        act.wait_ge(h_lo_s, e * NF + f - 1)
                    nc.scalar.activation(h_f[:, f % 2, :], ps_h[f % 2][:, :], ACT.Gelu, scale=UNSCALE).then_inc(gelu, 1)
                    act.wait_ge(gelu, e * NF + f + 1)
                    nc.scalar.activation(h_hi[:, f, :], h_f[:, f % 2, :], ACT.Copy, scale=A_SCALE).then_inc(h_hi_s, 1)
                    nc.scalar.activation(w2_hi[:, f, :], w2_raw[:, f, :], ACT.Copy, scale=W_SCALE).then_inc(w2_hi_s, 1)
                for n in range(NF):
                    split_w1(n, e + 1)

        @block.tensor
        def _(pe):
            for b in range(NB):
                pe.wait_ge(normed, b + 1)
                if b >= 2:
                    pe.wait_ge(tr_lo, b - 1)
                for c in range(NC):
                    last = nc.tensor.transpose(ps_h[b % 2][:, P * c:P * (c + 1)], hat[:, b, P * c:P * (c + 1)], t.ident[:, :])
                last.then_inc(tr, 1)
            for b in range(NB):
                pe.wait_ge(normed, NB + b + 1)
                for c in range(NC):
                    last = nc.tensor.transpose(ps_y[b][:, P * c:P * (c + 1)], hat2[:, b, P * c:P * (c + 1)], t.ident[:, :])
                last.then_inc(g_tr, 1)
            pe.wait_ge(tr_lo, NB)
            pe.wait_ge(misc_in, 32)
            for b in range(NB):
                pe.wait_ge(g_out, b + 1)
                for c in range(NC):
                    last = nc.tensor.matmul(ps_g[:, b, :], gT[:, c, P * b:P * (b + 1)], gate[:, c, :], start=(c == 0),
                                            stop=(c == NC - 1))
            last.then_inc(g_mm, 1)
            with pe.Fori(0, EXPERTS) as e:
                pe.wait_ge(w1_lo_s, (e + 1) * NF)
                for f in range(NF):
                    if f >= 2:
                        pe.wait_ge(gelu, e * NF + f - 1)
                    col = slice(P * f, P * (f + 1))
                    for c in range(NC):
                        nc.tensor.matmul(ps_h[f % 2][:, :], w1_hi[:, c, col], xT_hi[:, c, :], start=(c == 0), stop=False)
                        nc.tensor.matmul(ps_h[f % 2][:, :], w1_hi[:, c, col], xT_lo[:, c, :], start=False, stop=False)
                        last = nc.tensor.matmul(ps_h[f % 2][:, :], w1_lo[:, c, col], xT_hi[:, c, :], start=False,
                                                stop=(c == NC - 1))
                    last.then_inc(up, 1)
                for f in range(NF):
                    pe.wait_ge(h_lo_s, e * NF + f + 1)
                    pe.wait_ge(w2_lo_s, e * NF + f + 1)
                    for b in range(NB):
                        tok = slice(P * b, P * (b + 1))
                        nc.tensor.matmul(ps_y[b][:, :], h_hi[:, f, tok], w2_hi[:, f, :], start=(f == 0), stop=False)
                        nc.tensor.matmul(ps_y[b][:, :], h_hi[:, f, tok], w2_lo[:, f, :], start=False, stop=False)
                        last = nc.tensor.matmul(ps_y[b][:, :], h_lo[:, f, tok], w2_hi[:, f, :], start=False,
                                                stop=(f == NF - 1))
                last.then_inc(down, 1)


def program(nc, io):
    with ExitStack() as ctx:
        def sb(name, shape, dt=F32):
            return ctx.enter_context(nc.sbuf_tensor(name, shape, dt))

        t, s = Named(), Named()
        t.x = sb("x_sb", [P, NB, D])
        t.ident = sb("ident_sb", [P, P])
        t.half_neg, t.eps, t.inv_scale2 = sb("half_neg", [P, NB]), sb("eps", [P, NB]), sb("inv_scale2", [P, NB])
        s.wo_in = ctx.enter_context(nc.semaphore("wo_in"))
        s.mask_rows_out = ctx.enter_context(nc.semaphore("mask_rows_out"))
        io.mask_rows = nc.dram_tensor("mask_rows", [NB, KEYS], F16, kind="Internal").ap()
        with ExitStack() as cross:
            def cb(name, shape, dt=F32):
                return cross.enter_context(nc.sbuf_tensor(name, shape, dt))

            t.ones32 = cb("ones32", [P, HD])
            t.q_stack = cb("q_stack", [P, HEADS, TOK], F16)
            t.k_stack = [cb(f"k_stack{u}", [P, HPG, KEYS], F16) for u in range(2)]
            t.wk_hi, t.wk_lo = cb("wk_hi", [P, NC, D], F16), cb("wk_lo", [P, NC, D], F16)
            t.wv_hi, t.wv_lo = cb("wv_hi", [P, NC, D], F16), cb("wv_lo", [P, NC, D], F16)
            t.wo = cb("wo_x", [P, NC, D])
            t.kbias, t.vbias = cb("kbias", [P, NG]), cb("vbias", [P, NG])
            prologue(nc, io, t, s)
            cross_attention(nc, io, t, s)
        self_attention(nc, io, t, s)
        mixture(nc, io, t, s)


class Named:
    pass


def kernel(**inputs):
    import concourse.bacc as bacc
    from concourse.bass_utils import run_bass_kernel_spmd

    def plain(name):
        return np.ascontiguousarray(inputs[name])

    def transposed(name):
        return np.ascontiguousarray(np.asarray(inputs[name]).T)

    def column(name):
        return np.ascontiguousarray(np.asarray(inputs[name]).reshape(NC, P).T)

    def rotary():
        inv_freq = (1.0 / 10000.0 ** (np.arange(0, HD, 2, dtype=np.float32) / HD)).astype(np.float32)
        freqs = np.arange(P, dtype=np.float32)[:, None] * inv_freq[None, :]
        angle = np.concatenate([freqs, freqs], axis=-1).astype(np.float64)
        sign = np.concatenate([-np.ones(HD // 2), np.ones(HD // 2)])
        return np.stack([np.cos(angle), np.sin(angle) * sign], axis=1).astype(np.float32)

    def by_partition(w, ahead):
        w = w.reshape(EXPERTS, -1, P, w.shape[-1]).transpose(0, 2, 1, 3)
        return np.ascontiguousarray(np.concatenate([w, w[:ahead]]))

    tiles = np.asarray(inputs["ctx_1024"]).reshape(NB * NKT, P, D)
    arrays = {
        "x": plain("x"),
        "context": np.ascontiguousarray(np.concatenate([tiles, tiles[:2 * RAW]])),
        "mask": plain("mask_BxS2_bf1").view(np.uint8),
        "ident": np.eye(P, dtype=np.float32),
        "rope": rotary(),
        "g1": column("L0_xattn_g1"), "b1": column("L0_xattn_b1"),
        "g2": column("L0_xattn_g2"), "b2": column("L0_xattn_b2"),
        "xbo": plain("L0_xattn_bo"),
        "wqT": transposed("L0_xattn_Wq"), "wkT": transposed("L0_xattn_Wk"),
        "wvT": transposed("L0_xattn_Wv"), "woT": transposed("L0_xattn_Wo"),
        "a_wqT": transposed("L0_attn_Wq"), "a_wkT": transposed("L0_attn_Wk"),
        "a_wvT": transposed("L0_attn_Wv"), "a_woT": transposed("L0_attn_Wo"),
        "a_bq": plain("L0_attn_bq"), "a_bk": plain("L0_attn_bk"),
        "a_bv": plain("L0_attn_bv"), "a_bo": plain("L0_attn_bo"),
        "affine": np.ascontiguousarray(np.stack([column("L0_ffn_ln_gamma"), column("L0_ffn_ln_beta")], axis=1)),
        "gate": np.ascontiguousarray(np.asarray(inputs["L0_ffn_gate_w"]).T.reshape(NC, P, EXPERTS).transpose(1, 0, 2)),
        "w1": by_partition(np.asarray(inputs["L0_ffn_w1"]).transpose(0, 2, 1), 2),
        "w2": by_partition(np.asarray(inputs["L0_ffn_w2"]).transpose(0, 2, 1), 1),
    }
    nc = bacc.Bacc("TRN2", target_bir_lowering=False, num_devices=1)
    io = Named()
    for name, a in arrays.items():
        ap = nc.dram_tensor(f"in_{name}", a.shape, mybir.dt.from_np(a.dtype), kind="ExternalInput").ap()
        io.__dict__[name] = ap
    io.out = nc.dram_tensor("out", (NB, P, D), F32, kind="ExternalOutput").ap()
    program(nc, io)
    r = run_bass_kernel_spmd(nc, [{f"in_{name}": a for name, a in arrays.items()}], core_ids=[0])
    return r.results[0]["out"]
```

```python
from contextlib import ExitStack

import numpy as np
import concourse.bass as bass
from concourse import mybir

F32, F16, U8 = mybir.dt.float32, mybir.dt.float16, mybir.dt.uint8
ALU, ACT, AX = mybir.AluOpType, mybir.ActivationFunctionType, mybir.AxisListType

P = 128
NB = 4
D = 512
NC = D // P
TOK = NB * P
KEYS = 2048
NKT = KEYS // P
HEADS, HD = 16, 32
HPG = P // HD
NG = HEADS // HPG
NPAIR = NKT // 2
EPS = 1e-5
A_SCALE, W_SCALE = 16.0, 64.0
UNSCALE = 1.0 / (A_SCALE * W_SCALE)
SM_SCALE = float(1.0 / np.sqrt(HD))
MASKED = -60000.0
SHIFT_ROW, MASK_ROW = 96, 97
ROWS = 98
EXPERTS, FF = 8, 1024
NF = FF // P


def chunked(ap):
    return ap.rearrange("(c p) n -> p c n", p=P)


def prologue(nc, io, t, s):
    with ExitStack() as ctx:
        def sb(name, shape, dt=F32):
            return ctx.enter_context(nc.sbuf_tensor(name, shape, dt))

        def sem(name):
            return ctx.enter_context(nc.semaphore(name))

        w_raw = [sb(f"w_raw{i}", [P, NC, D]) for i in range(3)]
        w_fold = sb("w_fold", [P, NC, D])
        wq_hi, wq_lo = sb("wq_hi", [P, NC, D], F16), sb("wq_lo", [P, NC, D], F16)
        gains = sb("gains", [P, 3, NC])
        offsets = sb("offsets", [P, 2, NC])
        bo_bc = sb("bo_bc", [P, D])
        hat = sb("hat", [P, NB, D])
        hat2 = sb("hat2", [P, NB, D])
        xT_hi, xT_lo = sb("xT_hi", [P, NC, TOK], F16), sb("xT_lo", [P, NC, TOK], F16)
        q_f = sb("q_f", [P, NG, TOK])
        q_hi, q_lo = sb("q_hi", [P, NG, TOK], F16), sb("q_lo", [P, NG, TOK], F16)
        qbias = sb("qbias", [P, NG])
        stats = sb("stats", [P, NB, 6])
        mv = sb("mv", [P, 2, NB, 2])
        rstd = sb("rstd", [P, 2, NB])
        mask_u8 = sb("mask_u8", [NB, KEYS], U8)
        mask_neg = sb("mask_neg", [NB, KEYS], F16)
        ps_t = [ctx.enter_context(nc.psum_tensor(f"pro_t{i}", [P, D], F32)) for i in range(2)]
        ps_q = [ctx.enter_context(nc.psum_tensor(f"pro_q{i}", [P, D], F32)) for i in range(2)]
        ps_b = ctx.enter_context(nc.psum_tensor("pro_b", [P, 3, NG], F32))

        x_in, w_in, vec_in = sem("x_in"), [sem(f"w_in{i}") for i in range(3)], sem("vec_in")
        const = sem("const")
        pow_done = sem("pow_done")
        stat_done = sem("stat_done")
        dve = sem("dve_pro")
        folded = sem("folded")
        w_hi = sem("w_hi")
        w_lo = sem("w_lo")
        normed = sem("normed")
        tr, tr_hi, tr_lo = sem("tr"), sem("tr_hi"), sem("tr_lo")
        bias_mm, bias_out = sem("bias_mm"), sem("bias_out")
        q_mm, q_out, q_hi_s, q_lo_s = sem("q_mm"), sem("q_out"), sem("q_hi_s"), sem("q_lo_s")
        mask_in, mask_done, placed = sem("mask_in"), sem("mask_done"), sem("placed")
        ones_rows = sem("ones_rows")

        targets = [(wq_hi, wq_lo), (t.wk_hi, t.wk_lo), (t.wv_hi, t.wv_lo)]
        block = ctx.enter_context(nc.Block())

        @block.sync
        def _(sp):
            sp.dma_start(t.x[:, :, :], io.x.rearrange("b t c -> t b c")).then_inc(x_in, 16)
            sp.dma_start(t.ident[:, :], io.ident).then_inc(x_in, 16)
            sp.dma_start(w_raw[0][:, :, :], chunked(io.wqT)).then_inc(w_in[0], 16)
            sp.dma_start(gains[:, 0, :], io.g1).then_inc(vec_in, 16)
            sp.dma_start(gains[:, 1, :], io.g2).then_inc(vec_in, 16)
            sp.dma_start(gains[:, 2, :], io.g2).then_inc(vec_in, 16)
            sp.dma_start(offsets[:, 0, :], io.b1).then_inc(vec_in, 16)
            sp.dma_start(offsets[:, 1, :], io.b2).then_inc(vec_in, 16)
            sp.dma_start(bo_bc[:, :], io.xbo.partition_broadcast(P)).then_inc(vec_in, 16)
            for i, w in ((1, io.wkT), (2, io.wvT)):
                sp.dma_start(w_raw[i][:, :, :], chunked(w)).then_inc(w_in[i], 16)
            sp.dma_start(mask_u8[:, :], io.mask).then_inc(mask_in, 16)
            sp.dma_start(t.wo[:, :, :], chunked(io.woT)).then_inc(s.wo_in, 16)
            sp.wait_ge(mask_done, 1)
            sp.dma_start(io.mask_rows, mask_neg[:, :]).then_inc(s.mask_rows_out, 16)
            for part_sem, k, part in ((q_hi_s, 0, q_hi), (q_hi_s, 2, q_hi), (q_lo_s, 1, q_lo)):
                sp.wait_ge(part_sem, NG)
                for j in range(HPG):
                    heads = t.q_stack[HD * k:HD * (k + 1), :, :].rearrange("p (g j) n -> p j g n", j=HPG)
                    sp.dma_start(heads[:, j, :, :], part[HD * j:HD * (j + 1), :, :]).then_inc(placed, 16)
            sp.wait_ge(placed, 16 * 3 * HPG)
            sp.wait_ge(s.mask_rows_out, 16)

        @block.gpsimd
        def _(pool):
            small = [(t.half_neg[:, :], -0.5), (t.eps[:, :], EPS), (t.inv_scale2[:, :], A_SCALE ** -2)]
            whole = small + [(t.ones32[:, :], 1.0), (t.q_stack[SHIFT_ROW:ROWS, :, :], 1.0),
                             (t.q_stack[SHIFT_ROW:SHIFT_ROW + 1, :, :], 0.0)]
            whole += [(t.k_stack[u][SHIFT_ROW:ROWS, :, :], 1.0) for u in range(2)]
            for n, (what, value) in enumerate(small):
                nc.gpsimd.memset(what, value).then_inc(const, 1)
                pool.wait_ge(const, n + 1)
            for k in range(2):
                pool.wait_ge(dve, k + 1)
                nc.gpsimd.tensor_scalar(rstd[:, k, :], mv[:, k, :, 1], EPS, 1.0 if k == 0 else A_SCALE ** -2,
                                        ALU.add, ALU.mult).then_inc(pow_done, 1)
                pool.wait_ge(pow_done, 2 * k + 1)
                nc.gpsimd.tensor_tensor(rstd[:, k, :], rstd[:, k, :], t.half_neg[:, 0:NB],
                                        ALU.pow).then_inc(pow_done, 1)
                pool.wait_ge(pow_done, 2 * k + 2)
            for n in range(len(small), len(whole)):
                nc.gpsimd.memset(*whole[n]).then_inc(const, 1)
                pool.wait_ge(const, n + 1)

        @block.vector
        def _(v):
            n_stat = 0
            v.wait_ge(x_in, 32)
            for k, src in enumerate((t.x, hat)):
                for b in range(NB):
                    nc.vector.bn_stats(stats[:, b, :], src[:, b, :]).then_inc(stat_done, 1)
                n_stat += NB
                v.wait_ge(stat_done, n_stat)
                for b in range(NB):
                    last = nc.vector.bn_aggr(mv[:, k, b, :], stats[:, b, :])
                last.then_inc(dve, 1)
                v.wait_ge(dve, k + 1)
                v.wait_ge(pow_done, 2 * k + 2)
                for b in range(NB):
                    ins = nc.vector.tensor_scalar((hat, hat2)[k][:, b, :], src[:, b, :], mv[:, k, b, 0:1],
                                                  rstd[:, k, b:b + 1], ALU.subtract, ALU.mult)
                    ins.then_inc(normed, 1)
                v.wait_ge(normed, NB * (k + 1))
            v.wait_ge(vec_in, 96)
            for b in range(NB):
                nc.vector.tensor_tensor(t.x[:, b, :], t.x[:, b, :], bo_bc[:, :], ALU.add)
            for i in range(3):
                v.wait_ge(w_in[i], 16)
                if i:
                    v.wait_ge(w_hi, i)
                    v.wait_ge(w_lo, i)
                for c in range(NC):
                    ins = nc.vector.tensor_scalar(w_fold[:, c, :], w_raw[i][:, c, :], gains[:, i, c:c + 1],
                                                  W_SCALE, ALU.mult, ALU.mult)
                ins.then_inc(folded, 1)
                v.wait_ge(folded, i + 1)
                v.wait_ge(w_hi, i + 1)
                nc.vector.tensor_tensor(targets[i][1][:, :, :], w_fold[:, :, :], targets[i][0][:, :, :],
                                        ALU.subtract).then_inc(w_lo, 1)
                if i == 0:
                    for b in range(NB):
                        v.wait_ge(tr_hi, b + 1)
                        nc.vector.tensor_tensor(xT_lo[:, :, P * b:P * (b + 1)],
                                                ps_t[b % 2][:, :].rearrange("p (c n) -> p c n", c=NC),
                                                xT_hi[:, :, P * b:P * (b + 1)], ALU.subtract).then_inc(tr_lo, 1)
            v.wait_ge(mask_in, 16)
            nc.vector.tensor_scalar(mask_neg[:, :], mask_u8[:, :], 1.0, -MASKED,
                                    ALU.subtract, ALU.mult).then_inc(mask_done, 1)
            for g in range(NG):
                v.wait_ge(q_hi_s, g + 1)
                nc.vector.tensor_tensor(q_lo[:, g, :], q_f[:, g, :], q_hi[:, g, :],
                                        ALU.subtract).then_inc(q_lo_s, 1)

        @block.scalar
        def _(act):
            act.wait_ge(folded, 1)
            nc.scalar.activation(wq_hi[:, :, :], w_fold[:, :, :], ACT.Copy).then_inc(w_hi, 1)
            for b in range(NB):
                act.wait_ge(tr, b + 1)
                nc.scalar.activation(xT_hi[:, :, P * b:P * (b + 1)],
                                     ps_t[b % 2][:, :].rearrange("p (c n) -> p c n", c=NC),
                                     ACT.Copy).then_inc(tr_hi, 1)
            for i in (1, 2):
                act.wait_ge(folded, i + 1)
                nc.scalar.activation(targets[i][0][:, :, :], w_fold[:, :, :], ACT.Copy).then_inc(w_hi, 1)
            act.wait_ge(bias_mm, 1)
            for dst, i in ((qbias, 0), (t.kbias, 1), (t.vbias, 2)):
                nc.scalar.activation(dst[:, :], ps_b[:, i, :], ACT.Copy).then_inc(bias_out, 1)
            act.wait_ge(bias_out, 3)
            for g in range(NG):
                act.wait_ge(q_mm, g + 1)
                nc.scalar.activation(q_f[:, g, :], ps_q[g % 2][:, :], ACT.Identity, bias=qbias[:, g:g + 1],
                                     scale=UNSCALE).then_inc(q_out, 1)
                act.wait_ge(q_out, g + 1)
                nc.scalar.activation(q_hi[:, g, :], q_f[:, g, :], ACT.Copy).then_inc(q_hi_s, 1)

        @block.tensor
        def _(pe):
            for b in range(NB):
                pe.wait_ge(normed, NB + b + 1)
                if b >= 2:
                    pe.wait_ge(tr_lo, b - 1)
                for c in range(NC):
                    last = nc.tensor.transpose(ps_t[b % 2][:, P * c:P * (c + 1)], hat2[:, b, P * c:P * (c + 1)],
                                               t.ident[:, :])
                last.then_inc(tr, 1)
            pe.wait_ge(vec_in, 96)
            for i in range(3):
                pe.wait_ge(w_in[i], 16)
                for g in range(NG):
                    for c in range(NC):
                        last = nc.tensor.matmul(ps_b[:, i, g:g + 1], w_raw[i][:, c, P * g:P * (g + 1)],
                                                offsets[:, min(i, 1), c:c + 1], start=(c == 0), stop=(c == NC - 1))
            last.then_inc(bias_mm, 1)
            pe.wait_ge(w_lo, 1)
            pe.wait_ge(tr_lo, NB)
            for g in range(NG):
                if g >= 2:
                    pe.wait_ge(q_out, g - 1)
                col = slice(P * g, P * (g + 1))
                for c in range(NC):
                    nc.tensor.matmul(ps_q[g % 2][:, :], wq_hi[:, c, col], xT_hi[:, c, :], start=(c == 0), stop=False)
                    nc.tensor.matmul(ps_q[g % 2][:, :], wq_hi[:, c, col], xT_lo[:, c, :], start=False, stop=False)
                    last = nc.tensor.matmul(ps_q[g % 2][:, :], wq_lo[:, c, col], xT_hi[:, c, :], start=False,
                                            stop=(c == NC - 1))
                last.then_inc(q_mm, 1)


KB = 512
NKB = KEYS // KB
RAW = 4
PT = 4


def attention_steps():
    def scores(g, p):
        return [("s", g, p, 0), ("s", g, p, 1)]

    steps, t = [], RAW
    for kt in range(2, 10):
        while t < min(NKT, (7 * (kt - 2)) // 4 + RAW + 2):
            steps += [("ln", t // 2), ("t", t), ("t", t + 1)]
            t += 2
        steps += [("v", kt, c) for c in range(NC)]
    assert t == NKT
    steps += [("k", g, kb) for g in (0, 1) for kb in range(NKB)]
    p1 = [[("p1", g, j, kb) for h in range(2) for j in range(HPG) for kb in (2 * h, 2 * h + 1)] for g in range(NG)]
    for kt in range(10, 14):
        for c in range(NC):
            steps += [("v", kt, c), p1[0].pop(0)]
    steps += [("v", 14, c) for c in range(NC)] + [("mt", 0)] + scores(0, 0) + scores(0, 1)
    steps += [("v", 15, c) for c in range(NC)]
    p1_at = [{3: 3, 4: 3, 5: 3, 6: 3, 7: 4}] * 2 + [{3: 4, 4: 4, 5: 4, 6: 4}] + [{}]
    for g in range(NG):
        for p in range(NPAIR):
            work = [("av", g, p, 0), ("av", g, p, 1)]
            if p + 2 < NPAIR:
                work += scores(g, p + 2)
            tiles = [p1[g + 1].pop(0) for _ in range(p1_at[g].get(p, 0))]
            for n in range(4):
                steps += work[n:n + 1] + tiles[n:n + 1]
            if p == 1 and g:
                steps.append(("den", g - 1))
        steps.append(("sums", g))
        if g < 2:
            steps += [("k", g + 2, 0), ("mt", g + 1), ("k", g + 2, 1), ("k", g + 2, 2)]
            steps += scores(g + 1, 0) + scores(g + 1, 1) + [("k", g + 2, 3)]
        if g == 2:
            steps += [("mt", 3)] + scores(3, 0) + scores(3, 1) + [("next ln", 0), ("next ln", 1)]
    return steps + [("next t", kt) for kt in range(RAW)] + [("next v", 0, c) for c in range(NC)] + \
        [("den", NG - 1)] + [("next v", 1, c) for c in range(NC)] + [("op",)]


AHEAD_LN = (0, 1)
AHEAD_T = range(RAW)
AHEAD_V = (0, 1)


def of_batch(step, b):
    return ((step[0][5:], *step[1:]), b + 1) if step[0].startswith("next ") else (step, b)


def cross_attention(nc, io, t, s):
    steps = attention_steps()
    ring = [("v", kt) for kt in AHEAD_V]
    ring += [step[:2] if step[0] == "v" else step for step in steps
             if step[0] in ("k", "mt") or (step[0] == "v" and step[2] == 0) or (step[0] == "p1" and step[1] > 0)]
    assert len(ring) % 2 == 0
    PER_BATCH = {"v": NKT, "k": NG * NKB, "p1": NG * HPG * NKB, "mt": NG}

    def ring_place(step):
        return ring.index(step[:2] if step[0] == "v" else step)

    KIN = 16 * 3 * HPG

    with ExitStack() as ctx:
        def sb(name, shape, dt=F32):
            return ctx.enter_context(nc.sbuf_tensor(name, shape, dt))

        def sem(name):
            return ctx.enter_context(nc.semaphore(name))

        raw = sb("raw", [P, RAW, D])
        xn = sb("xn", [P, RAW, D])
        stats = sb("c_stats", [P, 4, 6])
        mv = sb("c_mv", [P, 4, 2])
        carrier = sb("carrier", [P, 1])
        rstd = sb("c_rstd", [P, 4])
        cT_hi, cT_lo = sb("cT_hi", [P, NC, KEYS], F16), sb("cT_lo", [P, NC, KEYS], F16)
        vals = sb("vals", [P, NKT, D])
        k_f = sb("k_f", [P, 2, KB])
        k_hi = [sb(f"k_hi{h}", [P, 2 * KB], F16) for h in range(2)]
        k_lo = [sb(f"k_lo{h}", [P, 2 * KB], F16) for h in range(2)]
        mpart = sb("mpart", [P, HPG, NKB])
        mgroup = sb("mgroup", [P, 2, HPG])
        pT = sb("pT", [P, PT, 2 * KB])
        acc_pool, acc_dve, acc = sb("acc_pool", [P, 2 * KB]), sb("acc_dve", [P, 2 * KB]), sb("acc", [P, KB])
        rden = sb("rden", [P, P])
        oT = sb("oT", [P, NG, P])
        ps_s = [ctx.enter_context(nc.psum_tensor(f"ps_s{i}", [P, 2 * KB], F32)) for i in range(2)]
        ps_r = [ctx.enter_context(nc.psum_tensor(f"ps_r{i}", [P, KB], F32)) for i in range(2)]
        ps_o = [ctx.enter_context(nc.psum_tensor(f"ps_o{i}", [P, KB], F32)) for i in range(2)]

        raw_in = [sem(f"raw_in{i}") for i in range(RAW)]
        stat_dve, var_dve, normed = sem("c_stat"), sem("c_var"), sem("c_normed")
        pool_pow = sem("c_pow")
        tr, tr_hi, tr_lo = sem("c_tr"), sem("c_tr_hi"), sem("c_tr_lo")
        v_mm, v_out = sem("v_mm"), sem("v_out")
        k_mm, k_f_out, k_hi_out, k_lo_out = sem("k_mm"), sem("k_f_out"), sem("k_hi_out"), sem("k_lo_out")
        k_in = [[sem(f"k_in{u}{h}") for h in range(2)] for u in range(2)]
        mask_in = sem("c_mask_in")
        p1_mm, p1_max, m_max, mt_mm, m_row = (sem("p1_mm"), sem("p1_max"), sem("m_max"), sem("mt_mm"),
                                                        sem("m_row"))
        s_mm, exp_done, av_mm = sem("s_mm"), sem("exp_done"), sem("av_mm")
        pool_add, dve_first, dve_second, sums_done = sem("pool_add"), sem("dve_first"), sem("dve_second"), sem("sums_done")
        den_mm, rden_done, norm_out, fin = sem("den_mm"), sem("rden_done"), sem("norm_out"), sem("fin")
        op_mm, x_done = sem("op_mm"), sem("x_done")

        def p1_bank(step, n):
            if step[1] == 0:
                return ps_s[n % 2][:, KB * (n // 2 % 2):KB * (n // 2 % 2 + 1)]
            return ps_r[ring_place(step) % 2][:, :]

        block = ctx.enter_context(nc.Block())

        @block.sync
        def _(sp):
            def load(b, kt):
                sp.dma_start(raw[:, kt % RAW, :],
                             io.context[bass.ds(b * NKT + kt, 1), :, :].rearrange("o p c -> (o p) c")
                             ).then_inc(raw_in[kt % RAW], 16)

            def reload(step, b):
                for kt in (2 * step[1], 2 * step[1] + 1):
                    sp.wait_ge(normed, b * NKT + kt + 1)
                    load(b, kt + RAW)

            for kt in range(RAW):
                load(0, kt)
            for n in AHEAD_LN:
                reload(("ln", n), 0)
            with sp.Fori(0, NB) as b:
                sp.wait_ge(tr, b * NKT + 1)
                for u in range(2):
                    for j in range(HPG):
                        sp.dma_start(t.k_stack[u][MASK_ROW:MASK_ROW + 1, j, :],
                                     io.mask_rows[bass.ds(b, 1), :]).then_inc(mask_in, 16)
                for step in steps:
                    step, bb = of_batch(step, b)
                    if step[0] == "ln":
                        reload(step, bb)
                    if step[0] == "k" and step[2] % 2 == 1:
                        g, h = step[1], step[2] // 2
                        u = g % 2
                        sp.wait_ge(k_lo_out, b * NG * NKB + NKB * g + 2 * h + 2)
                        for j in range(HPG):
                            for k, part in enumerate((k_hi[h], k_hi[h], k_lo[h])):
                                sp.dma_start(t.k_stack[u][HD * k:HD * (k + 1), j, 2 * KB * h:2 * KB * (h + 1)],
                                             part[HD * j:HD * (j + 1), :]).then_inc(k_in[u][h], 16)
            for i in range(RAW):
                sp.wait_ge(raw_in[i], (NB * (NKT // RAW) + 2) * 16)

        @block.gpsimd
        def _(pool):
            def deviations(n, b):
                two = slice(2 * (n % 2), 2 * (n % 2) + 2)
                pool.wait_ge(var_dve, b * (NKT // 2) + n + 1)
                for k, (x, y, op) in enumerate(((mv[:, two, 1], t.eps[:, 0:2], ALU.add),
                                                (rstd[:, two], t.inv_scale2[:, 0:2], ALU.mult),
                                                (rstd[:, two], t.half_neg[:, 0:2], ALU.pow))):
                    nc.gpsimd.tensor_tensor(rstd[:, two], x, y, op).then_inc(pool_pow, 1)
                    pool.wait_ge(pool_pow, (b * (NKT // 2) + n) * 3 + k + 1)

            deviations(0, 0)
            deviations(1, 0)
            with pool.Fori(0, NB) as b:
                n_add = 0
                for step in steps:
                    step, bb = of_batch(step, b)
                    if step[0] == "ln":
                        deviations(step[1], bb)
                    if step[0] == "sums":
                        g = step[1]
                        if g:
                            pool.wait_ge(dve_second, b * NG + g)
                        for p in range(1, 6):
                            pool.wait_ge(exp_done, b * NG * NPAIR + NPAIR * g + p + 1)
                            nc.gpsimd.tensor_tensor(acc_pool[:, :], pT[:, 0, :] if p == 1 else acc_pool[:, :],
                                                    pT[:, p % PT, :], ALU.add).then_inc(pool_add, 1)
                            n_add += 1
                            pool.wait_ge(pool_add, b * 5 * NG + n_add)

        @block.vector
        def _(v):
            def statistics(kt, b):
                v.wait_ge(raw_in[kt % RAW], (b * (NKT // RAW) + kt // RAW + 1) * 16)
                nc.vector.bn_stats(stats[:, kt % 4, :], raw[:, kt % RAW, :]).then_inc(stat_dve, 1)

            def variances(n, b):
                v.wait_ge(stat_dve, b * NKT + 2 * n + 2)
                nc.vector.memset(carrier[:, :], 0.0)
                for kt in (2 * n, 2 * n + 1):
                    last = nc.vector.bn_aggr(mv[:, kt % 4, :], stats[:, kt % 4, :])
                last.then_inc(var_dve, 1)

            def normalise(n, b):
                v.wait_ge(pool_pow, (b * (NKT // 2) + n + 1) * 3)
                for kt in (2 * n, 2 * n + 1):
                    if kt >= RAW:
                        v.wait_ge(tr, b * NKT + kt - RAW + 1)
                    nc.vector.tensor_scalar(xn[:, kt % RAW, :], raw[:, kt % RAW, :], mv[:, kt % 4, 0:1],
                                            rstd[:, kt % 4:kt % 4 + 1], ALU.subtract,
                                            ALU.mult).then_inc(normed, 1)

            def low_half(kt, b):
                if 2 <= kt < NKT - 2:
                    statistics(kt + 2, b)
                    if kt % 2:
                        variances(kt // 2 + 1, b)
                v.wait_ge(tr_hi, b * NKT + kt + 1)
                nc.vector.tensor_tensor(cT_lo[:, :, P * kt:P * (kt + 1)],
                                        ps_s[kt % 2][:, 0:KB].rearrange("p (c n) -> p c n", c=NC),
                                        cT_hi[:, :, P * kt:P * (kt + 1)], ALU.subtract).then_inc(tr_lo, 1)

            def first_tiles(b):
                for n in AHEAD_LN:
                    statistics(2 * n, b)
                    statistics(2 * n + 1, b)
                    variances(n, b)
                for n in AHEAD_LN:
                    normalise(n, b)

            first_tiles(0)
            for kt in AHEAD_T:
                low_half(kt, 0)
            with v.Fori(0, NB) as b:
                n_p1 = 0
                for step in steps:
                    step, bb = of_batch(step, b)
                    kind = step[0]
                    if kind == "ln":
                        if bb is b:
                            normalise(step[1], b)
                        elif step[1] == AHEAD_LN[-1]:
                            first_tiles(bb)
                    elif kind == "t":
                        low_half(step[1], bb)
                    elif kind == "k":
                        g, kb = step[1:]
                        n = NKB * g + kb
                        h, half = kb // 2, slice(KB * (kb % 2), KB * (kb % 2 + 1))
                        v.wait_ge(k_hi_out, b * NG * NKB + n + 1)
                        nc.vector.tensor_tensor(k_lo[h][:, half], k_f[:, kb % 2, :], k_hi[h][:, half],
                                                ALU.subtract).then_inc(k_lo_out, 1)
                    elif kind == "p1":
                        g, j, kb = step[1:]
                        n_p1 += 1
                        n = n_p1
                        v.wait_ge(p1_mm, b * PER_BATCH["p1"] + n)
                        nc.vector.tensor_reduce(mpart[:, j, kb:kb + 1], p1_bank(step, n - 1), AX.X,
                                                ALU.max).then_inc(p1_max, 1)
                        if (j, kb) == (HPG - 1, NKB - 1):
                            v.wait_ge(p1_max, b * PER_BATCH["p1"] + n)
                            nc.vector.tensor_reduce(mgroup[:, g % 2, :], mpart[:, :, :], AX.X,
                                                    ALU.max).then_inc(m_max, 1)
                    elif kind == "sums":
                        g = step[1]
                        v.wait_ge(exp_done, b * NG * NPAIR + NPAIR * (g + 1))
                        nc.vector.tensor_tensor(acc_dve[:, :], pT[:, 6 % PT, :], pT[:, 7 % PT, :],
                                                ALU.add).then_inc(dve_first, 1)
                        v.wait_ge(dve_first, b * NG + g + 1)
                        v.wait_ge(pool_add, b * 5 * NG + 5 * (g + 1))
                        nc.vector.tensor_tensor(acc_dve[:, :], acc_dve[:, :], acc_pool[:, :],
                                                ALU.add).then_inc(dve_second, 1)
                        v.wait_ge(dve_second, b * NG + g + 1)
                        if g:
                            v.wait_ge(den_mm, b * NG + g)
                        nc.vector.tensor_tensor(acc[:, :], acc_dve[:, 0:KB], acc_dve[:, KB:2 * KB],
                                                ALU.add).then_inc(sums_done, 1)
                    elif kind == "den":
                        g = step[1]
                        v.wait_ge(den_mm, b * NG + g + 1)
                        nc.vector.reciprocal(rden[:, :], ps_o[g % 2][:, P:2 * P]).then_inc(rden_done, 1)
                        v.wait_ge(rden_done, b * NG + g + 1)
                        nc.vector.tensor_tensor(oT[:, g, :], ps_o[g % 2][:, 0:P], rden[:, :],
                                                ALU.mult).then_inc(norm_out, 1)
                        v.wait_ge(norm_out, b * NG + g + 1)
                        nc.vector.tensor_scalar(oT[:, g, :], oT[:, g, :], t.vbias[:, g:g + 1], None,
                                                ALU.add).then_inc(fin, 1)
                    elif kind == "op":
                        v.wait_ge(op_mm, b + 1)
                        here = t.x[:, bass.ds(b, 1), :].rearrange("p o c -> p (o c)")
                        nc.vector.tensor_tensor(here, ps_s[0][:, KB:2 * KB], here, ALU.add).then_inc(x_done, 1)

        @block.scalar
        def _(act):
            def high_half(kt, b):
                act.wait_ge(tr, b * NKT + kt + 1)
                nc.scalar.activation(cT_hi[:, :, P * kt:P * (kt + 1)],
                                     ps_s[kt % 2][:, 0:KB].rearrange("p (c n) -> p c n", c=NC),
                                     ACT.Copy).then_inc(tr_hi, 1)

            def values_out(kt, b):
                act.wait_ge(v_mm, b * NKT + kt + 1)
                nc.scalar.activation(vals[:, kt, :], ps_r[ring_place(("v", kt)) % 2][:, :], ACT.Copy,
                                     scale=UNSCALE).then_inc(v_out, 1)

            for kt in AHEAD_T:
                high_half(kt, 0)
            for kt in AHEAD_V:
                values_out(kt, 0)
            with act.Fori(0, NB) as b:
                def exp(g, p):
                    n = NPAIR * g + p
                    act.wait_ge(s_mm, b * NG * NPAIR + n + 1)
                    if n >= PT:
                        act.wait_ge(av_mm, b * NG * NPAIR + n - PT + 1)
                        q = (n - PT) % NPAIR
                        before = (n - PT) // NPAIR
                        if q < 6:
                            act.wait_ge(pool_add, b * 5 * NG + 5 * before + max(q, 1))
                        else:
                            act.wait_ge(dve_first, b * NG + before + 1)
                    nc.scalar.activation(pT[:, p % PT, :], ps_s[p % 2][:, :], ACT.Exp,
                                         scale=SM_SCALE).then_inc(exp_done, 1)

                for step in steps:
                    step, bb = of_batch(step, b)
                    kind = step[0]
                    if kind == "t":
                        high_half(step[1], bb)
                    elif kind == "v" and step[2] == NC - 1:
                        values_out(step[1], bb)
                    elif kind == "k":
                        g, kb = step[1:]
                        n = NKB * g + kb
                        h, half = kb // 2, slice(KB * (kb % 2), KB * (kb % 2 + 1))
                        act.wait_ge(k_mm, b * NG * NKB + n + 1)
                        if n >= 2:
                            act.wait_ge(k_lo_out, b * NG * NKB + n - 1)
                        nc.scalar.activation(k_f[:, kb % 2, :], ps_r[ring_place(step) % 2][:, :], ACT.Identity,
                                             bias=t.kbias[:, g:g + 1], scale=UNSCALE).then_inc(k_f_out, 1)
                        act.wait_ge(k_f_out, b * NG * NKB + n + 1)
                        if g:
                            act.wait_ge(k_in[(g - 1) % 2][h], (b * 2 + (g - 1) // 2 + 1) * KIN)
                        nc.scalar.activation(k_hi[h][:, half], k_f[:, kb % 2, :], ACT.Copy).then_inc(k_hi_out, 1)
                    elif kind == "mt":
                        g = step[1]
                        act.wait_ge(mt_mm, b * NG + g + 1)
                        nc.scalar.activation(
                            t.q_stack[SHIFT_ROW:SHIFT_ROW + 1, HPG * g:HPG * (g + 1), bass.ds(b * P, P)],
                            ps_r[ring_place(step) % 2][SHIFT_ROW:SHIFT_ROW + 1, :].rearrange("o (j n) -> o j n", j=HPG),
                            ACT.Copy, scale=-1.0).then_inc(m_row, 1)
                    elif kind == "s" and step[3] == 1:
                        exp(*step[1:3])

        @block.tensor
        def _(pe):
            def transposes(kt, b):
                pe.wait_ge(normed, b * NKT + kt + 1)
                if kt >= 2:
                    pe.wait_ge(tr_lo, b * NKT + kt - 1)
                for c in range(NC):
                    last = nc.tensor.transpose(ps_s[kt % 2][:, P * c:P * (c + 1)],
                                               xn[:, kt % RAW, P * c:P * (c + 1)], t.ident[:, :])
                last.then_inc(tr, 1)

            released = {"v": v_out, "k": k_f_out, "p1": p1_max, "mt": m_row}

            def ring_bank(step, b):
                n = ring_place(step)
                kind = ring[n - 2][0]
                if n >= 2:
                    before = sum(r[0] == kind for r in ring[:n - 1]) + (HPG * NKB if kind == "p1" else 0)
                    pe.wait_ge(released[kind], b * PER_BATCH[kind] + before)
                return ps_r[n % 2]

            def values_quarter(kt, c, b):
                if c == 0:
                    ring_bank(("v", kt), b)
                    pe.wait_ge(tr_lo, b * NKT + kt + 1)
                bank, keys = ps_r[ring_place(("v", kt)) % 2], slice(P * kt, P * (kt + 1))
                nc.tensor.matmul(bank[:, :], cT_hi[:, c, keys], t.wv_hi[:, c, :], start=(c == 0), stop=False)
                nc.tensor.matmul(bank[:, :], cT_hi[:, c, keys], t.wv_lo[:, c, :], start=False, stop=False)
                last = nc.tensor.matmul(bank[:, :], cT_lo[:, c, keys], t.wv_hi[:, c, :], start=False,
                                        stop=(c == NC - 1))
                if c == NC - 1:
                    last.then_inc(v_mm, 1)

            for kt in AHEAD_T:
                transposes(kt, 0)
            for kt in AHEAD_V:
                for c in range(NC):
                    values_quarter(kt, c, 0)
            with pe.Fori(0, NB) as b:
                n_p1 = 0
                for step in steps:
                    step, bb = of_batch(step, b)
                    kind = step[0]
                    if kind == "t":
                        transposes(step[1], bb)
                    elif kind == "v":
                        kt, c = step[1:]
                        values_quarter(kt, c, bb)
                    elif kind == "k":
                        g, kb = step[1:]
                        bank = ring_bank(step, b)
                        if kb == 0:
                            pe.wait_ge(tr_lo, b * NKT + NKT)
                        col, keys = slice(P * g, P * (g + 1)), slice(KB * kb, KB * (kb + 1))
                        for c in range(NC):
                            nc.tensor.matmul(bank[:, :], t.wk_hi[:, c, col], cT_hi[:, c, keys], start=(c == 0), stop=False)
                            nc.tensor.matmul(bank[:, :], t.wk_hi[:, c, col], cT_lo[:, c, keys], start=False, stop=False)
                            last = nc.tensor.matmul(bank[:, :], t.wk_lo[:, c, col], cT_hi[:, c, keys], start=False,
                                                    stop=(c == NC - 1))
                        last.then_inc(k_mm, 1)
                    elif kind == "p1":
                        g, j, kb = step[1:]
                        if g:
                            ring_bank(step, b)
                        elif n_p1 >= 4:
                            pe.wait_ge(p1_max, b * PER_BATCH["p1"] + n_p1 - 3)
                        bank = p1_bank(step, n_p1)
                        n_p1 += 1
                        if (g, j, kb) == (0, 0, 0):
                            pe.wait_ge(mask_in, (b + 1) * 16 * 2 * HPG)
                        if j == 0 and kb % 2 == 0:
                            pe.wait_ge(k_in[g % 2][kb // 2], (b * 2 + g // 2 + 1) * KIN)
                        nc.tensor.matmul(bank, t.q_stack[0:ROWS, HPG * g + j, bass.ds(b * P, P)],
                                         t.k_stack[g % 2][0:ROWS, j, KB * kb:KB * (kb + 1)],
                                         start=True, stop=True).then_inc(p1_mm, 1)
                    elif kind == "mt":
                        g = step[1]
                        bank = ring_bank(step, b)
                        pe.wait_ge(m_max, b * NG + g + 1)
                        for j in range(HPG):
                            last = nc.tensor.matmul(bank[SHIFT_ROW:SHIFT_ROW + 1, P * j:P * (j + 1)],
                                                    mgroup[:, g % 2, j:j + 1], t.ident[:, :], start=True, stop=True)
                        last.then_inc(mt_mm, 1)
                    elif kind == "s":
                        g, p, i = step[1:]
                        n = NPAIR * g + p
                        if n >= 2 and i == 0:
                            pe.wait_ge(exp_done, b * NG * NPAIR + n - 1)
                        if p == 0 and i == 0:
                            pe.wait_ge(m_row, b * NG + g + 1)
                        for j in range(HPG):
                            at = KB * i + P * j
                            kt = 2 * p + i
                            last = nc.tensor.matmul(ps_s[p % 2][:, at:at + P],
                                                    t.k_stack[g % 2][0:ROWS, j, P * kt:P * (kt + 1)],
                                                    t.q_stack[0:ROWS, HPG * g + j, bass.ds(b * P, P)],
                                                    start=True, stop=True)
                        if i == 1:
                            last.then_inc(s_mm, 1)
                    elif kind == "av":
                        g, p, i = step[1:]
                        if i == 0:
                            pe.wait_ge(exp_done, b * NG * NPAIR + NPAIR * g + p + 1)
                            if g >= 2 and p == 0:
                                pe.wait_ge(fin, b * NG + g - 1)
                        for j in range(HPG):
                            at = KB * i + P * j
                            head = HD * (HPG * g + j)
                            last = nc.tensor.matmul(ps_o[g % 2][HD * j:HD * (j + 1), 0:P],
                                                    vals[:, 2 * p + i, head:head + HD],
                                                    pT[:, p % PT, at:at + P], start=(p == 0 and i == 0),
                                                    stop=(p == NPAIR - 1 and i == 1))
                        if i == 1:
                            last.then_inc(av_mm, 1)
                    elif kind == "den":
                        g = step[1]
                        pe.wait_ge(sums_done, b * NG + g + 1)
                        for j in range(HPG):
                            last = nc.tensor.matmul(ps_o[g % 2][HD * j:HD * (j + 1), P:2 * P], t.ones32[:, :],
                                                    acc[:, P * j:P * (j + 1)], start=True, stop=True)
                        last.then_inc(den_mm, 1)
                    elif kind == "op":
                        pe.wait_ge(fin, b * NG + NG)
                        pe.wait_ge(s.wo_in, 16)
                        for g in range(NG):
                            last = nc.tensor.matmul(ps_s[0][:, KB:2 * KB], oT[:, g, :], t.wo[:, g, :],
                                                    start=(g == 0), stop=(g == NG - 1))
                        last.then_inc(op_mm, 1)


def w1_part(n):
    return slice(n // 2, n // 2 + 1), slice(FF // 2 * (n % 2), FF // 2 * (n % 2 + 1))


def self_attention(nc, io, t, s):
    with ExitStack() as ctx:
        def sb(name, shape, dt=F32):
            return ctx.enter_context(nc.sbuf_tensor(name, shape, dt))

        def sem(name):
            return ctx.enter_context(nc.semaphore(name))

        w_raw = [sb(f"a_raw{i}", [P, NC, D]) for i in range(4)]
        w_hi = [sb(f"a_hi{i}", [P, NC, D], F16) for i in range(4)]
        w_lo = [sb(f"a_lo{i}", [P, NC, D], F16) for i in range(4)]
        bias = sb("a_bias", [P, 4, D])
        rope = sb("a_rope", [P, 2, HD])
        stats, mv, rstd = sb("a_stats", [P, NB, 6]), sb("a_mv", [P, NB, 2]), sb("a_rstd", [P, NB])
        hat = sb("a_hat", [P, NB, D])
        xT_hi, xT_lo = sb("a_xT_hi", [P, 2, NC, P], F16), sb("a_xT_lo", [P, 2, NC, P], F16)
        qk = sb("a_qk", [P, 2, D])
        vals = sb("a_vals", [P, 3, D])
        rot, cosed = sb("a_rot", [P, 2, D]), sb("a_cosed", [P, 2, D])
        qkT = sb("a_qkT", [P, 2, NG, P])
        m, rsum, rinv = sb("a_m", [P, HEADS]), sb("a_rsum", [P, HEADS]), sb("a_rinv", [P, HEADS])
        prob = sb("a_prob", [P, 2, HEADS, P])
        probT = sb("a_probT", [P, HEADS, P])
        oT_hi, oT_lo = sb("a_oT_hi", [P, NG, P], F16), sb("a_oT_lo", [P, NG, P], F16)
        y = sb("a_y", [P, D])
        m_stats, m_mv, m_rstd = sb("am_stats", [P, 2, 6]), sb("am_mv", [P, 2, 2]), sb("am_rstd", [P, 2])
        m_hat, gT = sb("am_hat", [P, 2, D]), sb("am_gT", [P, NC, P])
        ps_p = ctx.enter_context(nc.psum_tensor("a_psp", [P, HEADS, P], F32))
        ps_t = [ctx.enter_context(nc.psum_tensor(f"a_pst{i}", [P, HPG, P], F32)) for i in range(2)]
        ps_r = [ctx.enter_context(nc.psum_tensor(f"a_psr{i}", [P, D], F32)) for i in range(2)]

        w_in, misc_in = [sem(f"a_w_in{i}") for i in range(4)], sem("a_misc_in")
        st, var, powed, normed = sem("a_st"), sem("a_var"), sem("a_pow"), sem("a_normed")
        hi_done, lo_done = sem("a_hi_done"), sem("a_lo_done")
        tr, tr_hi, tr_lo = sem("a_tr"), sem("a_tr_hi"), sem("a_tr_lo")
        mm, biased = sem("a_mm"), sem("a_biased")
        cos_done, rot_done, roped = sem("a_cos"), sem("a_rot_s"), sem("a_roped")
        qk_tr, qk_tr_out = sem("a_qk_tr"), sem("a_qk_tr_out")
        scored, maxed, exped, inv, scaled = sem("a_scored"), sem("a_maxed"), sem("a_exped"), sem("a_inv"), sem("a_scaled")
        p_tr, p_out_act, p_out_dve = sem("a_p_tr"), sem("a_p_out_act"), sem("a_p_out_dve")
        o_mm, o_hi, o_lo = sem("a_o_mm"), sem("a_o_hi"), sem("a_o_lo")
        y_mm, y_out, x_done = sem("a_y_mm"), sem("a_y_out"), sem("a_x_done")

        m_st, m_var, m_powed, m_normed = sem("am_st"), sem("am_var"), sem("am_pow"), sem("am_normed")
        m_tr, m_tr_hi, m_tr_lo = sem("am_tr"), sem("am_tr_hi"), sem("am_tr_lo")
        g_tr, g_out, g_mm, logits_out = sem("am_g_tr"), sem("am_g_out"), sem("am_g_mm"), sem("am_logits")

        def slot(h):
            return NG * (h % HPG) + h // HPG

        def stages(step):
            return [step - k if 0 <= step - k < NB else None for k in range(4)]

        STEPS = range(NB + 2)

        def tail(step):
            return step == NB + 1

        groups = ((0, 1), (1, NB))
        ring = [("x", 0, tr_lo, 1)]
        for step in STEPS:
            a, b, c, d = stages(step)
            if b is not None:
                ring += [("qT", b, qk_tr_out, 2 * b + 1), ("kT", b, qk_tr_out, 2 * b + 2)]
            if a is not None:
                ring += [("q", a, biased, 3 * a + 1), ("k", a, biased, 3 * a + 2)]
            mx = [("mx", d, m_tr_lo, d + 1)] if d is not None else []
            if not tail(step):
                ring += mx
            if c is not None:
                ring += [("o", c, o_lo, c + 1)]
            if tail(step):
                ring += mx
            if a is not None:
                ring += [("v", a, biased, 3 * a + 3)]
            if a is not None and a + 1 < NB:
                ring += [("x", a + 1, tr_lo, a + 2)]
            if d is not None:
                ring += [("mg", d, g_out, d + 1)]
            if c is not None:
                ring += [("y", c, y_out, c + 1)]
            if d is not None:
                ring += [("gate", d, logits_out, d + 1)]
        place = {user[:2]: n for n, user in enumerate(ring)}

        def bank(kind, b):
            return ps_r[place[kind, b] % 2]

        block = ctx.enter_context(nc.Block())

        @block.sync
        def _(sp):
            for i, w in enumerate((io.a_wqT, io.a_wkT, io.a_wvT, io.a_woT)):
                sp.dma_start(w_raw[i][:, :, :], chunked(w)).then_inc(w_in[i], 16)
                if i == 0:
                    sp.dma_start(rope[:, :, :], io.rope).then_inc(misc_in, 16)
                    for k, v in enumerate((io.a_bq, io.a_bk, io.a_bv, io.a_bo)):
                        sp.dma_start(bias[:, k, :], v.partition_broadcast(P)).then_inc(misc_in, 16)
            sp.dma_start(t.affine[:, :, :], io.affine).then_inc(s.gate_in, 16)
            sp.dma_start(t.gate[:, :, :], io.gate).then_inc(s.gate_in, 16)
            sp.dma_start(t.w1_raw[:, :, :], io.w1[0:1, :, :, :].rearrange("e p c n -> (e p) c n")).then_inc(s.w1_in, 16)
            sp.dma_start(t.w2_raw[:, :, :], io.w2[0:1, :, :, :].rearrange("e p c n -> (e p) c n")).then_inc(s.w2_in, 16)

        @block.gpsimd
        def _(pool):
            for k, (lo, hi) in enumerate(groups):
                pool.wait_ge(var, k + 1)
                for n, (x, y_, op) in enumerate(((mv[:, lo:hi, 1], t.eps[:, lo:hi], ALU.add),
                                                 (rstd[:, lo:hi], t.inv_scale2[:, lo:hi], ALU.mult),
                                                 (rstd[:, lo:hi], t.half_neg[:, lo:hi], ALU.pow))):
                    nc.gpsimd.tensor_tensor(rstd[:, lo:hi], x, y_, op).then_inc(powed, 1)
                    pool.wait_ge(powed, 3 * k + n + 1)
            pool.wait_ge(misc_in, 16 * 5)

            def mixture_deviations(d, k):
                n = 2 * d + k
                pool.wait_ge(m_var, n + 1)
                nc.gpsimd.tensor_tensor(m_rstd[:, k:k + 1], m_mv[:, k, 1:2], t.eps[:, 0:1], ALU.add).then_inc(m_powed, 1)
                pool.wait_ge(m_powed, 2 * n + 1)
                nc.gpsimd.tensor_tensor(m_rstd[:, k:k + 1], m_rstd[:, k:k + 1], t.half_neg[:, 0:1],
                                        ALU.pow).then_inc(m_powed, 1)
                pool.wait_ge(m_powed, 2 * n + 2)

            for step in STEPS:
                b, _, c, d = stages(step)
                if d is not None:
                    mixture_deviations(d, 1)
                for i in range(2 if b is not None else 0):
                    n = 2 * b + i
                    src = qk[:, i, :].rearrange("p (h k) -> p h k", k=HD)
                    dst = rot[:, i, :].rearrange("p (h k) -> p h k", k=HD)
                    pool.wait_ge(biased, 3 * b + i + 1)
                    if n >= 2:
                        pool.wait_ge(roped, n - 1)
                    for half in range(2):
                        here, there = slice(HD // 2 * half, HD // 2 * (half + 1)), slice(HD // 2 * (1 - half), HD // 2 * (2 - half))
                        sines = rope[:, 1:2, here].broadcast_to([P, HEADS, HD // 2])
                        nc.gpsimd.tensor_tensor(dst[:, :, here], src[:, :, there], sines,
                                                ALU.mult).then_inc(rot_done, 1)
                        pool.wait_ge(rot_done, 2 * n + half + 1)
                if c is not None and c + 1 < NB:
                    mixture_deviations(c, 0)

        @block.vector
        def _(v):
            for k, (lo, hi) in enumerate(groups):
                for b in range(lo, hi):
                    nc.vector.bn_stats(stats[:, b, :], t.x[:, b, :]).then_inc(st, 1)
                v.wait_ge(st, hi)
                for b in range(lo, hi):
                    last = nc.vector.bn_aggr(mv[:, b, :], stats[:, b, :])
                last.then_inc(var, 1)
            for k, (lo, hi) in enumerate(groups):
                v.wait_ge(powed, 3 * (k + 1))
                for b in range(lo, hi):
                    nc.vector.tensor_scalar(hat[:, b, :], t.x[:, b, :], mv[:, b, 0:1], rstd[:, b:b + 1],
                                            ALU.subtract, ALU.mult).then_inc(normed, 1)

            def low_weights(i):
                v.wait_ge(hi_done, i + 1)
                nc.vector.scalar_tensor_tensor(
                    out=w_lo[i][:, :, :].rearrange("p c n -> p (c n)"),
                    in0=w_raw[i][:, :, :].rearrange("p c n -> p (c n)"), scalar=W_SCALE,
                    in1=w_hi[i][:, :, :].rearrange("p c n -> p (c n)"), op0=ALU.mult,
                    op1=ALU.subtract).then_inc(lo_done, 1)

            def project_out(i, b):
                if b == 0:
                    low_weights(i + 1)
                dst = vals[:, b % 3, :] if i == 2 else qk[:, i, :]
                v.wait_ge(mm, 3 * b + i + 1)
                nc.vector.scalar_tensor_tensor(out=dst, in0=bank("qkv"[i], b)[:, :], scalar=UNSCALE,
                                               in1=bias[:, i, :], op0=ALU.mult, op1=ALU.add).then_inc(biased, 1)
                if i < 2:
                    v.wait_ge(biased, 3 * b + i + 1)
                    nc.vector.tensor_tensor(cosed[:, i, :].rearrange("p (h k) -> p h k", k=HD),
                                            dst.rearrange("p (h k) -> p h k", k=HD),
                                            rope[:, 0:1, :].broadcast_to([P, HEADS, HD]), ALU.mult).then_inc(cos_done, 1)

            def rope_out(i, b):
                n = 2 * b + i
                v.wait_ge(cos_done, n + 1)
                v.wait_ge(rot_done, 2 * n + 2)
                nc.vector.tensor_tensor(qk[:, i, :], cosed[:, i, :], rot[:, i, :], ALU.add).then_inc(roped, 1)

            def x_low(b):
                v.wait_ge(tr_hi, b + 1)
                nc.vector.tensor_tensor(xT_lo[:, b % 2, :, :], bank("x", b)[:, :].rearrange("p (c n) -> p c n", c=NC),
                                        xT_hi[:, b % 2, :, :], ALU.subtract).then_inc(tr_lo, 1)

            def mixture_variance(src, d, k):
                n = 2 * d + k
                nc.vector.bn_stats(m_stats[:, k, :], src).then_inc(m_st, 1)
                v.wait_ge(m_st, n + 1)
                nc.vector.bn_aggr(m_mv[:, k, :], m_stats[:, k, :]).then_inc(m_var, 1)

            def mixture_normalise(src, d, k):
                n = 2 * d + k
                v.wait_ge(m_powed, 2 * n + 2)
                if d:
                    v.wait_ge((m_tr, g_tr)[k], d)
                nc.vector.tensor_scalar(m_hat[:, k, :], src, m_mv[:, k, 0:1], m_rstd[:, k:k + 1], ALU.subtract,
                                        ALU.mult).then_inc(m_normed, 1)

            def split_w1(n):
                c, half = w1_part(n)
                v.wait_ge(s.w1_hi, n + 1)
                nc.vector.scalar_tensor_tensor(out=t.w1_lo[:, c, half].rearrange("p c n -> p (c n)"),
                                               in0=t.w1_raw[:, c, half].rearrange("p c n -> p (c n)"), scalar=W_SCALE,
                                               in1=t.w1_hi[:, c, half].rearrange("p c n -> p (c n)"), op0=ALU.mult,
                                               op1=ALU.subtract).then_inc(s.w1_lo, 1)

            def mixture_low(d):
                v.wait_ge(m_tr_hi, d + 1)
                nc.vector.scalar_tensor_tensor(out=t.xT_lo[:, :, P * d:P * (d + 1)],
                                               in0=bank("mx", d)[:, :].rearrange("p (c n) -> p c n", c=NC),
                                               scalar=A_SCALE, in1=t.xT_hi[:, :, P * d:P * (d + 1)], op0=ALU.mult,
                                               op1=ALU.subtract).then_inc(m_tr_lo, 1)

            def scale(b):
                v.wait_ge(exped, b + 1)
                nc.vector.reciprocal(rinv[:, :], rsum[:, :]).then_inc(inv, 1)
                v.wait_ge(inv, b + 1)
                nc.vector.tensor_tensor(prob[:, b % 2, :, :], prob[:, b % 2, :, :],
                                        rinv[:, :].unsqueeze(2).broadcast_to([P, HEADS, P]),
                                        ALU.mult).then_inc(scaled, 1)

            x_low(0)
            low_weights(0)
            v.wait_ge(misc_in, 16 * 5)
            for step in STEPS:
                a, b, c, d = stages(step)
                if d is not None:
                    mixture_normalise(t.x[:, d, :], d, 0)
                    v.wait_ge(m_normed, 2 * d + 1)
                    mixture_variance(m_hat[:, 0, :], d, 1)
                if a is not None:
                    project_out(0, a)
                if b is not None:
                    v.wait_ge(scored, b + 1)
                    nc.vector.tensor_reduce(m[:, :], ps_p[:, :, :], AX.X, ALU.max).then_inc(maxed, 1)
                    v.wait_ge(maxed, 2 * b + 1)
                    nc.vector.tensor_scalar(m[:, :], m[:, :], -SM_SCALE, None, ALU.mult).then_inc(maxed, 1)
                if a is not None:
                    project_out(1, a)
                if d is not None and not tail(step):
                    mixture_low(d)
                if c is not None:
                    for n in (1, 3):
                        v.wait_ge(p_tr, 4 * c + n + 1)
                        nc.vector.tensor_copy(probT[:, HPG * n:HPG * (n + 1), :], ps_t[n % 2][:, :, :]).then_inc(p_out_dve, 1)
                if a is not None:
                    rope_out(0, a)
                if c is not None:
                    v.wait_ge(o_hi, c + 1)
                    nc.vector.scalar_tensor_tensor(out=oT_lo[:, :, :], in0=bank("o", c)[:, :].rearrange("p (g n) -> p g n", g=NG),
                                                   scalar=A_SCALE, in1=oT_hi[:, :, :], op0=ALU.mult,
                                                   op1=ALU.subtract).then_inc(o_lo, 1)
                if d is not None:
                    if tail(step):
                        mixture_low(d)
                    mixture_normalise(m_hat[:, 0, :], d, 1)
                if b is not None and a is None:
                    scale(b)
                if a is not None:
                    rope_out(1, a)
                    project_out(2, a)
                    if a + 1 < NB:
                        x_low(a + 1)
                if c is not None:
                    v.wait_ge(y_mm, c + 1)
                    nc.vector.scalar_tensor_tensor(out=y[:, :], in0=bank("y", c)[:, :], scalar=UNSCALE,
                                                   in1=bias[:, 3, :], op0=ALU.mult, op1=ALU.add).then_inc(y_out, 1)
                    v.wait_ge(y_out, c + 1)
                    nc.vector.tensor_tensor(t.x[:, c, :], t.x[:, c, :], y[:, :], ALU.add).then_inc(x_done, 1)
                    if c + 1 < NB:
                        v.wait_ge(x_done, c + 1)
                        mixture_variance(t.x[:, c, :], c, 0)
                if d is not None:
                    v.wait_ge(g_mm, d + 1)
                    nc.vector.tensor_copy(t.logits[:, d, :], bank("gate", d)[:, 0:EXPERTS]).then_inc(logits_out, 1)
                if b is not None and a is not None:
                    scale(b)
                if step in (NB - 1, NB):
                    for n in range(NF // 2 * (step - NB + 1), NF // 2 * (step - NB + 2)):
                        split_w1(n)

        @block.scalar
        def _(act):
            def high_weights(i):
                act.wait_ge(w_in[i], 16)
                nc.scalar.activation(w_hi[i][:, :, :], w_raw[i][:, :, :], ACT.Copy, scale=W_SCALE).then_inc(hi_done, 1)

            def x_high(b):
                act.wait_ge(tr, b + 1)
                if b >= 2:
                    act.wait_ge(mm, 3 * (b - 1))
                nc.scalar.activation(xT_hi[:, b % 2, :, :], bank("x", b)[:, :].rearrange("p (c n) -> p c n", c=NC),
                                     ACT.Copy).then_inc(tr_hi, 1)

            def mixture_high(d):
                act.wait_ge(m_tr, d + 1)
                nc.scalar.activation(t.xT_hi[:, :, P * d:P * (d + 1)],
                                     bank("mx", d)[:, :].rearrange("p (c n) -> p c n", c=NC), ACT.Copy,
                                     scale=A_SCALE).then_inc(m_tr_hi, 1)

            high_weights(0)
            x_high(0)
            for i in (1, 2, 3):
                high_weights(i)
            for step in STEPS:
                a, b, c, d = stages(step)
                if b is not None:
                    for i, kind in enumerate(("qT", "kT")):
                        act.wait_ge(qk_tr, 2 * b + i + 1)
                        nc.scalar.activation(qkT[:, i, :, :], bank(kind, b)[:, :].rearrange("p (g n) -> p g n", g=NG),
                                             ACT.Copy).then_inc(qk_tr_out, 1)
                if d is not None and not tail(step):
                    mixture_high(d)
                if c is not None:
                    for n in (0, 2):
                        act.wait_ge(p_tr, 4 * c + n + 1)
                        nc.scalar.activation(probT[:, HPG * n:HPG * (n + 1), :], ps_t[n % 2][:, :, :],
                                             ACT.Copy).then_inc(p_out_act, 1)
                if c is not None and b is None:
                    act.wait_ge(o_mm, c + 1)
                    nc.scalar.activation(oT_hi[:, :, :], bank("o", c)[:, :].rearrange("p (g n) -> p g n", g=NG),
                                         ACT.Copy, scale=A_SCALE).then_inc(o_hi, 1)
                if b is not None:
                    act.wait_ge(maxed, 2 * b + 2)
                    for n, h in enumerate(range(HEADS)):
                        if n == HEADS // 2 and c is not None:
                            act.wait_ge(o_mm, c + 1)
                            nc.scalar.activation(oT_hi[:, :, :], bank("o", c)[:, :].rearrange("p (g n) -> p g n", g=NG),
                                                 ACT.Copy, scale=A_SCALE).then_inc(o_hi, 1)
                        last = nc.scalar.activation(prob[:, b % 2, h, :], ps_p[:, h, :], ACT.Exp, bias=m[:, h:h + 1],
                                                    scale=SM_SCALE, accum_out=rsum[:, h:h + 1])
                    last.then_inc(exped, 1)
                if a is not None and a + 1 < NB:
                    x_high(a + 1)
                if d is not None and tail(step):
                    mixture_high(d)
                if d is not None:
                    if d == 0:
                        act.wait_ge(s.gate_in, 32)
                    act.wait_ge(g_tr, d + 1)
                    if d:
                        act.wait_ge(g_mm, d)
                    for k in range(NC):
                        last = nc.scalar.activation(gT[:, k, :], bank("mg", d)[:, P * k:P * (k + 1)], ACT.Identity,
                                                    bias=t.affine[:, 1, k:k + 1], scale=t.affine[:, 0, k:k + 1])
                    last.then_inc(g_out, 1)
                if step == NB - 1:
                    act.wait_ge(s.w1_in, 16)
                    for n in range(NF):
                        c_, half = w1_part(n)
                        nc.scalar.activation(t.w1_hi[:, c_, half], t.w1_raw[:, c_, half], ACT.Copy,
                                             scale=W_SCALE).then_inc(s.w1_hi, 1)

        @block.tensor
        def _(pe):
            def free_bank(kind, b):
                n = place[kind, b]
                if n >= 2:
                    pe.wait_ge(ring[n - 2][2], ring[n - 2][3])
                return ps_r[n % 2]

            def project(i, b):
                to = free_bank("qkv"[i], b)
                if b == 0:
                    pe.wait_ge(lo_done, i + 1)
                for c in range(NC):
                    hi, lo = xT_hi[:, b % 2, c, :], xT_lo[:, b % 2, c, :]
                    nc.tensor.matmul(to[:, :], hi, w_hi[i][:, c, :], start=(c == 0), stop=False)
                    nc.tensor.matmul(to[:, :], hi, w_lo[i][:, c, :], start=False, stop=False)
                    last = nc.tensor.matmul(to[:, :], lo, w_hi[i][:, c, :], start=False,
                                            stop=(c == NC - 1))
                last.then_inc(mm, 1)

            def transposes(kind, b, src):
                to = free_bank(kind, b)
                for k in range(NC):
                    last = nc.tensor.transpose(to[:, P * k:P * (k + 1)], src[:, P * k:P * (k + 1)], t.ident[:, :])
                return last

            pe.wait_ge(normed, 1)
            transposes("x", 0, hat[:, 0, :]).then_inc(tr, 1)
            for step in STEPS:
                a, b, c, d = stages(step)
                if b is not None:
                    for i in range(2):
                        pe.wait_ge(roped, 2 * b + i + 1)
                        transposes(("qT", "kT")[i], b, qk[:, i, :]).then_inc(qk_tr, 1)
                if a is not None:
                    pe.wait_ge(tr_lo, a + 1)
                    project(0, a)
                if b is not None:
                    pe.wait_ge(qk_tr_out, 2 * b + 2)
                    if b:
                        pe.wait_ge(exped, b)
                    for h in range(HEADS):
                        g, rows = h // HPG, slice(HD * (h % HPG), HD * (h % HPG + 1))
                        last = nc.tensor.matmul(ps_p[:, slot(h), :], qkT[rows, 0, g, :], qkT[rows, 1, g, :],
                                                start=True, stop=True)
                    last.then_inc(scored, 1)
                if a is not None:
                    project(1, a)
                if d is not None and not tail(step):
                    pe.wait_ge(m_normed, 2 * d + 1)
                    transposes("mx", d, m_hat[:, 0, :]).then_inc(m_tr, 1)
                if c is not None:
                    pe.wait_ge(scaled, c + 1)
                    for n in range(HEADS // HPG):
                        if n >= 2:
                            pe.wait_ge(p_out_act if n % 2 == 0 else p_out_dve, 2 * c + n // 2)
                        for k in range(HPG):
                            last = nc.tensor.transpose(ps_t[n % 2][:, k, :], prob[:, c % 2, HPG * n + k, :], t.ident[:, :])
                        last.then_inc(p_tr, 1)
                    pe.wait_ge(p_out_act, 2 * c + 2)
                    pe.wait_ge(p_out_dve, 2 * c + 2)
                    to = free_bank("o", c)
                    for h in range(HEADS):
                        g, rows = h // HPG, slice(HD * (h % HPG), HD * (h % HPG + 1))
                        last = nc.tensor.matmul(to[rows, P * g:P * (g + 1)], vals[:, c % 3, HD * h:HD * (h + 1)],
                                                probT[:, slot(h), :], start=True, stop=True)
                    last.then_inc(o_mm, 1)
                if d is not None and tail(step):
                    pe.wait_ge(m_normed, 2 * d + 1)
                    transposes("mx", d, m_hat[:, 0, :]).then_inc(m_tr, 1)
                if a is not None:
                    project(2, a)
                    if a + 1 < NB:
                        pe.wait_ge(normed, a + 2)
                        transposes("x", a + 1, hat[:, a + 1, :]).then_inc(tr, 1)
                if d is not None:
                    pe.wait_ge(m_normed, 2 * d + 2)
                    transposes("mg", d, m_hat[:, 1, :]).then_inc(g_tr, 1)
                if c is not None:
                    if c == 0:
                        pe.wait_ge(lo_done, 4)
                    to = free_bank("y", c)
                    pe.wait_ge(o_lo, c + 1)
                    for g in range(NG):
                        nc.tensor.matmul(to[:, :], oT_hi[:, g, :], w_hi[3][:, g, :], start=(g == 0), stop=False)
                        nc.tensor.matmul(to[:, :], oT_hi[:, g, :], w_lo[3][:, g, :], start=False, stop=False)
                        last = nc.tensor.matmul(to[:, :], oT_lo[:, g, :], w_hi[3][:, g, :], start=False,
                                                stop=(g == NG - 1))
                    last.then_inc(y_mm, 1)
                if d is not None:
                    to = free_bank("gate", d)
                    pe.wait_ge(g_out, d + 1)
                    for k in range(NC):
                        last = nc.tensor.matmul(to[:, 0:EXPERTS], gT[:, k, :], t.gate[:, k, :], start=(k == 0),
                                                stop=(k == NC - 1))
                    last.then_inc(g_mm, 1)


def mixture(nc, io, t, s):
    with ExitStack() as ctx:
        def sb(name, shape, dt=F32):
            return ctx.enter_context(nc.sbuf_tensor(name, shape, dt))

        def sem(name):
            return ctx.enter_context(nc.semaphore(name))

        w1_raw, w2_raw, w1_hi, w1_lo, xT_hi, xT_lo = t.w1_raw, t.w2_raw, t.w1_hi, t.w1_lo, t.xT_hi, t.xT_lo
        affine, gate = t.affine, t.gate
        w2_hi, w2_lo = sb("w2_hi", [P, NF, D], F16), sb("w2_lo", [P, NF, D], F16)
        h_f = sb("h_f", [P, 2, TOK])
        h_hi, h_lo = sb("h_hi", [P, NF, TOK], F16), sb("h_lo", [P, NF, TOK], F16)
        stats, mv, rstd = sb("m_stats", [P, 2, 6]), sb("m_mv", [P, 2, 2]), sb("m_rstd", [P, 2])
        hat = sb("m_hat", [P, 2, D])
        gT = sb("gT", [P, NC, P])
        rank = sb("rank", [P, NB, EXPERTS])
        prob, left = sb("m_prob", [P, NB, EXPERTS]), sb("m_left", [P, NB, EXPERTS])
        best, first = sb("m_best", [P, NB]), sb("m_first", [P, NB])
        sel = sb("m_sel", [P, 2, NB, EXPERTS])
        comb = sb("m_comb", [P, NB, EXPERTS])
        ps_h = [ctx.enter_context(nc.psum_tensor(f"ps_h{i}", [P, TOK], F32)) for i in range(2)]
        ps_y = [ctx.enter_context(nc.psum_tensor(f"ps_y{i}", [P, D], F32)) for i in range(NB)]
        ps_g = ctx.enter_context(nc.psum_tensor("ps_g", [P, EXPERTS], F32))

        w1_in, w2_in = s.w1_in, s.w2_in
        st, var, powed, chain = sem("m_st"), sem("m_var"), sem("m_pow"), sem("m_chain")
        normed, ranked = sem("m_normed"), sem("ranked")
        tr, tr_hi, tr_lo, g_tr, g_out, g_mm, g_exp = (sem("m_tr"), sem("m_tr_hi"), sem("m_tr_lo"), sem("g_tr"),
                                                      sem("g_out"), sem("g_mm"), sem("g_exp"))
        w1_hi_s, w1_lo_s, w2_hi_s, w2_lo_s = s.w1_hi, s.w1_lo, sem("w2_hi_s"), sem("w2_lo_s")
        up, gelu, h_hi_s, h_lo_s, down, y_out = (sem("up"), sem("gelu"), sem("h_hi_s"), sem("h_lo_s"), sem("down"),
                                                 sem("m_y_out"))
        out_sem = sem("out_sem")
        block = ctx.enter_context(nc.Block())

        @block.sync
        def _(sp):
            sp.wait_ge(w1_lo_s, NF)
            sp.dma_start(w1_raw[:, :, :], io.w1[1:2, :, :, :].rearrange("e p c n -> (e p) c n")).then_inc(w1_in, 16)
            with sp.Fori(0, EXPERTS) as e:
                sp.wait_ge(w2_lo_s, (e + 1) * NF)
                sp.dma_start(w2_raw[:, :, :],
                             io.w2[bass.ds(e + 1, 1), :, :, :].rearrange("e p c n -> (e p) c n")).then_inc(w2_in, 16)
                sp.wait_ge(w1_lo_s, (e + 2) * NF)
                sp.dma_start(w1_raw[:, :, :],
                             io.w1[bass.ds(e + 2, 1), :, :, :].rearrange("e p c n -> (e p) c n")).then_inc(w1_in, 16)
            sp.wait_ge(w1_in, 16 * (EXPERTS + 2))
            sp.wait_ge(w2_in, 16 * (EXPERTS + 1))
            sp.wait_ge(y_out, NB * EXPERTS)
            sp.dma_start(io.out.rearrange("b t c -> t b c"), t.x[:, :, :]).then_inc(out_sem, 16)
            sp.wait_ge(out_sem, 16)

        @block.gpsimd
        def _(pool):
            for k in range(2):
                pool.wait_ge(var, k + 1)
                nc.gpsimd.tensor_tensor(rstd[:, k:k + 1], mv[:, k, 1:2], t.eps[:, 0:1], ALU.add).then_inc(powed, 1)
                pool.wait_ge(powed, 2 * k + 1)
                nc.gpsimd.tensor_tensor(rstd[:, k:k + 1], rstd[:, k:k + 1], t.half_neg[:, 0:1], ALU.pow).then_inc(powed, 1)
                pool.wait_ge(powed, 2 * k + 2)
            for i in range(EXPERTS):
                nc.gpsimd.memset(rank[:, :, i:i + 1], float(EXPERTS - i)).then_inc(ranked, 1)
                pool.wait_ge(ranked, i + 1)

        @block.vector
        def _(v):
            done = [0]

            def then_wait(ins):
                done[0] += 1
                ins.then_inc(chain, 1)
                v.wait_ge(chain, done[0])

            last_b = NB - 1
            for k, src in enumerate((t.x[:, last_b, :], hat[:, 0, :])):
                nc.vector.bn_stats(stats[:, k, :], src).then_inc(st, 1)
                v.wait_ge(st, k + 1)
                nc.vector.bn_aggr(mv[:, k, :], stats[:, k, :]).then_inc(var, 1)
                v.wait_ge(var, k + 1)
                v.wait_ge(powed, 2 * k + 2)
                nc.vector.tensor_scalar(hat[:, k, :], src, mv[:, k, 0:1], rstd[:, k:k + 1],
                                        ALU.subtract, ALU.mult).then_inc(normed, 1)
                v.wait_ge(normed, k + 1)
                if k == 0:
                    here = slice(P * last_b, P * NB)
                    v.wait_ge(tr_hi, 1)
                    nc.vector.scalar_tensor_tensor(out=xT_lo[:, :, here],
                                                   in0=ps_h[0][:, :].rearrange("p (c n) -> p c n", c=NC), scalar=A_SCALE,
                                                   in1=xT_hi[:, :, here], op0=ALU.mult, op1=ALU.subtract).then_inc(tr_lo, 1)

            def split_w1(n, e):
                c, half = w1_part(n)
                v.wait_ge(w1_hi_s, e * NF + n + 1)
                nc.vector.scalar_tensor_tensor(out=w1_lo[:, c, half].rearrange("p c n -> p (c n)"),
                                               in0=w1_raw[:, c, half].rearrange("p c n -> p (c n)"), scalar=W_SCALE,
                                               in1=w1_hi[:, c, half].rearrange("p c n -> p (c n)"), op0=ALU.mult,
                                               op1=ALU.subtract).then_inc(w1_lo_s, 1)

            v.wait_ge(g_mm, 1)
            logits = t.logits
            then_wait(nc.vector.tensor_copy(logits[:, last_b, :], ps_g[:, :]))
            wide = [P, NB, EXPERTS]
            then_wait(nc.vector.tensor_reduce(best[:, :], logits[:, :, :], AX.X, ALU.max))
            then_wait(nc.vector.tensor_tensor(prob[:, :, :], logits[:, :, :], best[:, :].unsqueeze(2).broadcast_to(wide),
                                              ALU.subtract))
            v.wait_ge(g_exp, 1)
            then_wait(nc.vector.tensor_reduce(best[:, :], prob[:, :, :], AX.X, ALU.add))
            then_wait(nc.vector.reciprocal(best[:, :], best[:, :]))
            then_wait(nc.vector.tensor_tensor(prob[:, :, :], prob[:, :, :], best[:, :].unsqueeze(2).broadcast_to(wide),
                                              ALU.mult))
            v.wait_ge(ranked, EXPERTS)
            for k in range(2):
                src = prob if k == 0 else left
                now = sel[:, k, :, :]
                then_wait(nc.vector.tensor_reduce(best[:, :], src[:, :, :], AX.X, ALU.max))
                then_wait(nc.vector.tensor_tensor(now, src[:, :, :], best[:, :].unsqueeze(2).broadcast_to(wide),
                                                  ALU.is_equal))
                then_wait(nc.vector.tensor_tensor(now, now, rank[:, :, :], ALU.mult))
                then_wait(nc.vector.tensor_reduce(first[:, :], now, AX.X, ALU.max))
                then_wait(nc.vector.tensor_tensor(now, now, first[:, :].unsqueeze(2).broadcast_to(wide), ALU.is_equal))
                if k == 0:
                    then_wait(nc.vector.scalar_tensor_tensor(
                        out=left[:, :, :].rearrange("p b e -> p (b e)"), in0=now.rearrange("p b e -> p (b e)"), scalar=-4.0,
                        in1=prob[:, :, :].rearrange("p b e -> p (b e)"), op0=ALU.mult, op1=ALU.add))
            then_wait(nc.vector.tensor_tensor(sel[:, 0, :, :], sel[:, 0, :, :], sel[:, 1, :, :], ALU.add))
            then_wait(nc.vector.tensor_tensor(comb[:, :, :], sel[:, 0, :, :], prob[:, :, :], ALU.mult))
            then_wait(nc.vector.tensor_scalar(comb[:, :, :], comb[:, :, :], UNSCALE, None, ALU.mult))

            with v.Fori(0, EXPERTS) as e:
                for f in range(NF):
                    v.wait_ge(h_hi_s, e * NF + f + 1)
                    nc.vector.scalar_tensor_tensor(out=h_lo[:, f, :], in0=h_f[:, f % 2, :], scalar=A_SCALE,
                                                   in1=h_hi[:, f, :], op0=ALU.mult, op1=ALU.subtract).then_inc(h_lo_s, 1)
                    v.wait_ge(w2_hi_s, e * NF + f + 1)
                    nc.vector.scalar_tensor_tensor(out=w2_lo[:, f, :], in0=w2_raw[:, f, :], scalar=W_SCALE,
                                                   in1=w2_hi[:, f, :], op0=ALU.mult, op1=ALU.subtract).then_inc(w2_lo_s, 1)
                for n in range(NF):
                    split_w1(n, e + 1)
                v.wait_ge(down, e + 1)
                for b in range(NB):
                    nc.vector.scalar_tensor_tensor(
                        out=t.x[:, b, :], in0=ps_y[b][:, :],
                        scalar=comb[:, b, bass.ds(e, 1)], in1=t.x[:, b, :], op0=ALU.mult, op1=ALU.add).then_inc(y_out, 1)

        @block.scalar
        def _(act):
            def split_w1(n, e):
                c, half = w1_part(n)
                if n == 0:
                    act.wait_ge(w1_in, (e + 1) * 16)
                nc.scalar.activation(w1_hi[:, c, half], w1_raw[:, c, half], ACT.Copy, scale=W_SCALE).then_inc(w1_hi_s, 1)

            here = slice(P * (NB - 1), P * NB)
            act.wait_ge(tr, 1)
            nc.scalar.activation(xT_hi[:, :, here], ps_h[0][:, :].rearrange("p (c n) -> p c n", c=NC),
                                 ACT.Copy, scale=A_SCALE).then_inc(tr_hi, 1)
            act.wait_ge(g_tr, 1)
            for c in range(NC):
                last = nc.scalar.activation(gT[:, c, :], ps_y[0][:, P * c:P * (c + 1)], ACT.Identity,
                                            bias=affine[:, 1, c:c + 1], scale=affine[:, 0, c:c + 1])
            last.then_inc(g_out, 1)
            act.wait_ge(chain, 3)
            nc.scalar.activation(prob[:, :, :], prob[:, :, :], ACT.Exp).then_inc(g_exp, 1)
            with act.Fori(0, EXPERTS) as e:
                act.wait_ge(w2_in, (e + 1) * 16)
                for f in range(NF):
                    act.wait_ge(up, e * NF + f + 1)
                    if f >= 2:
                        act.wait_ge(h_lo_s, e * NF + f - 1)
                    nc.scalar.activation(h_f[:, f % 2, :], ps_h[f % 2][:, :], ACT.Gelu, scale=UNSCALE).then_inc(gelu, 1)
                    act.wait_ge(gelu, e * NF + f + 1)
                    nc.scalar.activation(h_hi[:, f, :], h_f[:, f % 2, :], ACT.Copy, scale=A_SCALE).then_inc(h_hi_s, 1)
                    nc.scalar.activation(w2_hi[:, f, :], w2_raw[:, f, :], ACT.Copy, scale=W_SCALE).then_inc(w2_hi_s, 1)
                for n in range(NF):
                    split_w1(n, e + 1)

        @block.tensor
        def _(pe):
            def transposes(to, src):
                for c in range(NC):
                    last = nc.tensor.transpose(to[:, P * c:P * (c + 1)], src[:, P * c:P * (c + 1)], t.ident[:, :])
                return last

            def router():
                pe.wait_ge(normed, 2)
                transposes(ps_y[0], hat[:, 1, :]).then_inc(g_tr, 1)

            def router_scores():
                pe.wait_ge(g_out, 1)
                for c in range(NC):
                    last = nc.tensor.matmul(ps_g[:, :], gT[:, c, :], gate[:, c, :], start=(c == 0), stop=(c == NC - 1))
                last.then_inc(g_mm, 1)

            def expert(e, first):
                pe.wait_ge(w1_lo_s, (e + 1) * NF)
                for f in range(NF):
                    if f >= 2:
                        pe.wait_ge(gelu, e * NF + f - 1)
                    col = slice(P * f, P * (f + 1))
                    for c in range(NC):
                        nc.tensor.matmul(ps_h[f % 2][:, :], w1_hi[:, c, col], xT_hi[:, c, :], start=(c == 0), stop=False)
                        nc.tensor.matmul(ps_h[f % 2][:, :], w1_hi[:, c, col], xT_lo[:, c, :], start=False, stop=False)
                        last = nc.tensor.matmul(ps_h[f % 2][:, :], w1_lo[:, c, col], xT_hi[:, c, :], start=False,
                                                stop=(c == NC - 1))
                    last.then_inc(up, 1)
                    if first and f == 0:
                        router()
                    if first and f == 1:
                        router_scores()
                for f in range(NF):
                    pe.wait_ge(h_lo_s, e * NF + f + 1)
                    pe.wait_ge(w2_lo_s, e * NF + f + 1)
                    for b in range(NB):
                        tok = slice(P * b, P * (b + 1))
                        nc.tensor.matmul(ps_y[b][:, :], h_hi[:, f, tok], w2_hi[:, f, :], start=(f == 0), stop=False)
                        nc.tensor.matmul(ps_y[b][:, :], h_hi[:, f, tok], w2_lo[:, f, :], start=False, stop=False)
                        last = nc.tensor.matmul(ps_y[b][:, :], h_lo[:, f, tok], w2_hi[:, f, :], start=False,
                                                stop=(f == NF - 1))
                last.then_inc(down, 1)

            pe.wait_ge(normed, 1)
            transposes(ps_h[0], hat[:, 0, :]).then_inc(tr, 1)
            pe.wait_ge(tr_lo, 1)
            expert(0, True)
            with pe.Fori(1, EXPERTS) as e:
                expert(e, False)


def program(nc, io):
    with ExitStack() as ctx:
        def sb(name, shape, dt=F32):
            return ctx.enter_context(nc.sbuf_tensor(name, shape, dt))

        t, s = Named(), Named()
        t.x = sb("x_sb", [P, NB, D])
        t.ident = sb("ident_sb", [P, P])
        t.half_neg, t.eps, t.inv_scale2 = sb("half_neg", [P, NB]), sb("eps", [P, NB]), sb("inv_scale2", [P, NB])
        s.wo_in = ctx.enter_context(nc.semaphore("wo_in"))
        s.mask_rows_out = ctx.enter_context(nc.semaphore("mask_rows_out"))
        io.mask_rows = nc.dram_tensor("mask_rows", [NB, KEYS], F16, kind="Internal").ap()
        with ExitStack() as cross:
            def cb(name, shape, dt=F32):
                return cross.enter_context(nc.sbuf_tensor(name, shape, dt))

            t.ones32 = cb("ones32", [P, HD])
            t.q_stack = cb("q_stack", [P, HEADS, TOK], F16)
            t.k_stack = [cb(f"k_stack{u}", [P, HPG, KEYS], F16) for u in range(2)]
            t.wk_hi, t.wk_lo = cb("wk_hi", [P, NC, D], F16), cb("wk_lo", [P, NC, D], F16)
            t.wv_hi, t.wv_lo = cb("wv_hi", [P, NC, D], F16), cb("wv_lo", [P, NC, D], F16)
            t.wo = cb("wo_x", [P, NC, D])
            t.kbias, t.vbias = cb("kbias", [P, NG]), cb("vbias", [P, NG])
            prologue(nc, io, t, s)
            cross_attention(nc, io, t, s)
        t.w1_raw, t.w2_raw = sb("w1_raw", [P, NC, FF]), sb("w2_raw", [P, NF, D])
        t.w1_hi, t.w1_lo = sb("w1_hi", [P, NC, FF], F16), sb("w1_lo", [P, NC, FF], F16)
        t.xT_hi, t.xT_lo = sb("m_xT_hi", [P, NC, TOK], F16), sb("m_xT_lo", [P, NC, TOK], F16)
        t.affine, t.gate = sb("affine", [P, 2, NC]), sb("gate", [P, NC, EXPERTS])
        t.logits = sb("logits", [P, NB, EXPERTS])
        s.gate_in, s.w1_in, s.w2_in, s.w1_hi, s.w1_lo = [
            ctx.enter_context(nc.semaphore(name))
            for name in ("m_gate_in", "m_w1_in", "m_w2_in", "m_w1_hi", "m_w1_lo")]
        self_attention(nc, io, t, s)
        mixture(nc, io, t, s)


class Named:
    pass


def kernel(**inputs):
    import concourse.bacc as bacc
    from concourse.bass_utils import run_bass_kernel_spmd

    def plain(name):
        return np.ascontiguousarray(inputs[name])

    def transposed(name):
        return np.ascontiguousarray(np.asarray(inputs[name]).T)

    def column(name):
        return np.ascontiguousarray(np.asarray(inputs[name]).reshape(NC, P).T)

    def rotary():
        inv_freq = (1.0 / 10000.0 ** (np.arange(0, HD, 2, dtype=np.float32) / HD)).astype(np.float32)
        freqs = np.arange(P, dtype=np.float32)[:, None] * inv_freq[None, :]
        angle = np.concatenate([freqs, freqs], axis=-1).astype(np.float64)
        sign = np.concatenate([-np.ones(HD // 2), np.ones(HD // 2)])
        return np.stack([np.cos(angle), np.sin(angle) * sign], axis=1).astype(np.float32)

    def by_partition(w, ahead):
        w = w.reshape(EXPERTS, -1, P, w.shape[-1]).transpose(0, 2, 1, 3)
        return np.ascontiguousarray(np.concatenate([w, w[:ahead]]))

    tiles = np.asarray(inputs["ctx_1024"]).reshape(NB * NKT, P, D)
    arrays = {
        "x": plain("x"),
        "context": np.ascontiguousarray(np.concatenate([tiles, tiles[:2 * RAW]])),
        "mask": plain("mask_BxS2_bf1").view(np.uint8),
        "ident": np.eye(P, dtype=np.float32),
        "rope": rotary(),
        "g1": column("L0_xattn_g1"), "b1": column("L0_xattn_b1"),
        "g2": column("L0_xattn_g2"), "b2": column("L0_xattn_b2"),
        "xbo": plain("L0_xattn_bo"),
        "wqT": transposed("L0_xattn_Wq"), "wkT": transposed("L0_xattn_Wk"),
        "wvT": transposed("L0_xattn_Wv"), "woT": transposed("L0_xattn_Wo"),
        "a_wqT": transposed("L0_attn_Wq"), "a_wkT": transposed("L0_attn_Wk"),
        "a_wvT": transposed("L0_attn_Wv"), "a_woT": transposed("L0_attn_Wo"),
        "a_bq": plain("L0_attn_bq"), "a_bk": plain("L0_attn_bk"),
        "a_bv": plain("L0_attn_bv"), "a_bo": plain("L0_attn_bo"),
        "affine": np.ascontiguousarray(np.stack([column("L0_ffn_ln_gamma"), column("L0_ffn_ln_beta")], axis=1)),
        "gate": np.ascontiguousarray(np.asarray(inputs["L0_ffn_gate_w"]).T.reshape(NC, P, EXPERTS).transpose(1, 0, 2)),
        "w1": by_partition(np.asarray(inputs["L0_ffn_w1"]).transpose(0, 2, 1), 2),
        "w2": by_partition(np.asarray(inputs["L0_ffn_w2"]).transpose(0, 2, 1), 1),
    }
    nc = bacc.Bacc("TRN2", target_bir_lowering=False, num_devices=1)
    io = Named()
    for name, a in arrays.items():
        ap = nc.dram_tensor(f"in_{name}", a.shape, mybir.dt.from_np(a.dtype), kind="ExternalInput").ap()
        io.__dict__[name] = ap
    io.out = nc.dram_tensor("out", (NB, P, D), F32, kind="ExternalOutput").ap()
    program(nc, io)
    r = run_bass_kernel_spmd(nc, [{f"in_{name}": a for name, a in arrays.items()}], core_ids=[0])
    return r.results[0]["out"]
```

```python
from contextlib import ExitStack

import numpy as np
import concourse.bass as bass
from concourse import mybir

F32, F16, U8 = mybir.dt.float32, mybir.dt.float16, mybir.dt.uint8
ALU, ACT, AX = mybir.AluOpType, mybir.ActivationFunctionType, mybir.AxisListType

P = 128
NB = 4
D = 512
NC = D // P
TOK = NB * P
KEYS = 2048
NKT = KEYS // P
HEADS, HD = 16, 32
HPG = P // HD
NG = HEADS // HPG
NPAIR = NKT // 2
EPS = 1e-5
A_SCALE, W_SCALE = 16.0, 64.0
UNSCALE = 1.0 / (A_SCALE * W_SCALE)
SM_SCALE = float(1.0 / np.sqrt(HD))
MASKED = -60000.0
SHIFT_ROW, MASK_ROW = 96, 97
ROWS = 98
EXPERTS, FF = 8, 1024
NF = FF // P


def chunked(ap):
    return ap.rearrange("(c p) n -> p c n", p=P)


KB = 512
NKB = KEYS // KB
POOL_ADDS = (5, 5, 5, 4)
RAW = 4
PT = 4


def attention_steps():
    def scores(g, p):
        return [("s", g, p, 0), ("s", g, p, 1)]

    steps = []
    for kt in range(2, 8):
        n = RAW // 2 + kt - 2
        if n > 2:
            steps.append(("ln", n))
        steps += [("t", 2 * n), ("t", 2 * n + 1)] + [("v", kt, c) for c in range(NC)]
    assert 2 * n + 1 == NKT - 1
    steps += [("k", 0, kb) for kb in range(NKB)] + [("v", kt, c) for kt in (8, 9) for c in range(NC)]
    steps += [("k", 1, 0), ("next ln", 0), ("next ln", 1)] + [("k", 1, kb) for kb in (1, 2, 3)]
    steps += [("next load", 0), ("next load", 1)]
    p1 = [[("p1", g, j, kb) for h in range(2) for j in range(HPG) for kb in (2 * h, 2 * h + 1)] for g in range(NG)]
    for kt in range(10, 14):
        for c in range(NC):
            steps += [("v", kt, c), p1[0].pop(0)]
    steps += [("v", 14, c) for c in range(NC)] + [("mt", 0)] + [("v", 15, c) for c in (0, 1)]
    steps += scores(0, 0) + scores(0, 1) + [("v", 15, c) for c in (2, 3)]
    for g in range(NG):
        for p in range(NPAIR):
            if (g, p) == (NG - 1, NPAIR - 1):
                steps.append(("presum", g))
            work = [("av", g, p, 0), ("av", g, p, 1)]
            if p + 2 < NPAIR:
                work += scores(g, p + 2)
            tiles = [p1[g + 1].pop(0) for _ in range(P1_AT[g].get(p, 0))]
            if (g, p) == (2, NPAIR - 1):
                steps += tiles + work[:1] + [("mt", 3)] + work[1:]
                continue
            for n in range(5):
                steps += work[n:n + 1] + tiles[n:n + 1]
            if g < 2 and p >= NPAIR - 3:
                steps.append(("k", g + 2, p - NPAIR + 3))
            if p == 1 and g:
                steps.append(("den", g - 1))
        if g < NG - 1:
            steps.append(("sums", g))
        if g < 2:
            steps += [("mt", g + 1), ("k", g + 2, 3)] + scores(g + 1, 0) + scores(g + 1, 1)
        if g == 2:
            steps += scores(3, 0) + scores(3, 1)
    assert not any(p1)
    return steps + [("next t", 0), ("next t", 1), ("sums", NG - 1), ("next t", 2), ("next t", 3)] + \
        [("next v", 0, c) for c in range(NC)] + [("next v", 1, 0), ("next v", 1, 1)] + \
        [("den", NG - 1)] + [("next v", 1, 2), ("next v", 1, 3), ("next ln", 2), ("op",)]


P1_AT = ({2: 2, 3: 3, 4: 5, 5: 1, 6: 2, 7: 3}, {3: 1, 4: 5, 5: 4, 6: 3, 7: 3}, {2: 2, 3: 4, 4: 4, 5: 4, 6: 2}, {})


def maxima_first(steps):
    order = list(steps)
    for step in [step for step in steps if step[0] == "k" and step[1] > 1]:
        at = order.index(step)
        behind = [n for n in range(at + 1, min(at + 8, len(order))) if order[n][0] == "p1"][:2]
        if behind:
            order.remove(step)
            order.insert(behind[-1], step)
    return order


SPLITS = [("av", g, p, 1) for g, p in ((2, 4), (2, 5), (2, 6), (2, 7), (3, 1), (3, 2), (3, 3), (3, 4))]


def last_steps():
    steps = []
    for step in attention_steps():
        if not step[0].startswith("next "):
            steps.append(step)
        if step in SPLITS:
            n = 2 * SPLITS.index(step)
            steps += [("spl", n), ("spl", n + 1)]
        if step == ("av", 2, 1, 1):
            steps.append(("xln",))
    return steps


AHEAD_LN = (0, 1)
AHEAD_T = range(RAW)
AHEAD_V = (0, 1)


def of_batch(step, b):
    return ((step[0][5:], *step[1:]), b + 1) if step[0].startswith("next ") else (step, b)


NORMED = ((0, NB - 1), (NB - 1, NB))


def self_deviations(nc, pool, t, s, k):
    lo, hi = NORMED[k]
    pool.wait_ge(s.a_var, k + 1)
    for n, (x, y, op) in enumerate(((t.a_mv[:, lo:hi, 1], t.eps[:, lo:hi], ALU.add),
                                    (t.a_rstd[:, lo:hi], t.inv_scale2[:, lo:hi], ALU.mult),
                                    (t.a_rstd[:, lo:hi], t.half_neg[:, lo:hi], ALU.pow))):
        nc.gpsimd.tensor_tensor(t.a_rstd[:, lo:hi], x, y, op).then_inc(s.a_powed, 1)
        pool.wait_ge(s.a_powed, 3 * k + n + 1)


def cross_attention(nc, io, t, s):
    in_loop, at_end = attention_steps(), last_steps()
    ring = [("v", kt) for kt in AHEAD_V]
    ring += [step[:2] if step[0] == "v" else step for step in in_loop
             if step[0] == "k" or (step[0] == "v" and step[2] == 0) or (step[0] == "p1" and step[1] > 0)]
    assert len(ring) % 2 == 0
    PER_BATCH = {"v": NKT, "k": NG * NKB, "p1": NG * HPG * NKB}

    def ring_place(step):
        return ring.index(step[:2] if step[0] == "v" else step)

    KIN = 16 * 3 * HPG

    with ExitStack() as ctx:
        def sb(name, shape, dt=F32):
            return ctx.enter_context(nc.sbuf_tensor(name, shape, dt))

        def sem(name):
            return ctx.enter_context(nc.semaphore(name))

        mask_u8 = sb("mask_u8", [NB, KEYS], U8)
        vectors = sb("vectors", [P, 4, NC])
        gains = sb("gains", [P, 3, NC])
        qbias, kbias, vbias = sb("qbias", [P, NG]), sb("kbias", [P, NG]), sb("vbias", [P, NG])
        x_stats, x_mv, x_rstd = sb("x_stats", [P, NB, 6]), sb("x_mv", [P, 2, NB, 2]), sb("x_rstd", [P, 2, NB])
        wo_hi, wo_lo = sb("wo_hi", [P, NC, D], F16), sb("wo_lo", [P, NC, D], F16)
        raw = sb("raw", [P, RAW, D])
        xn = sb("xn", [P, RAW, D])
        stats = sb("c_stats", [P, 4, 6])
        mv = sb("c_mv", [P, 4, 2])
        carrier = sb("carrier", [P, 1])
        rstd = sb("c_rstd", [P, 4])
        cT_hi, cT_lo = t.cT_hi, t.cT_lo
        vals = sb("vals", [P, NKT, D])
        k_f = sb("k_f", [P, 2, KB])
        k_hi = [sb(f"k_hi{h}", [P, 2 * KB], F16) for h in range(2)]
        k_lo = [sb(f"k_lo{h}", [P, 2 * KB], F16) for h in range(2)]
        mpart = sb("mpart", [P, HPG, NKB])
        mgroup = sb("mgroup", [P, 2, HPG])
        pT = sb("pT", [P, PT, 2 * KB])
        acc_pool, acc_dve, acc = sb("acc_pool", [P, 2 * KB]), sb("acc_dve", [P, 2 * KB]), sb("acc", [P, KB])
        rden = sb("rden", [P, P])
        oT = sb("oT", [P, NG, P])
        oT_hi, oT_lo = sb("oT_hi", [P, NG, P], F16), sb("oT_lo", [P, NG, P], F16)
        w_raw = [vals[:, NC * (i + 1):NC * (i + 2), :] for i in range(3)]
        hat = pT[:, 2:4, :].rearrange("p u n -> p (u n)").rearrange("p (b n) -> p b n", b=NB)
        wq_hi, wq_lo, xT_hi, xT_lo = [t.k_stack[1][:, j, :].rearrange("p (c n) -> p c n", c=NC) for j in range(4)]
        q_hi, q_lo = [t.k_stack[0][:, j, :].rearrange("p (g n) -> p g n", g=NG) for j in range(2)]
        mask_ones, mask_neg = t.k_stack[0][0:NB, 2, :], t.k_stack[0][0:NB, 3, :]
        q_f = k_f
        bo_bc = acc
        ps_s = [ctx.enter_context(nc.psum_tensor(f"ps_s{i}", [P, 2 * KB], F32)) for i in range(2)]
        ps_r = [ctx.enter_context(nc.psum_tensor(f"ps_r{i}", [P, KB], F32)) for i in range(2)]
        ps_o = [ctx.enter_context(nc.psum_tensor(f"ps_o{i}", [P, KB], F32)) for i in range(2)]

        raw_in = [sem(f"raw_in{i}") for i in range(RAW)]
        stat_dve, var_dve, normed = sem("c_stat"), sem("c_var"), sem("c_normed")
        pool_pow = sem("c_pow")
        tr, tr_hi, tr_lo = sem("c_tr"), sem("c_tr_hi"), sem("c_tr_lo")
        v_mm, v_out = sem("v_mm"), sem("v_out")
        k_mm, k_f_out, k_hi_out, k_lo_out = sem("k_mm"), sem("k_f_out"), sem("k_hi_out"), sem("k_lo_out")
        k_in = [[sem(f"k_in{u}{h}") for h in range(2)] for u in range(2)]
        mask_in = sem("c_mask_in")
        p1_mm, p1_max, m_max, mt_mm, m_row = (sem("p1_mm"), sem("p1_max"), sem("m_max"), sem("mt_mm"),
                                                        sem("m_row"))
        s_mm, exp_done, av_mm = sem("s_mm"), sem("exp_done"), sem("av_mm")
        pool_add, dve_first, dve_second, dve_third, sums_done = (sem("pool_add"), sem("dve_first"), sem("dve_second"),
                                                                 sem("dve_third"), sem("sums_done"))
        den_mm, rden_done, norm_out, fin = sem("den_mm"), sem("rden_done"), sem("norm_out"), sem("fin")
        op_mm, x_done = sem("op_mm"), sem("x_done")
        self_in = [sem(f"self_in{i}") for i in range(4)]

        def p1_bank(step, n):
            if step[1] == 0:
                return ps_s[n % 2][:, KB * (n // 2 % 2):KB * (n // 2 % 2 + 1)]
            return ps_r[ring_place(step) % 2][:, :]

        split_hi, split_lo = sem("split_hi"), sem("split_lo")
        x_in, ident_in = [sem(f"x_in{b}") for b in range(NB)], sem("ident_in")
        w_in, vec_in, bo_in = [sem(f"w_in{i}") for i in range(4)], sem("vec_in"), sem("bo_in")
        const = sem("const")
        x_st, x_var, x_pow, x_normed = sem("x_st"), sem("x_var"), sem("x_pow"), sem("x_normed")
        gains_done, w_hi, w_lo = sem("gains_done"), sem("w_hi"), sem("w_lo")
        x_tr, x_tr_hi, x_tr_lo = sem("x_tr"), sem("x_tr_hi"), sem("x_tr_lo")
        bias_mm, bias_out = sem("bias_mm"), sem("bias_out")
        q_mm, q_out, q_hi_s, q_lo_s = sem("q_mm"), sem("q_out"), sem("q_hi_s"), sem("q_lo_s")
        mask_u8_in, mask_done, mask_rows_out, placed = (sem("mask_u8_in"), sem("mask_done"), sem("mask_rows_out"),
                                                        sem("placed"))
        folded = [(0, w_raw[0], wq_hi, wq_lo), (2, w_raw[2], t.wv_hi, t.wv_lo), (3, w_raw[0], wo_hi, wo_lo),
                  (1, w_raw[1], t.wk_hi, t.wk_lo)]
        PLACED = 16 * 3 * HPG
        CONSTS = 5

        def self_weight(n, half):
            i, c = n // NC, n % NC
            if half == "raw":
                return (raw, xn)[i % 2][:, c, :]
            return (cT_hi if half == "hi" else cT_lo)[:, c, D * i:D * (i + 1)]

        def bias_bank(i):
            return (ps_o[0], 0) if i == 1 else (ps_r[1], NG * i)

        def t_bank(kt):
            half = kt // 2 % 2
            return ps_s[kt % 2][:, KB * half:KB * (half + 1)]

        block = ctx.enter_context(nc.Block())

        @block.sync
        def _(sp):
            def load(b, kt):
                sp.dma_start(raw[:, kt % RAW, :],
                             io.context[bass.ds(b * NKT + kt, 1), :, :].rearrange("o p c -> (o p) c")
                             ).then_inc(raw_in[kt % RAW], 16)

            def reload(step, b):
                for kt in (2 * step[1], 2 * step[1] + 1):
                    sp.wait_ge(normed, b * NKT + kt + 1)
                    load(b, kt + RAW)

            for b in range(NB):
                sp.dma_start(t.x[:, b, :], io.x[b:b + 1, :, :].rearrange("b t c -> (b t) c")).then_inc(x_in[b], 16)
            sp.dma_start(vectors[:, :, :], io.vectors).then_inc(vec_in, 16)
            sp.dma_start(t.ident[:, :], io.ident).then_inc(ident_in, 16)
            sp.dma_start(w_raw[0], chunked(io.wqT)).then_inc(w_in[0], 16)
            for kt in range(RAW):
                load(0, kt)
            sp.dma_start(w_raw[2], chunked(io.wvT)).then_inc(w_in[2], 16)
            sp.dma_start(w_raw[1], chunked(io.wkT)).then_inc(w_in[1], 16)
            sp.dma_start(mask_u8[:, :], io.mask).then_inc(mask_u8_in, 16)
            sp.dma_start(bo_bc[:, :], io.xbo.partition_broadcast(P)).then_inc(bo_in, 16)
            sp.wait_ge(w_lo, 1)
            sp.wait_ge(bias_mm, 1)
            sp.dma_start(w_raw[0], chunked(io.woT)).then_inc(w_in[3], 16)
            for n in AHEAD_LN:
                reload(("ln", n), 0)
            sp.wait_ge(mask_done, 1)
            sp.wait_ge(const, CONSTS)
            sp.dma_start(io.mask_rows[:, 0, :], mask_ones).then_inc(mask_rows_out, 16)
            sp.dma_start(io.mask_rows[:, 1, :], mask_neg).then_inc(mask_rows_out, 16)
            for part_sem, k, part in ((q_hi_s, 0, q_hi), (q_hi_s, 2, q_hi), (q_lo_s, 1, q_lo)):
                sp.wait_ge(part_sem, NG)
                for j in range(HPG):
                    heads = t.q_stack[HD * k:HD * (k + 1), :, :].rearrange("p (g j) n -> p j g n", j=HPG)
                    sp.dma_start(heads[:, j, :, :], part[HD * j:HD * (j + 1), :, :]).then_inc(placed, 16)
            reload(("ln", 2), 0)

            def self_weight_in(i):
                sp.dma_start((raw, xn)[i % 2][:, :, :], chunked((io.a_wqT, io.a_wkT, io.a_wvT, io.a_woT)[i])
                             ).then_inc(self_in[i], 16)

            def one_batch(b, steps):
                for step in steps:
                    step, bb = of_batch(step, b)
                    if step[0] == "load" or (step[0] == "ln" and (bb is b or step[1] > AHEAD_LN[-1])):
                        if steps is in_loop or step[1] + RAW // 2 < NKT // 2:
                            reload(step, bb)
                    if step[0] == "k" and step[2] % 2 == 1:
                        g, h = step[1], step[2] // 2
                        u = g % 2
                        sp.wait_ge(k_lo_out, b * NG * NKB + NKB * g + 2 * h + 2)
                        if (g, h) == (0, 0) and steps is at_end:
                            sp.wait_ge(tr, NB * NKT)
                            self_weight_in(0)
                            self_weight_in(1)
                        if (g, h) == (0, 0):
                            sp.wait_ge(placed, PLACED)
                            sp.wait_ge(mask_rows_out, 32)
                            for w in range(2):
                                sp.dma_start(t.k_stack[w][SHIFT_ROW:ROWS, :, :],
                                             io.mask_rows[bass.ds(b, 1), :, :].rearrange("o r k -> (o r) k"
                                             ).unsqueeze(1).broadcast_to([2, HPG, KEYS])).then_inc(mask_in, 16)
                        for j in range(HPG):
                            for k, part in enumerate((k_hi[h], k_hi[h], k_lo[h])):
                                sp.dma_start(t.k_stack[u][HD * k:HD * (k + 1), j, 2 * KB * h:2 * KB * (h + 1)],
                                             part[HD * j:HD * (j + 1), :]).then_inc(k_in[u][h], 16)

            with sp.Fori(0, NB - 1) as b:
                one_batch(b, in_loop)
            one_batch(NB - 1, at_end)
            for i in (2, 3):
                sp.wait_ge(s.self_lo, NC * (i - 1))
                self_weight_in(i)

        @block.gpsimd
        def _(pool):
            def deviations(n, b):
                two = slice(2 * (n % 2), 2 * (n % 2) + 2)
                pool.wait_ge(var_dve, b * (NKT // 2) + n + 1)
                for k, (x, y, op) in enumerate(((mv[:, two, 1], t.eps[:, 0:2], ALU.add),
                                                (rstd[:, two], t.inv_scale2[:, 0:2], ALU.mult),
                                                (rstd[:, two], t.half_neg[:, 0:2], ALU.pow))):
                    nc.gpsimd.tensor_tensor(rstd[:, two], x, y, op).then_inc(pool_pow, 1)
                    pool.wait_ge(pool_pow, (b * (NKT // 2) + n) * 3 + k + 1)

            small = [(t.half_neg[:, :], -0.5), (t.eps[:, :], EPS), (t.inv_scale2[:, :], A_SCALE ** -2)]
            whole = small + [(t.ones32[:, :], 1.0), (mask_ones, 1.0), (t.q_stack[SHIFT_ROW:ROWS, :, :], 1.0),
                             (t.q_stack[SHIFT_ROW:SHIFT_ROW + 1, :, :], 0.0)]
            for n, (what, value) in enumerate(small):
                nc.gpsimd.memset(what, value).then_inc(const, 1)
                pool.wait_ge(const, n + 1)
            for k in range(2):
                pool.wait_ge(x_var, k + 1)
                nc.gpsimd.tensor_scalar(x_rstd[:, k, :], x_mv[:, k, :, 1], EPS, 1.0 if k == 0 else A_SCALE ** -2,
                                        ALU.add, ALU.mult).then_inc(x_pow, 1)
                pool.wait_ge(x_pow, 2 * k + 1)
                nc.gpsimd.tensor_tensor(x_rstd[:, k, :], x_rstd[:, k, :], t.half_neg[:, 0:NB],
                                        ALU.pow).then_inc(x_pow, 1)
                pool.wait_ge(x_pow, 2 * k + 2)
            deviations(0, 0)
            deviations(1, 0)
            for n in range(len(small), len(whole)):
                nc.gpsimd.memset(*whole[n]).then_inc(const, 1)
                pool.wait_ge(const, n + 1)
            deviations(2, 0)

            def one_batch(b, steps):
                n_add = 0
                for step in steps:
                    step, bb = of_batch(step, b)
                    if step[0] == "ln":
                        deviations(step[1], bb)
                    if step[0] == "xln":
                        self_deviations(nc, pool, t, s, 0)
                    if step == ("presum", NG - 1) or (step[0] == "sums" and step[1] < NG - 1):
                        g = step[1]
                        if g:
                            pool.wait_ge(dve_second, b * NG + g)
                        for p in range(1, POOL_ADDS[g] + 1):
                            pool.wait_ge(exp_done, b * NG * NPAIR + NPAIR * g + p + 1)
                            nc.gpsimd.tensor_tensor(acc_pool[:, :], pT[:, 0, :] if p == 1 else acc_pool[:, :],
                                                    pT[:, p % PT, :], ALU.add).then_inc(pool_add, 1)
                            n_add += 1
                            pool.wait_ge(pool_add, b * sum(POOL_ADDS) + n_add)

            with pool.Fori(0, NB - 1) as b:
                one_batch(b, in_loop)
            one_batch(NB - 1, at_end)

        @block.vector
        def _(v):
            def statistics(kt, b):
                v.wait_ge(raw_in[kt % RAW], (b * (NKT // RAW) + kt // RAW + 1) * 16)
                nc.vector.bn_stats(stats[:, kt % 4, :], raw[:, kt % RAW, :]).then_inc(stat_dve, 1)

            def variances(n, b):
                v.wait_ge(stat_dve, b * NKT + 2 * n + 2)
                nc.vector.memset(carrier[:, :], 0.0)
                for kt in (2 * n, 2 * n + 1):
                    last = nc.vector.bn_aggr(mv[:, kt % 4, :], stats[:, kt % 4, :])
                last.then_inc(var_dve, 1)

            def normalise(n, b):
                v.wait_ge(pool_pow, (b * (NKT // 2) + n + 1) * 3)
                for kt in (2 * n, 2 * n + 1):
                    if kt >= RAW:
                        v.wait_ge(tr, b * NKT + kt - RAW + 1)
                    nc.vector.tensor_scalar(xn[:, kt % RAW, :], raw[:, kt % RAW, :], mv[:, kt % 4, 0:1],
                                            rstd[:, kt % 4:kt % 4 + 1], ALU.subtract,
                                            ALU.mult).then_inc(normed, 1)

            def low_half(kt, b):
                if 2 <= kt < NKT - 2 and kt % 2 == 0:
                    statistics(kt + 2, b)
                    statistics(kt + 3, b)
                    variances(kt // 2 + 1, b)
                v.wait_ge(tr_hi, b * NKT + kt + 1)
                nc.vector.tensor_tensor(cT_lo[:, :, P * kt:P * (kt + 1)],
                                        t_bank(kt).rearrange("p (c n) -> p c n", c=NC),
                                        cT_hi[:, :, P * kt:P * (kt + 1)], ALU.subtract).then_inc(tr_lo, 1)

            def first_tiles(b):
                for n in AHEAD_LN:
                    statistics(2 * n, b)
                    statistics(2 * n + 1, b)
                    variances(n, b)
                for n in AHEAD_LN:
                    normalise(n, b)

            def low_weight(n):
                i, w, hi, lo = folded[n]
                v.wait_ge(w_hi, n + 1)
                for c in range(NC):
                    last = nc.vector.scalar_tensor_tensor(out=lo[:, c, :], in0=w[:, c, :],
                                                          scalar=gains[:, i, c:c + 1] if i < 3 else W_SCALE,
                                                          in1=hi[:, c, :], op0=ALU.mult, op1=ALU.subtract)
                last.then_inc(w_lo, 1)

            for k, src in enumerate((t.x, hat)):
                for b in range(NB):
                    if k == 0:
                        v.wait_ge(x_in[b], 16)
                    nc.vector.bn_stats(x_stats[:, b, :], src[:, b, :]).then_inc(x_st, 1)
                v.wait_ge(x_st, NB * (k + 1))
                for b in range(NB):
                    last = nc.vector.bn_aggr(x_mv[:, k, b, :], x_stats[:, b, :])
                last.then_inc(x_var, 1)
                if k == 0:
                    v.wait_ge(vec_in, 16)
                    for i in range(3):
                        nc.vector.tensor_scalar(gains[:, i, :], vectors[:, min(i, 1), :], W_SCALE, None,
                                                ALU.mult).then_inc(gains_done, 1)
                else:
                    v.wait_ge(gains_done, 3)
                    low_weight(0)
                v.wait_ge(x_var, k + 1)
                v.wait_ge(x_pow, 2 * k + 2)
                for b in range(NB):
                    nc.vector.tensor_scalar(hat[:, b, :], src[:, b, :], x_mv[:, k, b, 0:1],
                                            x_rstd[:, k, b:b + 1], ALU.subtract, ALU.mult).then_inc(x_normed, 1)
                v.wait_ge(x_normed, NB * (k + 1))
            for b in range(NB):
                v.wait_ge(x_tr_hi, b + 1)
                nc.vector.tensor_tensor(xT_lo[:, :, P * b:P * (b + 1)],
                                        t_bank(b).rearrange("p (c n) -> p c n", c=NC),
                                        xT_hi[:, :, P * b:P * (b + 1)], ALU.subtract).then_inc(x_tr_lo, 1)
            first_tiles(0)
            v.wait_ge(mask_u8_in, 16)
            nc.vector.tensor_scalar(mask_neg, mask_u8[:, :], 1.0, -MASKED, ALU.subtract, ALU.mult).then_inc(mask_done, 1)
            low_weight(1)
            for g in range(NG):
                if g == 2:
                    v.wait_ge(bo_in, 16)
                    for b in range(NB):
                        nc.vector.tensor_tensor(t.x[:, b, :], t.x[:, b, :], bo_bc[:, :], ALU.add)
                v.wait_ge(q_hi_s, g + 1)
                nc.vector.tensor_tensor(q_lo[:, g, :], q_f[:, g % 2, :], q_hi[:, g, :],
                                        ALU.subtract).then_inc(q_lo_s, 1)
            for kt in AHEAD_T:
                low_half(kt, 0)
            normalise(2, 0)
            low_weight(2)
            low_weight(3)

            def one_batch(b, steps):
                n_p1 = 0
                for step in maxima_first(steps):
                    step, bb = of_batch(step, b)
                    kind = step[0]
                    if kind == "ln":
                        if bb is b or step[1] > AHEAD_LN[-1]:
                            normalise(step[1], bb)
                        elif step[1] == AHEAD_LN[-1]:
                            first_tiles(bb)
                    elif kind == "t":
                        low_half(step[1], bb)
                    elif kind == "k":
                        g, kb = step[1:]
                        n = NKB * g + kb
                        h, half = kb // 2, slice(KB * (kb % 2), KB * (kb % 2 + 1))
                        v.wait_ge(k_hi_out, b * NG * NKB + n + 1)
                        nc.vector.tensor_tensor(k_lo[h][:, half], k_f[:, kb % 2, :], k_hi[h][:, half],
                                                ALU.subtract).then_inc(k_lo_out, 1)
                    elif kind == "p1":
                        g, j, kb = step[1:]
                        n_p1 += 1
                        n = n_p1
                        v.wait_ge(p1_mm, b * PER_BATCH["p1"] + n)
                        nc.vector.tensor_reduce(mpart[:, j, kb:kb + 1], p1_bank(step, n - 1), AX.X,
                                                ALU.max).then_inc(p1_max, 1)
                        if (j, kb) == (HPG - 1, NKB - 1):
                            v.wait_ge(p1_max, b * PER_BATCH["p1"] + n)
                            nc.vector.tensor_reduce(mgroup[:, g % 2, :], mpart[:, :, :], AX.X,
                                                    ALU.max).then_inc(m_max, 1)
                    elif kind in ("presum", "sums"):
                        g = step[1]
                        p = POOL_ADDS[g] + 1
                        if kind == "presum" or g < NG - 1:
                            v.wait_ge(exp_done, b * NG * NPAIR + NPAIR * g + p + 2)
                            nc.vector.tensor_tensor(acc_dve[:, :], pT[:, p % PT, :], pT[:, (p + 1) % PT, :],
                                                    ALU.add).then_inc(dve_first, 1)
                        if kind == "presum":
                            continue
                        v.wait_ge(dve_first, b * NG + g + 1)
                        if p + 2 < NPAIR:
                            v.wait_ge(exp_done, b * NG * NPAIR + NPAIR * (g + 1))
                            nc.vector.tensor_tensor(acc_dve[:, :], acc_dve[:, :], pT[:, (p + 2) % PT, :],
                                                    ALU.add).then_inc(dve_third, 1)
                            v.wait_ge(dve_third, b + 1)
                        v.wait_ge(pool_add, b * sum(POOL_ADDS) + sum(POOL_ADDS[:g + 1]))
                        nc.vector.tensor_tensor(acc_dve[:, :], acc_dve[:, :], acc_pool[:, :],
                                                ALU.add).then_inc(dve_second, 1)
                        v.wait_ge(dve_second, b * NG + g + 1)
                        if g:
                            v.wait_ge(den_mm, b * NG + g)
                        nc.vector.tensor_tensor(acc[:, :], acc_dve[:, 0:KB], acc_dve[:, KB:2 * KB],
                                                ALU.add).then_inc(sums_done, 1)
                    elif kind == "den":
                        g = step[1]
                        v.wait_ge(den_mm, b * NG + g + 1)
                        nc.vector.reciprocal(rden[:, :], ps_o[g % 2][:, P:2 * P]).then_inc(rden_done, 1)
                        v.wait_ge(rden_done, b * NG + g + 1)
                        nc.vector.tensor_tensor(oT[:, g, :], ps_o[g % 2][:, 0:P], rden[:, :],
                                                ALU.mult).then_inc(norm_out, 1)
                        v.wait_ge(norm_out, b * NG + g + 1)
                        nc.vector.tensor_scalar(oT[:, g, :], oT[:, g, :], vbias[:, g:g + 1], A_SCALE,
                                                ALU.add, ALU.mult).then_inc(fin, 1)
                        v.wait_ge(split_hi, b * NG + g + 1)
                        nc.vector.tensor_tensor(oT_lo[:, g, :], oT[:, g, :], oT_hi[:, g, :],
                                                ALU.subtract).then_inc(split_lo, 1)
                    elif kind == "op":
                        v.wait_ge(op_mm, b + 1)
                        here = t.x[:, bass.ds(b, 1), :].rearrange("p o c -> p (o c)")
                        nc.vector.scalar_tensor_tensor(out=here, in0=ps_s[0][:, KB:2 * KB], scalar=UNSCALE, in1=here,
                                                       op0=ALU.mult, op1=ALU.add).then_inc(x_done, 1)
                    elif kind == "xln":
                        for b_ in range(NB - 1):
                            nc.vector.bn_stats(t.a_stats[:, b_, :], t.x[:, b_, :]).then_inc(s.a_st, 1)
                        v.wait_ge(s.a_st, NB - 1)
                        for b_ in range(NB - 1):
                            last = nc.vector.bn_aggr(t.a_mv[:, b_, :], t.a_stats[:, b_, :])
                        last.then_inc(s.a_var, 1)
                    elif kind == "spl":
                        n = step[1]
                        v.wait_ge(s.self_hi, n + 1)
                        nc.vector.scalar_tensor_tensor(out=self_weight(n, "lo"), in0=self_weight(n, "raw"),
                                                       scalar=W_SCALE, in1=self_weight(n, "hi"), op0=ALU.mult,
                                                       op1=ALU.subtract).then_inc(s.self_lo, 1)

            with v.Fori(0, NB - 1) as b:
                one_batch(b, in_loop)
            one_batch(NB - 1, at_end)

        @block.scalar
        def _(act):
            def high_half(kt, b):
                act.wait_ge(tr, b * NKT + kt + 1)
                nc.scalar.activation(cT_hi[:, :, P * kt:P * (kt + 1)],
                                     t_bank(kt).rearrange("p (c n) -> p c n", c=NC),
                                     ACT.Copy).then_inc(tr_hi, 1)

            def values_out(kt, b):
                act.wait_ge(v_mm, b * NKT + kt + 1)
                nc.scalar.activation(vals[:, kt, :], ps_r[ring_place(("v", kt)) % 2][:, :], ACT.Copy,
                                     scale=UNSCALE).then_inc(v_out, 1)

            def high_weight(n):
                i, w, hi, lo = folded[n]
                act.wait_ge(w_in[i], 16)
                for c in range(NC):
                    last = nc.scalar.activation(hi[:, c, :], w[:, c, :], ACT.Copy,
                                                scale=gains[:, i, c:c + 1] if i < 3 else W_SCALE)
                last.then_inc(w_hi, 1)

            def bias_columns_out(i, n):
                act.wait_ge(bias_mm, n)
                bank, at = bias_bank(i)
                nc.scalar.activation((qbias, kbias, vbias)[i][:, :], bank[:, at:at + NG], ACT.Copy).then_inc(bias_out, 1)
                act.wait_ge(bias_out, n)

            act.wait_ge(gains_done, 3)
            high_weight(0)
            for b in range(NB):
                act.wait_ge(x_tr, b + 1)
                nc.scalar.activation(xT_hi[:, :, P * b:P * (b + 1)],
                                     t_bank(b).rearrange("p (c n) -> p c n", c=NC),
                                     ACT.Copy).then_inc(x_tr_hi, 1)
            high_weight(1)
            bias_columns_out(0, 1)
            high_weight(2)
            for g in range(NG):
                act.wait_ge(q_mm, g + 1)
                if g >= 2:
                    act.wait_ge(q_lo_s, g - 1)
                nc.scalar.activation(q_f[:, g % 2, :], ps_o[g % 2][:, :], ACT.Identity, bias=qbias[:, g:g + 1],
                                     scale=UNSCALE).then_inc(q_out, 1)
                act.wait_ge(q_out, g + 1)
                nc.scalar.activation(q_hi[:, g, :], q_f[:, g % 2, :], ACT.Copy).then_inc(q_hi_s, 1)
            for kt in AHEAD_T:
                high_half(kt, 0)
            bias_columns_out(2, 2)
            high_weight(3)
            for kt in AHEAD_V:
                values_out(kt, 0)
            bias_columns_out(1, 3)

            def one_batch(b, steps):
                def exp(g, p):
                    n = NPAIR * g + p
                    act.wait_ge(s_mm, b * NG * NPAIR + n + 1)
                    if n >= PT:
                        act.wait_ge(av_mm, b * NG * NPAIR + n - PT + 1)
                        q = (n - PT) % NPAIR
                        before = (n - PT) // NPAIR
                        if q < 6:
                            act.wait_ge(pool_add, b * sum(POOL_ADDS) + sum(POOL_ADDS[:before]) + max(q, 1))
                        else:
                            act.wait_ge(dve_first, b * NG + before + 1)
                    nc.scalar.activation(pT[:, p % PT, :], ps_s[p % 2][:, :], ACT.Exp,
                                         scale=SM_SCALE).then_inc(exp_done, 1)

                for step in steps:
                    step, bb = of_batch(step, b)
                    kind = step[0]
                    if kind == "t":
                        high_half(step[1], bb)
                    elif kind == "v" and step[2] == NC - 1:
                        values_out(step[1], bb)
                    elif kind == "k":
                        g, kb = step[1:]
                        n = NKB * g + kb
                        h, half = kb // 2, slice(KB * (kb % 2), KB * (kb % 2 + 1))
                        act.wait_ge(k_mm, b * NG * NKB + n + 1)
                        if n >= 2:
                            act.wait_ge(k_lo_out, b * NG * NKB + n - 1)
                        nc.scalar.activation(k_f[:, kb % 2, :], ps_r[ring_place(step) % 2][:, :], ACT.Identity,
                                             bias=kbias[:, g:g + 1], scale=UNSCALE).then_inc(k_f_out, 1)
                        act.wait_ge(k_f_out, b * NG * NKB + n + 1)
                        if g:
                            act.wait_ge(k_in[(g - 1) % 2][h], (b * 2 + (g - 1) // 2 + 1) * KIN)
                        nc.scalar.activation(k_hi[h][:, half], k_f[:, kb % 2, :], ACT.Copy).then_inc(k_hi_out, 1)
                    elif kind == "mt":
                        g = step[1]
                        act.wait_ge(mt_mm, b * NG + g + 1)
                        nc.scalar.activation(
                            t.q_stack[SHIFT_ROW:SHIFT_ROW + 1, HPG * g:HPG * (g + 1), bass.ds(b * P, P)],
                            ps_s[0][SHIFT_ROW:SHIFT_ROW + 1, 0:KB].rearrange("o (j n) -> o j n", j=HPG),
                            ACT.Copy, scale=-1.0).then_inc(m_row, 1)
                    elif kind == "s" and step[3] == 1:
                        exp(*step[1:3])
                    elif kind == "den":
                        g = step[1]
                        act.wait_ge(fin, b * NG + g + 1)
                        nc.scalar.activation(oT_hi[:, g, :], oT[:, g, :], ACT.Copy).then_inc(split_hi, 1)
                    elif kind == "spl":
                        n = step[1]
                        act.wait_ge(self_in[n // NC], 16)
                        nc.scalar.activation(self_weight(n, "hi"), self_weight(n, "raw"), ACT.Copy,
                                             scale=W_SCALE).then_inc(s.self_hi, 1)

            with act.Fori(0, NB - 1) as b:
                one_batch(b, in_loop)
            one_batch(NB - 1, at_end)

        @block.tensor
        def _(pe):
            def transposes(kt, b):
                pe.wait_ge(normed, b * NKT + kt + 1)
                if kt >= 4:
                    pe.wait_ge(tr_lo, b * NKT + kt - 3)
                for c in range(NC):
                    last = nc.tensor.transpose(t_bank(kt)[:, P * c:P * (c + 1)],
                                               xn[:, kt % RAW, P * c:P * (c + 1)], t.ident[:, :])
                last.then_inc(tr, 1)

            released = {"v": v_out, "k": k_f_out, "p1": p1_max}

            def ring_bank(step, b):
                n = ring_place(step)
                kind = ring[n - 2][0]
                if n >= 2:
                    before = sum(r[0] == kind for r in ring[:n - 1]) + (HPG * NKB if kind == "p1" else 0)
                    pe.wait_ge(released[kind], b * PER_BATCH[kind] + before)
                return ps_r[n % 2]

            def values_quarter(kt, c, b):
                if c == 0:
                    ring_bank(("v", kt), b)
                    pe.wait_ge(tr_lo, b * NKT + kt + 1)
                bank, keys = ps_r[ring_place(("v", kt)) % 2], slice(P * kt, P * (kt + 1))
                nc.tensor.matmul(bank[:, :], cT_hi[:, c, keys], t.wv_hi[:, c, :], start=(c == 0), stop=False)
                nc.tensor.matmul(bank[:, :], cT_hi[:, c, keys], t.wv_lo[:, c, :], start=False, stop=False)
                last = nc.tensor.matmul(bank[:, :], cT_lo[:, c, keys], t.wv_hi[:, c, :], start=False,
                                        stop=(c == NC - 1))
                if c == NC - 1:
                    last.then_inc(v_mm, 1)

            def bias_columns(i):
                pe.wait_ge(w_in[i], 16)
                bank, at = bias_bank(i)
                for g in range(NG):
                    for c in range(NC):
                        last = nc.tensor.matmul(bank[:, at + g:at + g + 1],
                                                w_raw[i][:, c, P * g:P * (g + 1)],
                                                vectors[:, 2 + min(i, 1), c:c + 1], start=(c == 0), stop=(c == NC - 1))
                last.then_inc(bias_mm, 1)

            pe.wait_ge(vec_in, 16)
            bias_columns(0)
            pe.wait_ge(ident_in, 16)
            for b in range(NB):
                pe.wait_ge(x_normed, NB + b + 1)
                for c in range(NC):
                    last = nc.tensor.transpose(t_bank(b)[:, P * c:P * (c + 1)], hat[:, b, P * c:P * (c + 1)],
                                               t.ident[:, :])
                last.then_inc(x_tr, 1)
            pe.wait_ge(w_lo, 1)
            pe.wait_ge(x_tr_lo, NB)
            for g in range(NG):
                if g >= 2:
                    pe.wait_ge(q_out, g - 1)
                col = slice(P * g, P * (g + 1))
                for c in range(NC):
                    nc.tensor.matmul(ps_o[g % 2][:, :], wq_hi[:, c, col], xT_hi[:, c, :], start=(c == 0), stop=False)
                    nc.tensor.matmul(ps_o[g % 2][:, :], wq_hi[:, c, col], xT_lo[:, c, :], start=False, stop=False)
                    last = nc.tensor.matmul(ps_o[g % 2][:, :], wq_lo[:, c, col], xT_hi[:, c, :], start=False,
                                            stop=(c == NC - 1))
                last.then_inc(q_mm, 1)
            for kt in AHEAD_T:
                transposes(kt, 0)
            bias_columns(2)
            pe.wait_ge(w_lo, 2)
            for kt in AHEAD_V:
                if kt == 1:
                    pe.wait_ge(bias_out, 2)
                for c in range(NC):
                    values_quarter(kt, c, 0)
            pe.wait_ge(q_out, NG)
            bias_columns(1)

            def one_batch(b, steps):
                n_p1 = 0
                for step in steps:
                    step, bb = of_batch(step, b)
                    kind = step[0]
                    if kind == "t":
                        transposes(step[1], bb)
                    elif kind == "v":
                        kt, c = step[1:]
                        values_quarter(kt, c, bb)
                    elif kind == "k":
                        g, kb = step[1:]
                        bank = ring_bank(step, b)
                        if kb == 0:
                            pe.wait_ge(tr_lo, b * NKT + NKT)
                            pe.wait_ge(w_lo, 4)
                        col, keys = slice(P * g, P * (g + 1)), slice(KB * kb, KB * (kb + 1))
                        for c in range(NC):
                            nc.tensor.matmul(bank[:, :], t.wk_hi[:, c, col], cT_hi[:, c, keys], start=(c == 0), stop=False)
                            nc.tensor.matmul(bank[:, :], t.wk_hi[:, c, col], cT_lo[:, c, keys], start=False, stop=False)
                            last = nc.tensor.matmul(bank[:, :], t.wk_lo[:, c, col], cT_hi[:, c, keys], start=False,
                                                    stop=(c == NC - 1))
                        last.then_inc(k_mm, 1)
                    elif kind == "p1":
                        g, j, kb = step[1:]
                        if g:
                            ring_bank(step, b)
                        elif n_p1 >= 4:
                            pe.wait_ge(p1_max, b * PER_BATCH["p1"] + n_p1 - 3)
                        bank = p1_bank(step, n_p1)
                        n_p1 += 1
                        if (g, j, kb) == (0, 0, 0):
                            pe.wait_ge(mask_in, (b + 1) * 16 * 2)
                            pe.wait_ge(placed, PLACED)
                            pe.wait_ge(const, CONSTS + 2)
                        if j == 0 and kb % 2 == 0:
                            pe.wait_ge(k_in[g % 2][kb // 2], (b * 2 + g // 2 + 1) * KIN)
                        nc.tensor.matmul(bank, t.q_stack[0:ROWS, HPG * g + j, bass.ds(b * P, P)],
                                         t.k_stack[g % 2][0:ROWS, j, KB * kb:KB * (kb + 1)],
                                         start=True, stop=True).then_inc(p1_mm, 1)
                    elif kind == "mt":
                        g = step[1]
                        bank = ps_s[0]
                        pe.wait_ge(m_max, b * NG + g + 1)
                        for j in range(HPG):
                            last = nc.tensor.matmul(bank[SHIFT_ROW:SHIFT_ROW + 1, P * j:P * (j + 1)],
                                                    mgroup[:, g % 2, j:j + 1], t.ident[:, :], start=True, stop=True)
                        last.then_inc(mt_mm, 1)
                    elif kind == "s":
                        g, p, i = step[1:]
                        n = NPAIR * g + p
                        if n >= 2 and i == 0:
                            pe.wait_ge(exp_done, b * NG * NPAIR + n - 1)
                        if p == 0 and i == 0:
                            pe.wait_ge(m_row, b * NG + g + 1)
                        for j in range(HPG):
                            at = KB * i + P * j
                            kt = 2 * p + i
                            last = nc.tensor.matmul(ps_s[p % 2][:, at:at + P],
                                                    t.k_stack[g % 2][0:ROWS, j, P * kt:P * (kt + 1)],
                                                    t.q_stack[0:ROWS, HPG * g + j, bass.ds(b * P, P)],
                                                    start=True, stop=True)
                        if i == 1:
                            last.then_inc(s_mm, 1)
                    elif kind == "av":
                        g, p, i = step[1:]
                        if i == 0:
                            pe.wait_ge(exp_done, b * NG * NPAIR + NPAIR * g + p + 1)
                            if g >= 2 and p == 0:
                                pe.wait_ge(fin, b * NG + g - 1)
                        for j in range(HPG):
                            at = KB * i + P * j
                            head = HD * (HPG * g + j)
                            last = nc.tensor.matmul(ps_o[g % 2][HD * j:HD * (j + 1), 0:P],
                                                    vals[:, 2 * p + i, head:head + HD],
                                                    pT[:, p % PT, at:at + P], start=(p == 0 and i == 0),
                                                    stop=(p == NPAIR - 1 and i == 1))
                        if i == 1:
                            last.then_inc(av_mm, 1)
                    elif kind == "den":
                        g = step[1]
                        pe.wait_ge(sums_done, b * NG + g + 1)
                        for j in range(HPG):
                            last = nc.tensor.matmul(ps_o[g % 2][HD * j:HD * (j + 1), P:2 * P], t.ones32[:, :],
                                                    acc[:, P * j:P * (j + 1)], start=True, stop=True)
                        last.then_inc(den_mm, 1)
                    elif kind == "op":
                        if steps is in_loop:
                            pe.wait_ge(tr_lo, (b + 1) * NKT + 3)
                        to = ps_s[0][:, KB:2 * KB]
                        for g in range(NG):
                            pe.wait_ge(split_lo, b * NG + g + 1)
                            nc.tensor.matmul(to, oT_hi[:, g, :], wo_hi[:, g, :], start=(g == 0), stop=False)
                            nc.tensor.matmul(to, oT_hi[:, g, :], wo_lo[:, g, :], start=False, stop=False)
                            last = nc.tensor.matmul(to, oT_lo[:, g, :], wo_hi[:, g, :], start=False,
                                                    stop=(g == NG - 1))
                        last.then_inc(op_mm, 1)

            with pe.Fori(0, NB - 1) as b:
                one_batch(b, in_loop)
            one_batch(NB - 1, at_end)


def w1_part(n):
    return slice(n // 2, n // 2 + 1), slice(FF // 2 * (n % 2), FF // 2 * (n % 2 + 1))


def self_attention(nc, io, t, s):
    with ExitStack() as ctx:
        def sb(name, shape, dt=F32):
            return ctx.enter_context(nc.sbuf_tensor(name, shape, dt))

        def sem(name):
            return ctx.enter_context(nc.semaphore(name))

        w_hi = [t.cT_hi[:, :, D * i:D * (i + 1)] for i in range(4)]
        w_lo = [t.cT_lo[:, :, D * i:D * (i + 1)] for i in range(4)]
        bias = sb("a_bias", [P, 4, D])
        rope = sb("a_rope", [P, 2, HD])
        stats, mv, rstd = t.a_stats, t.a_mv, t.a_rstd
        hat = sb("a_hat", [P, NB, D])
        xT_hi, xT_lo = sb("a_xT_hi", [P, 2, NC, P], F16), sb("a_xT_lo", [P, 2, NC, P], F16)
        qk = sb("a_qk", [P, 2, D])
        vals = sb("a_vals", [P, 3, D])
        rot, cosed = sb("a_rot", [P, 2, D]), sb("a_cosed", [P, 2, D])
        qkT = sb("a_qkT", [P, 2, NG, P])
        m, rsum, rinv = sb("a_m", [P, HEADS]), sb("a_rsum", [P, HEADS]), sb("a_rinv", [P, HEADS])
        prob = sb("a_prob", [P, 2, HEADS, P])
        probT = sb("a_probT", [P, HEADS, P])
        oT_hi, oT_lo = sb("a_oT_hi", [P, NG, P], F16), sb("a_oT_lo", [P, NG, P], F16)
        y = sb("a_y", [P, D])
        m_stats, m_mv, m_rstd = sb("am_stats", [P, 2, 6]), sb("am_mv", [P, 2, 2]), sb("am_rstd", [P, 2])
        m_hat, gT = sb("am_hat", [P, 2, D]), sb("am_gT", [P, NC, P])
        ps_p = ctx.enter_context(nc.psum_tensor("a_psp", [P, HEADS, P], F32))
        ps_t = [ctx.enter_context(nc.psum_tensor(f"a_pst{i}", [P, HPG, P], F32)) for i in range(2)]
        ps_r = [ctx.enter_context(nc.psum_tensor(f"a_psr{i}", [P, D], F32)) for i in range(2)]

        misc_in = sem("a_misc_in")
        normed = sem("a_normed")
        tr, tr_hi, tr_lo = sem("a_tr"), sem("a_tr_hi"), sem("a_tr_lo")
        mm, biased = sem("a_mm"), sem("a_biased")
        cos_done, rot_done, roped = sem("a_cos"), sem("a_rot_s"), sem("a_roped")
        qk_tr, qk_tr_out = sem("a_qk_tr"), sem("a_qk_tr_out")
        scored, maxed, exped, inv, scaled = sem("a_scored"), sem("a_maxed"), sem("a_exped"), sem("a_inv"), sem("a_scaled")
        p_tr, p_out_act, p_out_dve = sem("a_p_tr"), sem("a_p_out_act"), sem("a_p_out_dve")
        o_mm, o_hi, o_lo = sem("a_o_mm"), sem("a_o_hi"), sem("a_o_lo")
        y_mm, y_out, x_done = sem("a_y_mm"), sem("a_y_out"), sem("a_x_done")

        m_st, m_var, m_powed, m_normed = sem("am_st"), sem("am_var"), sem("am_pow"), sem("am_normed")
        m_tr, m_tr_hi, m_tr_lo = sem("am_tr"), sem("am_tr_hi"), sem("am_tr_lo")
        g_tr, g_out, g_mm, logits_out = sem("am_g_tr"), sem("am_g_out"), sem("am_g_mm"), sem("am_logits")

        def slot(h):
            return NG * (h % HPG) + h // HPG

        def stages(step):
            return [step - k if 0 <= step - k < NB else None for k in range(4)]

        STEPS = range(NB + 2)

        def tail(step):
            return step == NB + 1

        ring = [("x", 0, tr_lo, 1)]
        for step in STEPS:
            a, b, c, d = stages(step)
            if b is not None:
                ring += [("qT", b, qk_tr_out, 2 * b + 1), ("kT", b, qk_tr_out, 2 * b + 2)]
            if a is not None:
                ring += [("q", a, biased, 3 * a + 1), ("k", a, biased, 3 * a + 2)]
            mx = [("mx", d, m_tr_lo, d + 1)] if d is not None else []
            if not tail(step):
                ring += mx
            if c is not None:
                ring += [("o", c, o_lo, c + 1)]
            if tail(step):
                ring += mx
            if a is not None:
                ring += [("v", a, biased, 3 * a + 3)]
            if a is not None and a + 1 < NB:
                ring += [("x", a + 1, tr_lo, a + 2)]
            if d is not None:
                ring += [("mg", d, g_out, d + 1)]
            if c is not None:
                ring += [("y", c, y_out, c + 1)]
            if d is not None:
                ring += [("gate", d, logits_out, d + 1)]
        place = {user[:2]: n for n, user in enumerate(ring)}

        def bank(kind, b):
            return ps_r[place[kind, b] % 2]

        block = ctx.enter_context(nc.Block())

        @block.sync
        def _(sp):
            sp.dma_start(rope[:, :, :], io.rope).then_inc(misc_in, 16)
            for k, v in enumerate((io.a_bq, io.a_bk, io.a_bv, io.a_bo)):
                sp.dma_start(bias[:, k, :], v.partition_broadcast(P)).then_inc(misc_in, 16)
            sp.dma_start(t.affine[:, :, :], io.affine).then_inc(s.gate_in, 16)
            sp.dma_start(t.gate[:, :, :], io.gate).then_inc(s.gate_in, 16)
            sp.dma_start(t.w1_raw[:, :, :], io.w1[0:1, :, :, :].rearrange("e p c n -> (e p) c n")).then_inc(s.w1_in, 16)
            sp.dma_start(t.w2_raw[:, :, :], io.w2[0:1, :, :, :].rearrange("e p c n -> (e p) c n")).then_inc(s.w2_in, 16)

        @block.gpsimd
        def _(pool):
            self_deviations(nc, pool, t, s, 1)
            pool.wait_ge(misc_in, 16 * 5)

            def mixture_deviations(d, k):
                n = 2 * d + k
                pool.wait_ge(m_var, n + 1)
                nc.gpsimd.tensor_tensor(m_rstd[:, k:k + 1], m_mv[:, k, 1:2], t.eps[:, 0:1], ALU.add).then_inc(m_powed, 1)
                pool.wait_ge(m_powed, 2 * n + 1)
                nc.gpsimd.tensor_tensor(m_rstd[:, k:k + 1], m_rstd[:, k:k + 1], t.half_neg[:, 0:1],
                                        ALU.pow).then_inc(m_powed, 1)
                pool.wait_ge(m_powed, 2 * n + 2)

            for step in STEPS:
                b, _, c, d = stages(step)
                if d is not None:
                    mixture_deviations(d, 1)
                for i in range(2 if b is not None else 0):
                    n = 2 * b + i
                    src = qk[:, i, :].rearrange("p (h k) -> p h k", k=HD)
                    dst = rot[:, i, :].rearrange("p (h k) -> p h k", k=HD)
                    pool.wait_ge(biased, 3 * b + i + 1)
                    if n >= 2:
                        pool.wait_ge(roped, n - 1)
                    for half in range(2):
                        here, there = slice(HD // 2 * half, HD // 2 * (half + 1)), slice(HD // 2 * (1 - half), HD // 2 * (2 - half))
                        sines = rope[:, 1:2, here].broadcast_to([P, HEADS, HD // 2])
                        nc.gpsimd.tensor_tensor(dst[:, :, here], src[:, :, there], sines,
                                                ALU.mult).then_inc(rot_done, 1)
                        pool.wait_ge(rot_done, 2 * n + half + 1)
                if c is not None and c + 1 < NB:
                    mixture_deviations(c, 0)

        @block.vector
        def _(v):
            def normalise(b):
                v.wait_ge(s.a_powed, 3 if b < NB - 1 else 6)
                nc.vector.tensor_scalar(hat[:, b, :], t.x[:, b, :], mv[:, b, 0:1], rstd[:, b:b + 1],
                                        ALU.subtract, ALU.mult).then_inc(normed, 1)

            normalise(0)
            nc.vector.bn_stats(stats[:, NB - 1, :], t.x[:, NB - 1, :]).then_inc(s.a_st, 1)
            v.wait_ge(s.a_st, NB)
            nc.vector.bn_aggr(mv[:, NB - 1, :], stats[:, NB - 1, :]).then_inc(s.a_var, 1)

            def project_out(i, b):
                dst = vals[:, b % 3, :] if i == 2 else qk[:, i, :]
                v.wait_ge(mm, 3 * b + i + 1)
                nc.vector.scalar_tensor_tensor(out=dst, in0=bank("qkv"[i], b)[:, :], scalar=UNSCALE,
                                               in1=bias[:, i, :], op0=ALU.mult, op1=ALU.add).then_inc(biased, 1)
                if i < 2:
                    v.wait_ge(biased, 3 * b + i + 1)
                    nc.vector.tensor_tensor(cosed[:, i, :].rearrange("p (h k) -> p h k", k=HD),
                                            dst.rearrange("p (h k) -> p h k", k=HD),
                                            rope[:, 0:1, :].broadcast_to([P, HEADS, HD]), ALU.mult).then_inc(cos_done, 1)

            def rope_out(i, b):
                n = 2 * b + i
                v.wait_ge(cos_done, n + 1)
                v.wait_ge(rot_done, 2 * n + 2)
                nc.vector.tensor_tensor(qk[:, i, :], cosed[:, i, :], rot[:, i, :], ALU.add).then_inc(roped, 1)

            def x_low(b):
                v.wait_ge(tr_hi, b + 1)
                nc.vector.tensor_tensor(xT_lo[:, b % 2, :, :], bank("x", b)[:, :].rearrange("p (c n) -> p c n", c=NC),
                                        xT_hi[:, b % 2, :, :], ALU.subtract).then_inc(tr_lo, 1)

            def mixture_variance(src, d, k):
                n = 2 * d + k
                nc.vector.bn_stats(m_stats[:, k, :], src).then_inc(m_st, 1)
                v.wait_ge(m_st, n + 1)
                nc.vector.bn_aggr(m_mv[:, k, :], m_stats[:, k, :]).then_inc(m_var, 1)

            def mixture_normalise(src, d, k):
                n = 2 * d + k
                v.wait_ge(m_powed, 2 * n + 2)
                if d:
                    v.wait_ge((m_tr, g_tr)[k], d)
                nc.vector.tensor_scalar(m_hat[:, k, :], src, m_mv[:, k, 0:1], m_rstd[:, k:k + 1], ALU.subtract,
                                        ALU.mult).then_inc(m_normed, 1)

            def split_w1(n):
                c, half = w1_part(n)
                v.wait_ge(s.w1_hi, n + 1)
                nc.vector.scalar_tensor_tensor(out=t.w1_lo[:, c, half].rearrange("p c n -> p (c n)"),
                                               in0=t.w1_raw[:, c, half].rearrange("p c n -> p (c n)"), scalar=W_SCALE,
                                               in1=t.w1_hi[:, c, half].rearrange("p c n -> p (c n)"), op0=ALU.mult,
                                               op1=ALU.subtract).then_inc(s.w1_lo, 1)

            def mixture_input(d):
                mixture_normalise(t.x[:, d, :], d, 0)
                v.wait_ge(m_normed, 2 * d + 1)
                mixture_variance(m_hat[:, 0, :], d, 1)

            def mixture_low(d):
                v.wait_ge(m_tr_hi, d + 1)
                nc.vector.scalar_tensor_tensor(out=t.xT_lo[:, :, P * d:P * (d + 1)],
                                               in0=bank("mx", d)[:, :].rearrange("p (c n) -> p c n", c=NC),
                                               scalar=A_SCALE, in1=t.xT_hi[:, :, P * d:P * (d + 1)], op0=ALU.mult,
                                               op1=ALU.subtract).then_inc(m_tr_lo, 1)

            def scale(b):
                for half in range(2):
                    n, heads = 2 * b + half, slice(HEADS // 2 * half, HEADS // 2 * (half + 1))
                    v.wait_ge(exped, n + 1)
                    nc.vector.reciprocal(rinv[:, heads], rsum[:, heads]).then_inc(inv, 1)
                    v.wait_ge(inv, n + 1)
                    nc.vector.tensor_tensor(prob[:, b % 2, heads, :], prob[:, b % 2, heads, :],
                                            rinv[:, heads].unsqueeze(2).broadcast_to([P, HEADS // 2, P]),
                                            ALU.mult).then_inc(scaled, 1)

            x_low(0)
            for b in range(1, NB):
                normalise(b)
            v.wait_ge(misc_in, 16 * 5)
            for step in STEPS:
                a, b, c, d = stages(step)
                if d is not None and not tail(step):
                    mixture_input(d)
                if step == NB:
                    for n in range(NF // 2, NF):
                        split_w1(n)
                if a is not None:
                    project_out(0, a)
                if b is not None:
                    v.wait_ge(scored, b + 1)
                    nc.vector.tensor_reduce(m[:, :], ps_p[:, :, :], AX.X, ALU.max).then_inc(maxed, 1)
                    v.wait_ge(maxed, 2 * b + 1)
                    nc.vector.tensor_scalar(m[:, :], m[:, :], -SM_SCALE, None, ALU.mult).then_inc(maxed, 1)
                if a is not None:
                    project_out(1, a)
                if d is not None and not tail(step):
                    mixture_low(d)
                if c is not None:
                    for n in (1, 3):
                        v.wait_ge(p_tr, 4 * c + n + 1)
                        nc.vector.tensor_copy(probT[:, HPG * n:HPG * (n + 1), :], ps_t[n % 2][:, :, :]).then_inc(p_out_dve, 1)
                if d is not None and tail(step):
                    mixture_input(d)
                if a is not None:
                    rope_out(0, a)
                if c is not None:
                    v.wait_ge(o_hi, c + 1)
                    nc.vector.scalar_tensor_tensor(out=oT_lo[:, :, :], in0=bank("o", c)[:, :].rearrange("p (g n) -> p g n", g=NG),
                                                   scalar=A_SCALE, in1=oT_hi[:, :, :], op0=ALU.mult,
                                                   op1=ALU.subtract).then_inc(o_lo, 1)
                if d is not None:
                    if tail(step):
                        mixture_low(d)
                    mixture_normalise(m_hat[:, 0, :], d, 1)
                if b is not None and a is None:
                    scale(b)
                if a is not None:
                    rope_out(1, a)
                    project_out(2, a)
                    if a + 1 < NB:
                        x_low(a + 1)
                if c is not None:
                    v.wait_ge(y_mm, c + 1)
                    nc.vector.scalar_tensor_tensor(out=y[:, :], in0=bank("y", c)[:, :], scalar=UNSCALE,
                                                   in1=bias[:, 3, :], op0=ALU.mult, op1=ALU.add).then_inc(y_out, 1)
                    v.wait_ge(y_out, c + 1)
                    nc.vector.tensor_tensor(t.x[:, c, :], t.x[:, c, :], y[:, :], ALU.add).then_inc(x_done, 1)
                    if c + 1 < NB:
                        v.wait_ge(x_done, c + 1)
                        mixture_variance(t.x[:, c, :], c, 0)
                if d is not None:
                    v.wait_ge(g_mm, d + 1)
                    nc.vector.tensor_copy(t.logits[:, d, :], bank("gate", d)[:, 0:EXPERTS]).then_inc(logits_out, 1)
                if b is not None and a is not None:
                    scale(b)
                if step == NB - 1:
                    for n in range(NF // 2):
                        split_w1(n)

        @block.scalar
        def _(act):
            def x_high(b):
                act.wait_ge(tr, b + 1)
                if b >= 2:
                    act.wait_ge(mm, 3 * (b - 1))
                nc.scalar.activation(xT_hi[:, b % 2, :, :], bank("x", b)[:, :].rearrange("p (c n) -> p c n", c=NC),
                                     ACT.Copy).then_inc(tr_hi, 1)

            def mixture_high(d):
                act.wait_ge(m_tr, d + 1)
                nc.scalar.activation(t.xT_hi[:, :, P * d:P * (d + 1)],
                                     bank("mx", d)[:, :].rearrange("p (c n) -> p c n", c=NC), ACT.Copy,
                                     scale=A_SCALE).then_inc(m_tr_hi, 1)

            x_high(0)
            for step in STEPS:
                a, b, c, d = stages(step)
                if b is not None:
                    for i, kind in enumerate(("qT", "kT")):
                        act.wait_ge(qk_tr, 2 * b + i + 1)
                        nc.scalar.activation(qkT[:, i, :, :], bank(kind, b)[:, :].rearrange("p (g n) -> p g n", g=NG),
                                             ACT.Copy).then_inc(qk_tr_out, 1)
                if d is not None and not tail(step):
                    mixture_high(d)
                if c is not None:
                    for n in (0, 2):
                        act.wait_ge(p_tr, 4 * c + n + 1)
                        nc.scalar.activation(probT[:, HPG * n:HPG * (n + 1), :], ps_t[n % 2][:, :, :],
                                             ACT.Copy).then_inc(p_out_act, 1)
                if c is not None and b is None:
                    act.wait_ge(o_mm, c + 1)
                    nc.scalar.activation(oT_hi[:, :, :], bank("o", c)[:, :].rearrange("p (g n) -> p g n", g=NG),
                                         ACT.Copy, scale=A_SCALE).then_inc(o_hi, 1)
                if b is not None:
                    act.wait_ge(maxed, 2 * b + 2)
                    for n, h in enumerate(range(HEADS)):
                        if n == HEADS // 2 and c is not None:
                            act.wait_ge(o_mm, c + 1)
                            nc.scalar.activation(oT_hi[:, :, :], bank("o", c)[:, :].rearrange("p (g n) -> p g n", g=NG),
                                                 ACT.Copy, scale=A_SCALE).then_inc(o_hi, 1)
                        last = nc.scalar.activation(prob[:, b % 2, h, :], ps_p[:, h, :], ACT.Exp, bias=m[:, h:h + 1],
                                                    scale=SM_SCALE, accum_out=rsum[:, h:h + 1])
                        if n % (HEADS // 2) == HEADS // 2 - 1:
                            last.then_inc(exped, 1)
                if a is not None and a + 1 < NB:
                    x_high(a + 1)
                if d is not None and tail(step):
                    mixture_high(d)
                if d is not None:
                    if d == 0:
                        act.wait_ge(s.gate_in, 32)
                    act.wait_ge(g_tr, d + 1)
                    if d:
                        act.wait_ge(g_mm, d)
                    for k in range(NC):
                        last = nc.scalar.activation(gT[:, k, :], bank("mg", d)[:, P * k:P * (k + 1)], ACT.Identity,
                                                    bias=t.affine[:, 1, k:k + 1], scale=t.affine[:, 0, k:k + 1])
                    last.then_inc(g_out, 1)
                if step == NB - 1:
                    act.wait_ge(s.w1_in, 16)
                    for n in range(NF):
                        c_, half = w1_part(n)
                        nc.scalar.activation(t.w1_hi[:, c_, half], t.w1_raw[:, c_, half], ACT.Copy,
                                             scale=W_SCALE).then_inc(s.w1_hi, 1)

        @block.tensor
        def _(pe):
            def free_bank(kind, b):
                n = place[kind, b]
                if n >= 2:
                    pe.wait_ge(ring[n - 2][2], ring[n - 2][3])
                return ps_r[n % 2]

            def project(i, b):
                to = free_bank("qkv"[i], b)
                if b == 0 and i == 0:
                    pe.wait_ge(s.self_lo, 4 * NC)
                for c in range(NC):
                    hi, lo = xT_hi[:, b % 2, c, :], xT_lo[:, b % 2, c, :]
                    nc.tensor.matmul(to[:, :], hi, w_hi[i][:, c, :], start=(c == 0), stop=False)
                    nc.tensor.matmul(to[:, :], hi, w_lo[i][:, c, :], start=False, stop=False)
                    last = nc.tensor.matmul(to[:, :], lo, w_hi[i][:, c, :], start=False,
                                            stop=(c == NC - 1))
                last.then_inc(mm, 1)

            def transposes(kind, b, src):
                to = free_bank(kind, b)
                for k in range(NC):
                    last = nc.tensor.transpose(to[:, P * k:P * (k + 1)], src[:, P * k:P * (k + 1)], t.ident[:, :])
                return last

            pe.wait_ge(normed, 1)
            transposes("x", 0, hat[:, 0, :]).then_inc(tr, 1)
            for step in STEPS:
                a, b, c, d = stages(step)
                if b is not None:
                    for i in range(2):
                        pe.wait_ge(roped, 2 * b + i + 1)
                        transposes(("qT", "kT")[i], b, qk[:, i, :]).then_inc(qk_tr, 1)
                if a is not None:
                    pe.wait_ge(tr_lo, a + 1)
                    project(0, a)
                if b is not None:
                    pe.wait_ge(qk_tr_out, 2 * b + 2)
                    if b:
                        pe.wait_ge(exped, 2 * b)
                    for h in range(HEADS):
                        g, rows = h // HPG, slice(HD * (h % HPG), HD * (h % HPG + 1))
                        last = nc.tensor.matmul(ps_p[:, slot(h), :], qkT[rows, 0, g, :], qkT[rows, 1, g, :],
                                                start=True, stop=True)
                    last.then_inc(scored, 1)
                if a is not None:
                    project(1, a)
                if d is not None and not tail(step):
                    pe.wait_ge(m_normed, 2 * d + 1)
                    transposes("mx", d, m_hat[:, 0, :]).then_inc(m_tr, 1)
                if c is not None:
                    for n in range(HEADS // HPG):
                        pe.wait_ge(scaled, 2 * c + 1 + n // 2)
                        if n >= 2:
                            pe.wait_ge(p_out_act if n % 2 == 0 else p_out_dve, 2 * c + n // 2)
                        for k in range(HPG):
                            last = nc.tensor.transpose(ps_t[n % 2][:, k, :], prob[:, c % 2, HPG * n + k, :], t.ident[:, :])
                        last.then_inc(p_tr, 1)
                    pe.wait_ge(p_out_act, 2 * c + 2)
                    pe.wait_ge(p_out_dve, 2 * c + 2)
                    to = free_bank("o", c)
                    for h in range(HEADS):
                        g, rows = h // HPG, slice(HD * (h % HPG), HD * (h % HPG + 1))
                        last = nc.tensor.matmul(to[rows, P * g:P * (g + 1)], vals[:, c % 3, HD * h:HD * (h + 1)],
                                                probT[:, slot(h), :], start=True, stop=True)
                    last.then_inc(o_mm, 1)
                if d is not None and tail(step):
                    pe.wait_ge(m_normed, 2 * d + 1)
                    transposes("mx", d, m_hat[:, 0, :]).then_inc(m_tr, 1)
                if a is not None:
                    project(2, a)
                    if a + 1 < NB:
                        pe.wait_ge(normed, a + 2)
                        transposes("x", a + 1, hat[:, a + 1, :]).then_inc(tr, 1)
                if d is not None:
                    pe.wait_ge(m_normed, 2 * d + 2)
                    transposes("mg", d, m_hat[:, 1, :]).then_inc(g_tr, 1)
                if c is not None:
                    to = free_bank("y", c)
                    pe.wait_ge(o_lo, c + 1)
                    for g in range(NG):
                        nc.tensor.matmul(to[:, :], oT_hi[:, g, :], w_hi[3][:, g, :], start=(g == 0), stop=False)
                        nc.tensor.matmul(to[:, :], oT_hi[:, g, :], w_lo[3][:, g, :], start=False, stop=False)
                        last = nc.tensor.matmul(to[:, :], oT_lo[:, g, :], w_hi[3][:, g, :], start=False,
                                                stop=(g == NG - 1))
                    last.then_inc(y_mm, 1)
                if d is not None:
                    to = free_bank("gate", d)
                    pe.wait_ge(g_out, d + 1)
                    for k in range(NC):
                        last = nc.tensor.matmul(to[:, 0:EXPERTS], gT[:, k, :], t.gate[:, k, :], start=(k == 0),
                                                stop=(k == NC - 1))
                    last.then_inc(g_mm, 1)


def mixture(nc, io, t, s):
    with ExitStack() as ctx:
        def sb(name, shape, dt=F32):
            return ctx.enter_context(nc.sbuf_tensor(name, shape, dt))

        def sem(name):
            return ctx.enter_context(nc.semaphore(name))

        w1_raw, w2_raw, w1_hi, w1_lo, xT_hi, xT_lo = t.w1_raw, t.w2_raw, t.w1_hi, t.w1_lo, t.xT_hi, t.xT_lo
        affine, gate = t.affine, t.gate
        w2_hi, w2_lo = sb("w2_hi", [P, NF, D], F16), sb("w2_lo", [P, NF, D], F16)
        h_f = sb("h_f", [P, 2, TOK])
        h_hi, h_lo = sb("h_hi", [P, NF, TOK], F16), sb("h_lo", [P, NF, TOK], F16)
        stats, mv, rstd = sb("m_stats", [P, 2, 6]), sb("m_mv", [P, 2, 2]), sb("m_rstd", [P, 2])
        hat = sb("m_hat", [P, 2, D])
        gT = sb("gT", [P, NC, P])
        rank = sb("rank", [P, NB, EXPERTS])
        prob, left = sb("m_prob", [P, NB, EXPERTS]), sb("m_left", [P, NB, EXPERTS])
        best, first = sb("m_best", [P, NB]), sb("m_first", [P, NB])
        sel = sb("m_sel", [P, 2, NB, EXPERTS])
        comb = sb("m_comb", [P, NB, EXPERTS])
        ps_h = [ctx.enter_context(nc.psum_tensor(f"ps_h{i}", [P, TOK], F32)) for i in range(2)]
        ps_y = [ctx.enter_context(nc.psum_tensor(f"ps_y{i}", [P, D], F32)) for i in range(NB)]
        ps_g = ctx.enter_context(nc.psum_tensor("ps_g", [P, EXPERTS], F32))

        w1_in, w2_in = s.w1_in, s.w2_in
        st, var, powed, chain = sem("m_st"), sem("m_var"), sem("m_pow"), sem("m_chain")
        normed, ranked = sem("m_normed"), sem("ranked")
        tr, tr_hi, tr_lo, g_tr, g_out, g_mm, g_exp = (sem("m_tr"), sem("m_tr_hi"), sem("m_tr_lo"), sem("g_tr"),
                                                      sem("g_out"), sem("g_mm"), sem("g_exp"))
        w1_hi_s, w1_lo_s, w2_hi_s, w2_lo_s = s.w1_hi, s.w1_lo, sem("w2_hi_s"), sem("w2_lo_s")
        up, gelu, h_hi_s, h_lo_s, down, y_out = (sem("up"), sem("gelu"), sem("h_hi_s"), sem("h_lo_s"), sem("down"),
                                                 sem("m_y_out"))
        out_sem = sem("out_sem")
        block = ctx.enter_context(nc.Block())

        @block.sync
        def _(sp):
            sp.wait_ge(w1_lo_s, NF)
            sp.dma_start(w1_raw[:, :, :], io.w1[1:2, :, :, :].rearrange("e p c n -> (e p) c n")).then_inc(w1_in, 16)
            with sp.Fori(0, EXPERTS) as e:
                sp.wait_ge(w2_lo_s, (e + 1) * NF)
                sp.dma_start(w2_raw[:, :, :],
                             io.w2[bass.ds(e + 1, 1), :, :, :].rearrange("e p c n -> (e p) c n")).then_inc(w2_in, 16)
                sp.wait_ge(w1_lo_s, (e + 2) * NF)
                sp.dma_start(w1_raw[:, :, :],
                             io.w1[bass.ds(e + 2, 1), :, :, :].rearrange("e p c n -> (e p) c n")).then_inc(w1_in, 16)
            sp.wait_ge(w1_in, 16 * (EXPERTS + 2))
            sp.wait_ge(w2_in, 16 * (EXPERTS + 1))
            for b in range(NB):
                sp.wait_ge(y_out, NB * (EXPERTS - 1) + b + 1)
                sp.dma_start(io.out[b:b + 1, :, :].rearrange("b t c -> (b t) c"), t.x[:, b, :]).then_inc(out_sem, 16)
            sp.wait_ge(out_sem, 16 * NB)

        @block.gpsimd
        def _(pool):
            for k in range(2):
                pool.wait_ge(var, k + 1)
                nc.gpsimd.tensor_tensor(rstd[:, k:k + 1], mv[:, k, 1:2], t.eps[:, 0:1], ALU.add).then_inc(powed, 1)
                pool.wait_ge(powed, 2 * k + 1)
                nc.gpsimd.tensor_tensor(rstd[:, k:k + 1], rstd[:, k:k + 1], t.half_neg[:, 0:1], ALU.pow).then_inc(powed, 1)
                pool.wait_ge(powed, 2 * k + 2)
            for i in range(EXPERTS):
                nc.gpsimd.memset(rank[:, :, i:i + 1], float(EXPERTS - i)).then_inc(ranked, 1)
                pool.wait_ge(ranked, i + 1)

        @block.vector
        def _(v):
            done = [0]

            def then_wait(ins):
                done[0] += 1
                ins.then_inc(chain, 1)
                v.wait_ge(chain, done[0])

            last_b = NB - 1
            for k, src in enumerate((t.x[:, last_b, :], hat[:, 0, :])):
                nc.vector.bn_stats(stats[:, k, :], src).then_inc(st, 1)
                v.wait_ge(st, k + 1)
                nc.vector.bn_aggr(mv[:, k, :], stats[:, k, :]).then_inc(var, 1)
                v.wait_ge(var, k + 1)
                v.wait_ge(powed, 2 * k + 2)
                nc.vector.tensor_scalar(hat[:, k, :], src, mv[:, k, 0:1], rstd[:, k:k + 1],
                                        ALU.subtract, ALU.mult).then_inc(normed, 1)
                v.wait_ge(normed, k + 1)
                if k == 0:
                    here = slice(P * last_b, P * NB)
                    v.wait_ge(tr_hi, 1)
                    nc.vector.scalar_tensor_tensor(out=xT_lo[:, :, here],
                                                   in0=ps_h[0][:, :].rearrange("p (c n) -> p c n", c=NC), scalar=A_SCALE,
                                                   in1=xT_hi[:, :, here], op0=ALU.mult, op1=ALU.subtract).then_inc(tr_lo, 1)

            def split_w1(n, e):
                c, half = w1_part(n)
                v.wait_ge(w1_hi_s, e * NF + n + 1)
                nc.vector.scalar_tensor_tensor(out=w1_lo[:, c, half].rearrange("p c n -> p (c n)"),
                                               in0=w1_raw[:, c, half].rearrange("p c n -> p (c n)"), scalar=W_SCALE,
                                               in1=w1_hi[:, c, half].rearrange("p c n -> p (c n)"), op0=ALU.mult,
                                               op1=ALU.subtract).then_inc(w1_lo_s, 1)

            v.wait_ge(g_mm, 1)
            logits = t.logits
            then_wait(nc.vector.tensor_copy(logits[:, last_b, :], ps_g[:, :]))
            wide = [P, NB, EXPERTS]
            then_wait(nc.vector.tensor_reduce(best[:, :], logits[:, :, :], AX.X, ALU.max))
            then_wait(nc.vector.tensor_tensor(prob[:, :, :], logits[:, :, :], best[:, :].unsqueeze(2).broadcast_to(wide),
                                              ALU.subtract))
            def router_weights():
                v.wait_ge(g_exp, 1)
                then_wait(nc.vector.tensor_reduce(best[:, :], prob[:, :, :], AX.X, ALU.add))
                then_wait(nc.vector.reciprocal(best[:, :], best[:, :]))
                then_wait(nc.vector.tensor_tensor(prob[:, :, :], prob[:, :, :], best[:, :].unsqueeze(2).broadcast_to(wide),
                                                  ALU.mult))
                v.wait_ge(ranked, EXPERTS)
                for k in range(2):
                    src = prob if k == 0 else left
                    now = sel[:, k, :, :]
                    then_wait(nc.vector.tensor_reduce(best[:, :], src[:, :, :], AX.X, ALU.max))
                    then_wait(nc.vector.tensor_tensor(now, src[:, :, :], best[:, :].unsqueeze(2).broadcast_to(wide),
                                                      ALU.is_equal))
                    then_wait(nc.vector.tensor_tensor(now, now, rank[:, :, :], ALU.mult))
                    then_wait(nc.vector.tensor_reduce(first[:, :], now, AX.X, ALU.max))
                    then_wait(nc.vector.tensor_tensor(now, now, first[:, :].unsqueeze(2).broadcast_to(wide), ALU.is_equal))
                    if k == 0:
                        then_wait(nc.vector.scalar_tensor_tensor(
                            out=left[:, :, :].rearrange("p b e -> p (b e)"), in0=now.rearrange("p b e -> p (b e)"), scalar=-4.0,
                            in1=prob[:, :, :].rearrange("p b e -> p (b e)"), op0=ALU.mult, op1=ALU.add))
                then_wait(nc.vector.tensor_tensor(sel[:, 0, :, :], sel[:, 0, :, :], sel[:, 1, :, :], ALU.add))
                then_wait(nc.vector.tensor_tensor(comb[:, :, :], sel[:, 0, :, :], prob[:, :, :], ALU.mult))
                then_wait(nc.vector.tensor_scalar(comb[:, :, :], comb[:, :, :], UNSCALE, None, ALU.mult))

            def expert(e, first):
                for f in range(NF):
                    v.wait_ge(h_hi_s, e * NF + f + 1)
                    nc.vector.scalar_tensor_tensor(out=h_lo[:, f, :], in0=h_f[:, f % 2, :], scalar=A_SCALE,
                                                   in1=h_hi[:, f, :], op0=ALU.mult, op1=ALU.subtract).then_inc(h_lo_s, 1)
                    v.wait_ge(w2_hi_s, e * NF + f + 1)
                    nc.vector.scalar_tensor_tensor(out=w2_lo[:, f, :], in0=w2_raw[:, f, :], scalar=W_SCALE,
                                                   in1=w2_hi[:, f, :], op0=ALU.mult, op1=ALU.subtract).then_inc(w2_lo_s, 1)
                if first:
                    router_weights()
                for n in range(NF):
                    split_w1(n, e + 1)
                for b in range(NB):
                    v.wait_ge(down, e * NB + b + 1)
                    nc.vector.scalar_tensor_tensor(
                        out=t.x[:, b, :], in0=ps_y[b][:, :],
                        scalar=comb[:, b, bass.ds(e, 1)], in1=t.x[:, b, :], op0=ALU.mult, op1=ALU.add).then_inc(y_out, 1)

            expert(0, True)
            with v.Fori(1, EXPERTS) as e:
                expert(e, False)

        @block.scalar
        def _(act):
            def split_w1(n, e):
                c, half = w1_part(n)
                if n == 0:
                    act.wait_ge(w1_in, (e + 1) * 16)
                nc.scalar.activation(w1_hi[:, c, half], w1_raw[:, c, half], ACT.Copy, scale=W_SCALE).then_inc(w1_hi_s, 1)

            here = slice(P * (NB - 1), P * NB)
            act.wait_ge(tr, 1)
            nc.scalar.activation(xT_hi[:, :, here], ps_h[0][:, :].rearrange("p (c n) -> p c n", c=NC),
                                 ACT.Copy, scale=A_SCALE).then_inc(tr_hi, 1)
            act.wait_ge(g_tr, 1)
            for c in range(NC):
                last = nc.scalar.activation(gT[:, c, :], ps_y[0][:, P * c:P * (c + 1)], ACT.Identity,
                                            bias=affine[:, 1, c:c + 1], scale=affine[:, 0, c:c + 1])
            last.then_inc(g_out, 1)

            def expert(e, first):
                act.wait_ge(w2_in, (e + 1) * 16)
                for f in range(NF):
                    if first and f == 2:
                        act.wait_ge(chain, 3)
                        nc.scalar.activation(prob[:, :, :], prob[:, :, :], ACT.Exp).then_inc(g_exp, 1)
                    act.wait_ge(up, e * NF + f + 1)
                    if f >= 2:
                        act.wait_ge(h_lo_s, e * NF + f - 1)
                    nc.scalar.activation(h_f[:, f % 2, :], ps_h[f % 2][:, :], ACT.Gelu, scale=UNSCALE).then_inc(gelu, 1)
                    act.wait_ge(gelu, e * NF + f + 1)
                    nc.scalar.activation(h_hi[:, f, :], h_f[:, f % 2, :], ACT.Copy, scale=A_SCALE).then_inc(h_hi_s, 1)
                    nc.scalar.activation(w2_hi[:, f, :], w2_raw[:, f, :], ACT.Copy, scale=W_SCALE).then_inc(w2_hi_s, 1)
                for n in range(NF):
                    split_w1(n, e + 1)

            expert(0, True)
            with act.Fori(1, EXPERTS) as e:
                expert(e, False)

        @block.tensor
        def _(pe):
            def transposes(to, src):
                for c in range(NC):
                    last = nc.tensor.transpose(to[:, P * c:P * (c + 1)], src[:, P * c:P * (c + 1)], t.ident[:, :])
                return last

            def router():
                pe.wait_ge(normed, 2)
                transposes(ps_y[0], hat[:, 1, :]).then_inc(g_tr, 1)

            def router_scores():
                pe.wait_ge(g_out, 1)
                for c in range(NC):
                    last = nc.tensor.matmul(ps_g[:, :], gT[:, c, :], gate[:, c, :], start=(c == 0), stop=(c == NC - 1))
                last.then_inc(g_mm, 1)

            def expert(e, first):
                pe.wait_ge(w1_lo_s, (e + 1) * NF)
                for f in range(NF):
                    if f >= 2:
                        pe.wait_ge(gelu, e * NF + f - 1)
                    col = slice(P * f, P * (f + 1))
                    for c in range(NC):
                        nc.tensor.matmul(ps_h[f % 2][:, :], w1_hi[:, c, col], xT_hi[:, c, :], start=(c == 0), stop=False)
                        nc.tensor.matmul(ps_h[f % 2][:, :], w1_hi[:, c, col], xT_lo[:, c, :], start=False, stop=False)
                        last = nc.tensor.matmul(ps_h[f % 2][:, :], w1_lo[:, c, col], xT_hi[:, c, :], start=False,
                                                stop=(c == NC - 1))
                    last.then_inc(up, 1)
                    if first and f == 0:
                        router()
                    if first and f == 1:
                        router_scores()
                for f in range(NF):
                    pe.wait_ge(h_lo_s, e * NF + f + 1)
                    pe.wait_ge(w2_lo_s, e * NF + f + 1)
                    for b in range(NB):
                        tok = slice(P * b, P * (b + 1))
                        nc.tensor.matmul(ps_y[b][:, :], h_hi[:, f, tok], w2_hi[:, f, :], start=(f == 0), stop=False)
                        nc.tensor.matmul(ps_y[b][:, :], h_hi[:, f, tok], w2_lo[:, f, :], start=False, stop=False)
                        last = nc.tensor.matmul(ps_y[b][:, :], h_lo[:, f, tok], w2_hi[:, f, :], start=False,
                                                stop=(f == NF - 1))
                        if f == NF - 1:
                            last.then_inc(down, 1)

            pe.wait_ge(normed, 1)
            transposes(ps_h[0], hat[:, 0, :]).then_inc(tr, 1)
            pe.wait_ge(tr_lo, 1)
            expert(0, True)
            with pe.Fori(1, EXPERTS) as e:
                expert(e, False)


def program(nc, io):
    with ExitStack() as ctx:
        def sb(name, shape, dt=F32):
            return ctx.enter_context(nc.sbuf_tensor(name, shape, dt))

        t, s = Named(), Named()
        t.x = sb("x_sb", [P, NB, D])
        t.ident = sb("ident_sb", [P, P])
        t.half_neg, t.eps, t.inv_scale2 = sb("half_neg", [P, NB]), sb("eps", [P, NB]), sb("inv_scale2", [P, NB])
        s.self_hi, s.self_lo = ctx.enter_context(nc.semaphore("self_hi")), ctx.enter_context(nc.semaphore("self_lo"))
        io.mask_rows = nc.dram_tensor("mask_rows", [NB, 2, KEYS], F16, kind="Internal").ap()
        t.a_stats, t.a_mv, t.a_rstd = sb("a_stats", [P, NB, 6]), sb("a_mv", [P, NB, 2]), sb("a_rstd", [P, NB])
        s.a_st, s.a_var, s.a_powed = [ctx.enter_context(nc.semaphore(name)) for name in ("a_st", "a_var", "a_powed")]
        t.cT_hi, t.cT_lo = sb("cT_hi", [P, NC, KEYS], F16), sb("cT_lo", [P, NC, KEYS], F16)
        with ExitStack() as cross:
            def cb(name, shape, dt=F32):
                return cross.enter_context(nc.sbuf_tensor(name, shape, dt))

            t.ones32 = cb("ones32", [P, HD])
            t.q_stack = cb("q_stack", [P, HEADS, TOK], F16)
            t.k_stack = [cb(f"k_stack{u}", [P, HPG, KEYS], F16) for u in range(2)]
            t.wk_hi, t.wk_lo = cb("wk_hi", [P, NC, D], F16), cb("wk_lo", [P, NC, D], F16)
            t.wv_hi, t.wv_lo = cb("wv_hi", [P, NC, D], F16), cb("wv_lo", [P, NC, D], F16)
            cross_attention(nc, io, t, s)
        t.w1_raw, t.w2_raw = sb("w1_raw", [P, NC, FF]), sb("w2_raw", [P, NF, D])
        t.w1_hi, t.w1_lo = sb("w1_hi", [P, NC, FF], F16), sb("w1_lo", [P, NC, FF], F16)
        t.xT_hi, t.xT_lo = sb("m_xT_hi", [P, NC, TOK], F16), sb("m_xT_lo", [P, NC, TOK], F16)
        t.affine, t.gate = sb("affine", [P, 2, NC]), sb("gate", [P, NC, EXPERTS])
        t.logits = sb("logits", [P, NB, EXPERTS])
        s.gate_in, s.w1_in, s.w2_in, s.w1_hi, s.w1_lo = [
            ctx.enter_context(nc.semaphore(name))
            for name in ("m_gate_in", "m_w1_in", "m_w2_in", "m_w1_hi", "m_w1_lo")]
        self_attention(nc, io, t, s)
        mixture(nc, io, t, s)


class Named:
    pass


def kernel(**inputs):
    import concourse.bacc as bacc
    from concourse.bass_utils import run_bass_kernel_spmd

    def plain(name):
        return np.ascontiguousarray(inputs[name])

    def transposed(name):
        return np.ascontiguousarray(np.asarray(inputs[name]).T)

    def column(name):
        return np.ascontiguousarray(np.asarray(inputs[name]).reshape(NC, P).T)

    def rotary():
        inv_freq = (1.0 / 10000.0 ** (np.arange(0, HD, 2, dtype=np.float32) / HD)).astype(np.float32)
        freqs = np.arange(P, dtype=np.float32)[:, None] * inv_freq[None, :]
        angle = np.concatenate([freqs, freqs], axis=-1).astype(np.float64)
        sign = np.concatenate([-np.ones(HD // 2), np.ones(HD // 2)])
        return np.stack([np.cos(angle), np.sin(angle) * sign], axis=1).astype(np.float32)

    def by_partition(w, ahead):
        w = w.reshape(EXPERTS, -1, P, w.shape[-1]).transpose(0, 2, 1, 3)
        return np.ascontiguousarray(np.concatenate([w, w[:ahead]]))

    tiles = np.asarray(inputs["ctx_1024"]).reshape(NB * NKT, P, D)
    arrays = {
        "x": plain("x"),
        "context": np.ascontiguousarray(tiles),
        "mask": plain("mask_BxS2_bf1").view(np.uint8),
        "ident": np.eye(P, dtype=np.float32),
        "rope": rotary(),
        "vectors": np.ascontiguousarray(np.stack([column(f"L0_xattn_{v}") for v in ("g1", "g2", "b1", "b2")], axis=1)),
        "xbo": plain("L0_xattn_bo"),
        "wqT": transposed("L0_xattn_Wq"), "wkT": transposed("L0_xattn_Wk"),
        "wvT": transposed("L0_xattn_Wv"), "woT": transposed("L0_xattn_Wo"),
        "a_wqT": transposed("L0_attn_Wq"), "a_wkT": transposed("L0_attn_Wk"),
        "a_wvT": transposed("L0_attn_Wv"), "a_woT": transposed("L0_attn_Wo"),
        "a_bq": plain("L0_attn_bq"), "a_bk": plain("L0_attn_bk"),
        "a_bv": plain("L0_attn_bv"), "a_bo": plain("L0_attn_bo"),
        "affine": np.ascontiguousarray(np.stack([column("L0_ffn_ln_gamma"), column("L0_ffn_ln_beta")], axis=1)),
        "gate": np.ascontiguousarray(np.asarray(inputs["L0_ffn_gate_w"]).T.reshape(NC, P, EXPERTS).transpose(1, 0, 2)),
        "w1": by_partition(np.asarray(inputs["L0_ffn_w1"]).transpose(0, 2, 1), 2),
        "w2": by_partition(np.asarray(inputs["L0_ffn_w2"]).transpose(0, 2, 1), 1),
    }
    nc = bacc.Bacc("TRN2", target_bir_lowering=False, num_devices=1)
    io = Named()
    for name, a in arrays.items():
        ap = nc.dram_tensor(f"in_{name}", a.shape, mybir.dt.from_np(a.dtype), kind="ExternalInput").ap()
        io.__dict__[name] = ap
    io.out = nc.dram_tensor("out", (NB, P, D), F32, kind="ExternalOutput").ap()
    program(nc, io)
    r = run_bass_kernel_spmd(nc, [{f"in_{name}": a for name, a in arrays.items()}], core_ids=[0])
    return r.results[0]["out"]
```
